# Optimizing a Trainium2 kernel written in Bass

```python
import numpy as np
import jax
import jax.numpy as jnp

def _softmax(x, axis=-1):
    return jax.nn.softmax(x, axis=axis)

def _gelu(x):
    return jax.nn.gelu(x, approximate=True)

def _silu(x):
    return jax.nn.silu(x)

def _sigmoid(x):
    return jax.nn.sigmoid(x)

def _layernorm(x, axis=-1, eps=1e-05):
    m = jnp.mean(x, axis=axis, keepdims=True)
    v = jnp.var(x, axis=axis, keepdims=True)
    return (x - m) / jnp.sqrt(v + eps)

def _scatter_add(tgt, idx, src, axis=0):
    return tgt.at[idx].add(src)

def _segment_sum(src, seg, n):
    return jax.ops.segment_sum(src, seg, n)
kernel_name = 'mk_flamingo_gated_d1_seqx_r8_0989f2'

def setup_inputs(seed: int=0):
    np.random.seed(seed)
    _w = jnp.asarray

    def _rec_inputs():
        import jax
        import jax.numpy as jnp
        _rk = jax.random.key(seed)
        x = -0.0005207 + 1.001 * jax.random.normal(jax.random.fold_in(_rk, 1), (4, 256, 512), jnp.float32)
        _lenS = 256 - jax.random.randint(jax.random.fold_in(_rk, 7), (4,), 0, max(1, 256 // 4) + 1, jnp.int32)
        _lenS2 = 1601 - jax.random.randint(jax.random.fold_in(_rk, 8), (4,), 0, max(1, 1601 // 4) + 1, jnp.int32)
        _ctx_4096P = jax.random.normal(jax.random.fold_in(_rk, 11), (4, 16, 512), jnp.float32)
        _ctx_4096c = jax.random.dirichlet(jax.random.fold_in(_rk, 511), 0.3 * jnp.ones((16,), jnp.float32), (4, 1601))
        _ctx_4096t = jnp.einsum('bsk,bkd->bsd', _ctx_4096c, _ctx_4096P)
        _ctx_4096t = _ctx_4096t * jax.lax.rsqrt(jnp.mean(jnp.square(_ctx_4096t)) + 1e-12) * 0.953939
        ctx_4096 = -0.00010331 + 0.999899 * (_ctx_4096t + 0.3 * jax.random.normal(jax.random.fold_in(_rk, 611), (4, 1601, 512), jnp.float32))
        _g = jax.random.normal(jax.random.fold_in(_rk, 9001), (2, 1), jnp.float32)
        _g = jnp.sign(_g) * jnp.maximum(jnp.abs(_g), 1.0) + (_g == 0) * 1.0
        g_xattn = _g[0]
        g_ffn = _g[1]
        return (x, ctx_4096, g_xattn, g_ffn)
    x, ctx_4096, g_xattn, g_ffn = _rec_inputs()

    def _L0_xattn_setup():
        import jax, jax.numpy as jnp
        import numpy as np
        HEADS = 32
        KV_HEADS = 8
        HEAD_DIM = 128
        EPS = 1e-06

        def rms_norm(x, w):
            var = jnp.mean(jnp.square(x.astype(jnp.float32)), axis=-1, keepdims=True)
            return (x.astype(jnp.float32) * jax.lax.rsqrt(var + EPS)).astype(x.dtype) * w
        key = jax.random.key(seed)
        ks = jax.random.split(key, 6)
        bsz, n_lat, seq, hidden = (8, 64, 512, 512)
        return {'latents': jax.random.normal(ks[0], (bsz, n_lat, hidden), jnp.float32), 'context': jax.random.normal(ks[1], (bsz, seq, hidden), jnp.float32), 'Wq': jax.random.normal(ks[2], (hidden, HEADS * HEAD_DIM), jnp.float32) * 0.02, 'Wk': jax.random.normal(ks[3], (hidden, KV_HEADS * HEAD_DIM), jnp.float32) * 0.02, 'Wv': jax.random.normal(ks[4], (hidden, KV_HEADS * HEAD_DIM), jnp.float32) * 0.02, 'Wo': jax.random.normal(ks[5], (HEADS * HEAD_DIM, hidden), jnp.float32) * 0.02, 'q_norm_w': jnp.ones((HEAD_DIM,), jnp.float32), 'k_norm_w': jnp.ones((HEAD_DIM,), jnp.float32)}
    _L0_xattn_all = _L0_xattn_setup()
    _L0_xattn_in = {k: v for k, v in _L0_xattn_all.items() if k in ('Wq', 'Wk', 'Wv', 'Wo', 'q_norm_w', 'k_norm_w')}
    del _L0_xattn_all

    def _L0_ffn_setup():
        import jax, jax.numpy as jnp
        import numpy as np
        DIM = 512
        INTER = 1792
        SPARSITY = 32
        RANK = 16
        key = jax.random.key(seed)
        ks = jax.random.split(key, 5)
        B, T = (32, 1)
        x = jax.random.normal(ks[0], (B, T, DIM), dtype=jnp.float32)
        c1_w = jax.random.normal(ks[1], (RANK, DIM), dtype=jnp.float32) * (1.0 / np.sqrt(DIM))
        c2_w = jax.random.normal(ks[2], (INTER, RANK), dtype=jnp.float32) * (1.0 / np.sqrt(RANK))
        w1 = jax.random.normal(ks[3], (INTER, DIM), dtype=jnp.float32) * (1.0 / np.sqrt(DIM))
        w2t = jax.random.normal(ks[4], (INTER, DIM), dtype=jnp.float32) * (1.0 / np.sqrt(INTER))
        return {'x': x, 'c1_w': c1_w, 'c2_w': c2_w, 'w1': w1, 'w2t': w2t}
    _L0_ffn_all = _L0_ffn_setup()
    _L0_ffn_in = {k: v for k, v in _L0_ffn_all.items() if k in ('c1_w', 'c2_w', 'w1', 'w2t')}
    del _L0_ffn_all
    return {'x': x, 'ctx_4096': ctx_4096, 'g_xattn': g_xattn, 'g_ffn': g_ffn, 'L0_xattn_Wq': _L0_xattn_in['Wq'], 'L0_xattn_Wk': _L0_xattn_in['Wk'], 'L0_xattn_Wv': _L0_xattn_in['Wv'], 'L0_xattn_Wo': _L0_xattn_in['Wo'], 'L0_xattn_q_norm_w': _L0_xattn_in['q_norm_w'], 'L0_xattn_k_norm_w': _L0_xattn_in['k_norm_w'], 'L0_ffn_c1_w': _L0_ffn_in['c1_w'], 'L0_ffn_c2_w': _L0_ffn_in['c2_w'], 'L0_ffn_w1': _L0_ffn_in['w1'], 'L0_ffn_w2t': _L0_ffn_in['w2t']}

def reference(x, ctx_4096, g_xattn, g_ffn, L0_xattn_Wq, L0_xattn_Wk, L0_xattn_Wv, L0_xattn_Wo, L0_xattn_q_norm_w, L0_xattn_k_norm_w, L0_ffn_c1_w, L0_ffn_c2_w, L0_ffn_w1, L0_ffn_w2t):
    import jax
    import jax.numpy as jnp

    def _L0_xattn_ref(latents, context, Wq, Wk, Wv, Wo, q_norm_w, k_norm_w):
        import jax, jax.numpy as jnp
        import numpy as np
        HEADS = 32
        KV_HEADS = 8
        HEAD_DIM = 128
        EPS = 1e-06

        def rms_norm(x, w):
            var = jnp.mean(jnp.square(x.astype(jnp.float32)), axis=-1, keepdims=True)
            return (x.astype(jnp.float32) * jax.lax.rsqrt(var + EPS)).astype(x.dtype) * w
        bsz, q_len, hidden = latents.shape
        kv = jnp.concatenate([context, latents], axis=1)
        kv_len = kv.shape[1]
        groups = HEADS // KV_HEADS
        q = (latents @ Wq).reshape(bsz, q_len, HEADS, HEAD_DIM).transpose(0, 2, 1, 3)
        k = (kv @ Wk).reshape(bsz, kv_len, KV_HEADS, HEAD_DIM).transpose(0, 2, 1, 3)
        v = (kv @ Wv).reshape(bsz, kv_len, KV_HEADS, HEAD_DIM).transpose(0, 2, 1, 3)
        q = rms_norm(q, q_norm_w)
        k = rms_norm(k, k_norm_w)
        qg = q.reshape(bsz, KV_HEADS, groups, q_len, HEAD_DIM)
        scale = 1.0 / np.sqrt(HEAD_DIM)
        scores = jnp.einsum('bhgqd,bhkd->bhgqk', qg, k) * scale
        probs = jax.nn.softmax(scores.astype(jnp.float32), axis=-1).astype(q.dtype)
        out = jnp.einsum('bhgqk,bhkd->bhgqd', probs, v)
        out = out.reshape(bsz, HEADS, q_len, HEAD_DIM).transpose(0, 2, 1, 3)
        out = out.reshape(bsz, q_len, HEADS * HEAD_DIM)
        return out @ Wo

    def _L0_ffn_ref(x, c1_w, c2_w, w1, w2t):
        import jax, jax.numpy as jnp
        import numpy as np
        DIM = 512
        INTER = 1792
        SPARSITY = 32
        RANK = 16
        B, T, M = x.shape
        xf = x.reshape(B * T, M)
        inter = xf @ c1_w.T @ c2_w.T
        n_blocks = INTER // SPARSITY
        blk = inter.reshape(B * T, n_blocks, SPARSITY)
        idx = jnp.argmax(blk, axis=-1) + jnp.arange(0, INTER, SPARSITY)
        w1_g = w1[idx]
        w2_g = w2t[idx]
        h = jax.nn.relu(jnp.einsum('bkm,bm->bk', w1_g, xf))
        out = jnp.einsum('bk,bkm->bm', h, w2_g)
        return out.reshape(B, T, M)
    x = x + jnp.tanh(g_xattn[0]) * _L0_xattn_ref(_layernorm(x, axis=-1), ctx_4096, L0_xattn_Wq, L0_xattn_Wk, L0_xattn_Wv, L0_xattn_Wo, L0_xattn_q_norm_w, L0_xattn_k_norm_w)
    x = x + jnp.tanh(g_ffn[0]) * _L0_ffn_ref(_layernorm(x, axis=-1), L0_ffn_c1_w, L0_ffn_c2_w, L0_ffn_w1, L0_ffn_w2t)
    return x

_drawn_inputs = setup_inputs


def setup_inputs(seed=0):
    import zlib

    import numpy as np

    out = dict(_drawn_inputs(seed))
    spreads = {'L0_xattn_q_norm_w': (1.0, 0.6), 'L0_xattn_k_norm_w': (1.0, 0.6)}
    factors = {}
    for name, (base, spread) in spreads.items():
        noise = np.random.default_rng([zlib.crc32(name.encode()), seed]).standard_normal(out[name].shape)
        drawn = base * np.exp(spread * noise) if base else spread * noise
        out[name] = jnp.asarray(drawn.astype(out[name].dtype))
    for name, factor in factors.items():
        out[name] = (out[name] * factor).astype(out[name].dtype)
    return out
```

```python
from contextlib import ExitStack

import concourse.bass as bass
from concourse import mybir

F32 = mybir.dt.float32
F32R = mybir.dt.float32r
ALU = mybir.AluOpType
ACT = mybir.ActivationFunctionType
AX = mybir.AxisListType

P = 128
AHEAD = 32
HI, LO = 0, 1
EPS_LN = 1e-5
EPS_RMS = 1e-6


def passes(w, m):
    return ((w[HI], m[HI]), (w[LO], m[HI]), (w[HI], m[LO]))


def program(nc, x, ctx_4096, g_xattn, g_ffn, Wq, Wk, Wv, Wo, q_norm_w, k_norm_w, c1_w, c2_w, w1, w2t, out):
    B, S, D = x.shape
    L = ctx_4096.shape[1]
    DH = q_norm_w.shape[0]
    HEADS = Wq.shape[1] // DH
    KVH = Wk.shape[1] // DH
    G = HEADS // KVH
    KT = D // P
    QT = B * S // P
    dims = dict(B=B, S=S, D=D, L=L, DH=DH, HEADS=HEADS, KVH=KVH, G=G, KT=KT, QT=QT)

    scratch = dict(
        lat=nc.dram_tensor("lat_scr", [B, P, 2, KT, S], F32, kind="Internal").ap(),
        q=nc.dram_tensor("q_scr", [B * KVH, P, 2, G, S], F32, kind="Internal").ap(),
        kv=nc.dram_tensor("kv_scr", [KVH, P, 2, 2, KT, DH], F32, kind="Internal").ap(),
        o=nc.dram_tensor("o_scr", [B * KVH, P, G, S], F32, kind="Internal").ap(),
        x2=nc.dram_tensor("x2_scr", [QT * P, D], F32, kind="Internal").ap(),
        xn=nc.dram_tensor("xn_scr", [QT * P, D], F32, kind="Internal").ap(),
    )
    prepare(nc, dims, scratch, x, Wq, Wk, Wv, q_norm_w, k_norm_w)
    attend(nc, dims, scratch, ctx_4096)
    project(nc, dims, scratch, x, Wo, g_xattn)
    ffn(nc, dims, scratch, g_ffn, c1_w, c2_w, w1, w2t, out)


def tools(nc, ctx, tag):
    def sb(name, shape, dt=F32):
        return ctx.enter_context(nc.sbuf_tensor(f"{tag}_{name}", shape, dt))

    def ps(name, shape):
        return ctx.enter_context(nc.psum_tensor(f"{tag}_{name}", shape, F32))

    def sem(name):
        return ctx.enter_context(nc.semaphore(f"{tag}_{name}"))
    return sb, ps, sem


def start_ahead(pool, sems):
    for s in sems:
        pool.sem_inc(s, AHEAD)


def identity(pool, ident, sem):
    pool.memset(ident[:], 0.0).then_inc(sem, 1)
    pool.wait_ge(sem, 1)
    pool.affine_select(out=ident[:], in_=ident[:], compare_op=ALU.not_equal, fill=1.0, base=0,
                       pattern=[[-1, P]], channel_multiplier=1).then_inc(sem, 1)



def prepare(nc, d, scr, x, Wq, Wk, Wv, q_norm_w, k_norm_w):
    B, S, D, DH, KVH, G, KT, QT = (d[k] for k in ("B", "S", "D", "DH", "KVH", "G", "KT", "QT"))
    N = G * DH
    SCALE = float(DH) ** -0.5
    BT = S // P
    with ExitStack() as ctx:
        sb, ps, sem = tools(nc, ctx, "pre")
        ident = sb("ident", [P, P])
        mhalf = sb("mhalf", [P, G])
        wcol = sb("wcol", [P, 4])
        xin = sb("xin", [P, 2, D])
        stats = sb("stats", [P, 2, 6])
        mv = sb("mv", [P, 2, 2])
        veps = sb("veps", [P, 2, 1])
        rstd = sb("rstd", [P, 2, 1])
        xn = sb("xn", [P, 2, D])
        xT = sb("xT", [P, 2, KT, QT * P], F32R)
        wq_raw = sb("wq_raw", [P, 2, KT, N])
        wq = sb("wq", [P, 2, 2, KT, N], F32R)
        kv_raw = sb("kv_raw", [P, 2, 2, KT, DH])
        kv = sb("kv", [P, 2, 2, 2, KT, DH], F32R)
        sq = sb("sq", [P, 2, N])
        ss = sb("ss", [P, 2, G])
        ms = sb("ms", [P, 2, G])
        rq = sb("rq", [P, 2, G])
        qn = sb("qn", [P, 2, N])
        qT = sb("qT", [P, 2, 2, N], F32R)
        ptr = ps("ptr", [P, 2, 512])
        pq = ps("pq", [P, 2, 512])

        w_in, lat_out, id_ok, half_ok, w_ok = (sem(n) for n in ("w_in", "lat_out", "id_ok", "half_ok", "w_ok"))
        x_in = [sem("x_in0"), sem("x_in1")]
        bn, var_ok, ve_ok, rstd_ok, xn_ok, xt_ps, xhi_ok, xlo_ok = (
            sem(n) for n in ("bn", "var_ok", "ve_ok", "rstd_ok", "xn_ok", "xt_ps", "xhi_ok", "xlo_ok"))
        wq_in = [sem("wq_in0"), sem("wq_in1")]
        kv_in = [sem("kv_in0"), sem("kv_in1")]
        kv_out = [sem("kv_out0"), sem("kv_out1")]
        q_out = [sem("q_out0"), sem("q_out1")]
        wqhi_ok, wqlo_ok, kvhi_ok, kvlo_ok = (sem(n) for n in ("wqhi_ok", "wqlo_ok", "kvhi_ok", "kvlo_ok"))
        q_ps, sq_ok, ss_ok, ms_ok, rq_ok, qn_ok, qt_ps, qhi_ok, qlo_ok = (
            sem(n) for n in ("q_ps", "sq_ok", "ss_ok", "ms_ok", "rq_ok", "qn_ok", "qt_ps", "qhi_ok", "qlo_ok"))

        x_t = x.rearrange("b (t p) n -> (b t) p n", p=P)
        wq_v = Wq.rearrange("(t p) n -> p t n", p=P)
        wk_v = Wk.rearrange("(t p) n -> p t n", p=P)
        wv_v = Wv.rearrange("(t p) n -> p t n", p=P)

        with nc.Block() as block:

            @block.sync
            def _(sp):
                sp.dma_start(wcol[:, 0:1], q_norm_w.rearrange("(p o) -> p o", o=1)).then_inc(w_in, 16)
                sp.dma_start(wcol[:, 1:2], k_norm_w.rearrange("(p o) -> p o", o=1)).then_inc(w_in, 16)
                for t in range(QT):
                    if t >= 2:
                        sp.wait_ge(xn_ok, t - 1)
                    sp.dma_start(xin[:, t % 2], x_t[t]).then_inc(x_in[t % 2], 16)
                sp.wait_ge(xhi_ok, QT)
                sp.wait_ge(xlo_ok, QT)
                for b in range(B):
                    sp.dma_start(scr["lat"][b], xT[:, :, :, b * S:(b + 1) * S].bitcast(F32)).then_inc(lat_out, 16)
                sp.wait_ge(lat_out, 16 * B)

            @block.gpsimd
            def _(pool):
                start_ahead(pool, wq_in + kv_in + kv_out + q_out + [wqhi_ok, wqlo_ok, kvhi_ok, kvlo_ok,
                            q_ps, sq_ok, ss_ok, ms_ok, rq_ok, qn_ok, qt_ps, qhi_ok, qlo_ok])
                identity(pool, ident, id_ok)
                pool.memset(mhalf[:], -0.5).then_inc(half_ok, 1)
                pool.wait_ge(half_ok, 1)
                for t in range(QT):
                    pool.wait_ge(ve_ok, t + 1)
                    pool.tensor_tensor(rstd[:, t % 2], veps[:, t % 2], mhalf[:, 0:1], ALU.pow).then_inc(rstd_ok, 1)

            @block.scalar
            def _(act):
                for t in range(QT):
                    act.wait_ge(xt_ps, t + 1)
                    act.copy(xT[:, HI, :, t * P:(t + 1) * P],
                             ptr[:, t % 2].rearrange("p (c r) -> p c r", c=KT)).then_inc(xhi_ok, 1)

            @block.tensor
            def _(pe):
                pe.wait_ge(id_ok, 2)
                for t in range(QT):
                    pe.wait_ge(xn_ok, t + 1)
                    if t >= 2:
                        pe.wait_ge(xlo_ok, t - 1)
                    for c in range(KT):
                        last = pe.transpose(ptr[:, t % 2, c * P:(c + 1) * P], xn[:, t % 2, c * P:(c + 1) * P], ident[:])
                    last.then_inc(xt_ps, 1)

            @block.vector
            def _(dve):
                dve.wait_ge(w_in, 32)
                dve.tensor_tensor(wcol[:, 2:3], wcol[:, 0:1], wcol[:, 1:2], ALU.mult).then_inc(w_ok, 1)
                dve.wait_ge(w_ok, 1)
                dve.tensor_scalar(wcol[:, 3:4], wcol[:, 2:3], SCALE, None, ALU.mult).then_inc(w_ok, 1)
                for t in range(QT + 1):
                    if t < QT:
                        s = t % 2
                        dve.wait_ge(x_in[s], 16 * (t // 2) + 16)
                        dve.bn_stats(stats[:, s], xin[:, s]).then_inc(bn, 1)
                        dve.wait_ge(bn, t + 1)
                        dve.bn_aggr(mv[:, s], stats[:, s]).then_inc(var_ok, 1)
                        dve.wait_ge(var_ok, t + 1)
                        dve.tensor_scalar(veps[:, s], mv[:, s, 1:2], EPS_LN, None, ALU.add).then_inc(ve_ok, 1)
                        dve.wait_ge(rstd_ok, t + 1)
                        if t >= 2:
                            dve.wait_ge(xt_ps, t - 1)
                        dve.tensor_scalar(xn[:, s], xin[:, s], mv[:, s, 0:1], rstd[:, s],
                                          ALU.subtract, ALU.mult).then_inc(xn_ok, 1)
                    if t >= 1:
                        v = t - 1
                        dve.wait_ge(xhi_ok, v + 1)
                        dve.tensor_tensor(xT[:, LO, :, v * P:(v + 1) * P],
                                          ptr[:, v % 2].rearrange("p (c r) -> p c r", c=KT),
                                          xT[:, HI, :, v * P:(v + 1) * P].bitcast(F32),
                                          ALU.subtract).then_inc(xlo_ok, 1)

        with nc.Block() as block:

            @block.sync
            def _(sp):
                with sp.Fori(0, KVH // 2) as kk:
                    for j in range(2):
                        k = 2 * kk + j
                        sp.wait_ge(wqlo_ok, AHEAD + k - 1)
                        sp.dma_start(wq_raw[:, j], wq_v[:, :, bass.ds(k * N, N)]).then_inc(wq_in[j], 16)
                        sp.wait_ge(kvlo_ok, AHEAD + k - 1)
                        sp.dma_start(kv_raw[:, j, 0], wk_v[:, :, bass.ds(k * DH, DH)]).then_inc(kv_in[j], 16)
                        sp.dma_start(kv_raw[:, j, 1], wv_v[:, :, bass.ds(k * DH, DH)]).then_inc(kv_in[j], 16)
                        for t in range(QT):
                            sp.wait_ge(qlo_ok, AHEAD + k * QT + t + 1)
                            row = scr["q"][bass.ds(k + (t // BT) * KVH, 1)].rearrange("o p c g s -> (o p) c g s")
                            for c in range(2):
                                sp.dma_start(row[:, c, :, (t % BT) * P:(t % BT + 1) * P],
                                             qT[:, t % 2, c].bitcast(F32).rearrange("p (g s) -> p g s", g=G)
                                             ).then_inc(q_out[t % 2], 16)
                        sp.wait_ge(kvlo_ok, AHEAD + k + 1)
                        sp.dma_start(scr["kv"][bass.ds(k, 1)].rearrange("o p a c t n -> (o p) (a c t n)"),
                                     kv[:, j].bitcast(F32).rearrange("p a c t n -> p (a c t n)")).then_inc(kv_out[j], 16)
                for j in range(2):
                    sp.wait_ge(kv_out[j], AHEAD + 16 * (KVH // 2))
                    sp.wait_ge(q_out[j], AHEAD + 32 * (KVH * QT // 2))

            @block.gpsimd
            def _(pool):
                with pool.Fori(0, KVH // 2) as kk:
                    for j in range(2):
                        for t in range(QT):
                            pool.wait_ge(ms_ok, AHEAD + (2 * kk + j) * QT + t + 1)
                            pool.tensor_tensor(rq[:, t % 2], ms[:, t % 2], mhalf[:], ALU.pow).then_inc(rq_ok, 1)

            @block.scalar
            def _(act):
                with act.Fori(0, KVH // 2) as kk:
                    for j in range(2):
                        k = 2 * kk + j
                        act.wait_ge(wq_in[j], AHEAD + 16 * kk + 16)
                        act.wait_ge(q_ps, AHEAD + (k - 1) * QT)
                        act.copy(wq[:, j, HI], wq_raw[:, j]).then_inc(wqhi_ok, 1)
                        act.wait_ge(kv_in[j], AHEAD + 32 * kk + 32)
                        act.wait_ge(kv_out[j], AHEAD + 16 * kk)
                        for a in range(2):
                            act.copy(kv[:, j, a, HI], kv_raw[:, j, a]).then_inc(kvhi_ok, 1)
                        for t in range(QT + 2):
                            if t < QT:
                                act.wait_ge(q_ps, AHEAD + k * QT + t + 1)
                                act.wait_ge(ss_ok, AHEAD + k * QT + t - 1)
                                act.activation(sq[:, t % 2], pq[:, t % 2], ACT.Square).then_inc(sq_ok, 1)
                            if t >= 2:
                                v = t - 2
                                act.wait_ge(qt_ps, AHEAD + k * QT + v + 1)
                                act.wait_ge(q_out[v % 2], AHEAD + 32 * (k * (QT // 2) + v // 2))
                                act.activation(qT[:, v % 2, HI], ptr[:, v % 2], ACT.Copy,
                                               scale=wcol[:, 3:4]).then_inc(qhi_ok, 1)

            @block.tensor
            def _(pe):
                with pe.Fori(0, KVH // 2) as kk:
                    for j in range(2):
                        k = 2 * kk + j
                        pe.wait_ge(wqlo_ok, AHEAD + k + 1)
                        for t in range(QT + 2):
                            if t < QT:
                                pe.wait_ge(qn_ok, AHEAD + k * QT + t - 1)
                                n = 0
                                for c in range(KT):
                                    for xp, wp in ((HI, HI), (LO, HI), (HI, LO)):
                                        last = pe.matmul(pq[:, t % 2], xT[:, xp, c, t * P:(t + 1) * P], wq[:, j, wp, c],
                                                         start=(n == 0), stop=(n == 3 * KT - 1))
                                        n += 1
                                last.then_inc(q_ps, 1)
                            if t >= 2:
                                v = t - 2
                                pe.wait_ge(qn_ok, AHEAD + k * QT + v + 1)
                                pe.wait_ge(qlo_ok, AHEAD + k * QT + v - 1)
                                for g in range(G):
                                    last = pe.transpose(ptr[:, v % 2, g * P:(g + 1) * P],
                                                        qn[:, v % 2, g * DH:(g + 1) * DH], ident[:])
                                last.then_inc(qt_ps, 1)

            @block.vector
            def _(dve):
                with dve.Fori(0, KVH // 2) as kk:
                    for j in range(2):
                        k = 2 * kk + j
                        dve.wait_ge(wqhi_ok, AHEAD + k + 1)
                        dve.tensor_tensor(wq[:, j, LO], wq_raw[:, j], wq[:, j, HI].bitcast(F32),
                                          ALU.subtract).then_inc(wqlo_ok, 1)
                        dve.wait_ge(kvhi_ok, AHEAD + 2 * k + 2)
                        dve.tensor_tensor(kv[:, j, :, LO], kv_raw[:, j], kv[:, j, :, HI].bitcast(F32),
                                          ALU.subtract).then_inc(kvlo_ok, 1)
                        for t in range(QT + 2):
                            if t < QT:
                                s, u = t % 2, k * QT + t
                                dve.wait_ge(sq_ok, AHEAD + u + 1)
                                dve.tensor_reduce(ss[:, s], sq[:, s].rearrange("p (g n) -> p g n", g=G),
                                                  AX.X, ALU.add).then_inc(ss_ok, 1)
                                dve.wait_ge(ss_ok, AHEAD + u + 1)
                                dve.tensor_scalar(ms[:, s], ss[:, s], 1.0 / DH, EPS_RMS,
                                                  ALU.mult, ALU.add).then_inc(ms_ok, 1)
                            if t >= 2:
                                v = t - 2
                                dve.wait_ge(qhi_ok, AHEAD + k * QT + v + 1)
                                dve.scalar_tensor_tensor(out=qT[:, v % 2, LO], in0=ptr[:, v % 2], scalar=wcol[:, 3:4],
                                                         in1=qT[:, v % 2, HI].bitcast(F32), op0=ALU.mult,
                                                         op1=ALU.subtract).then_inc(qlo_ok, 1)
                            if t < QT:
                                dve.wait_ge(rq_ok, AHEAD + u + 1)
                                dve.wait_ge(qt_ps, AHEAD + u - 1)
                                dve.tensor_tensor(qn[:, s].rearrange("p (g n) -> p g n", g=G),
                                                  pq[:, s].rearrange("p (g n) -> p g n", g=G),
                                                  rq[:, s].unsqueeze(2).to_broadcast([P, G, DH]),
                                                  ALU.mult).then_inc(qn_ok, 1)


def attend(nc, d, scr, ctx_4096):
    B, S, D, L, DH, KVH, G, KT = (d[k] for k in ("B", "S", "D", "L", "DH", "KVH", "G", "KT"))
    KV = S + L
    NT = -(-KV // P)
    LAST = KV - (NT - 1) * P
    KVP = KV + KV % 2
    NH = 2
    HALF = G * S // NH
    UT = NH * NT
    CH = [(c, min(c + 512, KVP)) for c in range(0, KVP, 512)]
    NC = len(CH)
    CT = -(-L // P)
    NP = 3
    NR = NC + 1
    assert UT % NP == 0 and UT % 2 == 0 and HALF == 512 and NC == 4 and NT > 4 * (NC - 1) + 1 and CT <= NT

    def rows(t):
        return P if t < NT - 1 else LAST

    def chunk_tiles(c):
        return range(4 * c, min(4 * c + 4, NT))

    with ExitStack() as ctx:
        sb, ps, sem = tools(nc, ctx, "att")
        ident = sb("ident", [P, P])
        ones = sb("ones", [P, P])
        mhalf = sb("mhalf", [P, 4])
        ctxT = sb("ctxT", [P, 2, KT, KVP], F32R)
        wkv = sb("wkv", [P, 2, 2, KT, DH], F32R)
        kT = sb("kT", [P, 2, KVP], F32R)
        vraw = sb("vraw", [P, NT * P])
        V = sb("V", [P, 2, NT, DH], F32R)
        sq = sb("sq", [P, 2, 512])
        var = sb("var", [P, NT])
        rk = sb("rk", [P, NT])
        q = sb("q", [P, 2, NH, HALF], F32R)
        sc = sb("sc", [P, UT, HALF])
        pr = sb("pr", [P, 2, NP, HALF], F32R)
        mx = sb("mx", [P, NH, HALF])
        sm = sb("sm", [P, NH, HALF])
        red = sb("red", [P, 4])
        den = sb("den", [P, 4])
        rden = sb("rden", [P, 4])
        diag = sb("diag", [P, 4, P])
        oraw = sb("oraw", [P, HALF])
        on = sb("on", [P, HALF])
        pqk = ps("pqk", [P, 2, 512])
        ppv = ps("ppv", [P, 512])
        pkv = ps("pkv", [P, 2, 512])
        pss = ps("pss", [P, 512])
        pred = ps("pred", [P, 512])
        pmax = ps("pmax", [P, 512])

        x_in, lat_in, w_in, o_out = sem("x_in"), sem("lat_in"), sem("w_in"), sem("o_out")
        q_in = [sem("q_in0"), sem("q_in1")]
        id_ok, cst_ok = sem("id_ok"), sem("cst_ok")
        names = ("xt_ps xhi_ok xlo_ok k_ps v_ps khi_ok klo_ok ksq_ok vraw_ok vt_ps vhi_ok vlo_ok ss_ps var_ok rk_ok "
                 "qk_ps sc_ok max_ok mt_ps red_ok diag_ok mb_ps sub_ok exp_ok phi_ok plo_ok sum_ok pv_ps oraw_ok "
                 "dt_ps den_ok rden_ok ddiag_ok db_ps on_ok").split()
        loop_sems = [sem(n) for n in names]
        (xt_ps, xhi_ok, xlo_ok, k_ps, v_ps, khi_ok, klo_ok, ksq_ok, vraw_ok, vt_ps, vhi_ok, vlo_ok, ss_ps, var_ok, rk_ok,
         qk_ps, sc_ok, max_ok, mt_ps, red_ok, diag_ok, mb_ps, sub_ok, exp_ok, phi_ok, plo_ok, sum_ok, pv_ps, oraw_ok,
         dt_ps, den_ok, rden_ok, ddiag_ok, db_ps, on_ok) = loop_sems

        LAG = 22.5
        steps = []
        for h in range(NH):
            for t in range(NT):
                p = h * NT + t
                steps += [(p, "qk", h, t), (p + .3, "copy", h, t)]
                steps += [(p + LAG - 3.8, "sub", h, t), (p + LAG - 2.8, "exp", h, t), (p + LAG - 2, "hi", h, t),
                          (p + LAG - 1.2, "lo", h, t), (p + LAG, "pv", h, t)]
                if t >= 1:
                    steps += [(p + 1, "max", h, t), (p + LAG - 1.5, "sum", h, t)]
            e = (h + 1) * NT
            steps += [(e + 1.5, "mt", h, 0), (e + 1.6, "red", h, 0), (e + 3, "mb", h, 0)]
            f = e + LAG
            steps += [(f - .6, "oraw", h, 0), (f + 1.5, "dt", h, 0), (f + 1.6, "dred", h, 0), (f + 3.3, "db", h, 0),
                      (f + 3.4, "on", h, 0), (f + 3.5, "st", h, 0)]
            steps += [(h * NT - NT + .1, "ldq", h, 0)]
        for c, (k, v, vt) in enumerate(((-10.7, -13, 11.5), (-6.7, -7.7, 15.5), (-2.7, -4.5, 19.5), (.5, 7.3, 22.7))):
            steps += [(k, "k", 0, c), (k + 1.2, "khi", 0, c), (k + 1.6, "klo", 0, c), (k + 2.2, "kn", 0, c),
                      (k + 2.3, "var", 0, c), (k + 2.4, "pow", 0, c)]
            steps += [(v, "v", 0, c), (v + 1.2, "vhi", 0, c)]
            steps += [(vt, "vt", 0, c), (vt + .3, "vthi", 0, c), (vt + .6, "vtlo", 0, c)]
        steps += [(-20.5, "ldw", 0, 0)]
        steps.sort()

        def window(own, before, after):
            w = []
            for p, what, h, t in steps:
                if own and 0 <= p < UT:
                    w.append((p, 0, what, h, t))
                if before and p >= UT:
                    w.append((p - UT, -1, what, h, t))
                if after and p < 0:
                    w.append((p + UT, 1, what, h, t))
            return [x[1:] for x in sorted(w)]

        FIRST, MIDDLE, LAST_ONE, TAIL = window(1, 0, 1), window(1, 1, 1), window(1, 1, 0), window(0, 1, 0)
        AHEAD_OF_FIRST = [(what, h, t) for p, what, h, t in steps if p < 0]

        USES = [(dn, what, c) for dn, what, _, c in MIDDLE if what in ("k", "v", "vt")]
        BANK = {(what, c): i % 2 for i, (_, what, c) in enumerate(USES)}
        assert len(USES) == 3 * NC

        def bank_before(seen, what, c):
            return next(u for u in reversed(seen) if BANK[u[1:]] == BANK[(what, c)])

        def rounds(eng, prologue, step):
            def run(n, steps_of, last):
                seen = [(dn - 1, w, c) for dn, w, c in USES]
                for dn, what, h, t in steps_of:
                    if what in ("k", "v", "vt"):
                        step(n + dn, what, h, t, before=bank_before(seen, what, t), dn=dn)
                        seen.append((dn, what, t))
                    else:
                        step(n + dn, what, h, t, last=last)

            with eng.Fori(0, B) as b:
                prologue(b)
                run(b * KVH, FIRST, False)
                with eng.Fori(1, KVH - 1) as r:
                    run(b * KVH + r, MIDDLE, False)
                run(b * KVH + (KVH - 1), LAST_ONE, False)
                run(b * KVH + KVH, TAIL, True)

        def sums(n, h, t):
            return n * (NH * (NT - 1)) + (h * (NT - 1) + max(t, 1))

        def tiles(n, h, t):
            return n * UT + (h * NT + t + 1)

        def rk_signals(n, c):
            return n * NR + (c + 1 if c < NC - 1 else NR)

        with nc.Block() as block:

            @block.gpsimd
            def _(pool):
                start_ahead(pool, loop_sems + [x_in, lat_in, w_in, o_out] + q_in)
                identity(pool, ident, id_ok)
                pool.memset(mhalf[:], -0.5).then_inc(cst_ok, 1)

            @block.vector
            def _(dve):
                dve.memset(ones[:], 1.0).then_inc(cst_ok, 1)
                dve.memset(vraw[:, KVP:], 0.0).then_inc(cst_ok, 1)
                dve.memset(ctxT[:, :, :, KV:KVP].bitcast(F32), 0.0).then_inc(cst_ok, 1)

        with nc.Block() as block:

            @block.sync
            def _(sp):
                def head(n, b):
                    return n - b * KVH

                with sp.Fori(0, B) as b:
                    n0 = b * KVH

                    def step(n, k, what, h):
                        if what == "ldw":
                            sp.wait_ge(k_ps, AHEAD + NC * n)
                            sp.wait_ge(v_ps, AHEAD + NC * n)
                            sp.dma_start(wkv[:].bitcast(F32).rearrange("p a c t n -> p (a c t n)"),
                                         scr["kv"][bass.ds(k, 1)].rearrange("o p a c t n -> (o p) (a c t n)")
                                         ).then_inc(w_in, 16)
                        elif what == "ldq":
                            sp.wait_ge(qk_ps, AHEAD + (n - 1) * UT + (h + 1) * NT)
                            sp.dma_start(q[:, :, h].bitcast(F32),
                                         scr["q"][bass.ds(n, 1), :, :, h * G // NH:(h + 1) * G // NH]
                                         .rearrange("o p c g s -> (o p) c (g s)")).then_inc(q_in[h], 16)
                        elif what == "st":
                            sp.wait_ge(on_ok, AHEAD + NH * n + h + 1)
                            sp.dma_start(scr["o"][bass.ds(n, 1), :, h * G // NH:(h + 1) * G // NH]
                                         .rearrange("o p g s -> (o p) (g s)"), on[:]).then_inc(o_out, 16)

                    step(n0, 0, "ldw", 0)
                    sp.wait_ge(plo_ok, AHEAD + n0 * UT - NT)
                    sp.wait_ge(sum_ok, AHEAD + sums(n0 - 1, 0, NT - 1))
                    full = L // P
                    sp.dma_start(sc[:, 0:full], ctx_4096[bass.ds(b, 1), 0:full * P]
                                 .rearrange("o (t p) n -> (o p) t n", p=P)).then_inc(x_in, 16)
                    sp.dma_start(sc[0:L - full * P, full], ctx_4096[bass.ds(b, 1), full * P:L]
                                 .rearrange("o p n -> (o p) n")).then_inc(x_in, 16)
                    sp.dma_start(ctxT[:, :, :, 0:S].bitcast(F32),
                                 scr["lat"][bass.ds(b, 1)].rearrange("o p c t s -> (o p) c t s")).then_inc(lat_in, 16)
                    step(n0, 0, "ldq", 0)

                    def run(n, k, steps_of):
                        for dn, what, h, t in steps_of:
                            step(n + dn, k + dn, what, h)

                    run(n0, 0, FIRST)
                    with sp.Fori(1, KVH - 1) as r:
                        run(n0 + r, r, MIDDLE)
                    run(n0 + (KVH - 1), KVH - 1, LAST_ONE)
                    run(n0 + KVH, KVH, TAIL)
                sp.wait_ge(o_out, AHEAD + 16 * NH * B * KVH)

            @block.tensor
            def _(pe):
                def project_chunk(which, bank, a, z):
                    i = 0
                    for t in range(KT):
                        for wp, xp in ((HI, HI), (LO, HI), (HI, LO)):
                            last = pe.matmul(bank, wkv[:, which, wp, t], ctxT[:, xp, t, a:z],
                                             start=(i == 0), stop=(i == 3 * KT - 1))
                            i += 1
                    return last

                def wait_for_bank(n, dn, before):
                    bn, what, c = before
                    pe.wait_ge({"k": klo_ok, "v": vraw_ok, "vt": vlo_ok}[what], AHEAD + NC * (n - dn + bn) + c + 1)

                def prologue(b):
                    n = b * KVH
                    pe.wait_ge(x_in, AHEAD + 32 * b + 32)
                    pe.wait_ge(vlo_ok, AHEAD + NC * n)
                    pe.wait_ge(vraw_ok, AHEAD + NC * n)
                    pe.wait_ge(klo_ok, AHEAD + NC * n)
                    for t in range(CT):
                        m = min(P, L - t * P)
                        if t >= 2:
                            pe.wait_ge(xlo_ok, AHEAD + b * CT + t - 1)
                        for c in range(KT):
                            last = pe.transpose(pkv[:, t % 2, c * P:c * P + m], sc[0:m, t, c * P:(c + 1) * P],
                                                ident[0:m, 0:m])
                        last.then_inc(xt_ps, 1)
                    pe.wait_ge(xlo_ok, AHEAD + b * CT + CT)
                    pe.wait_ge(lat_in, AHEAD + 16 * b + 16)
                    seen = [(0, "k", 0), (0, "k", 1)]
                    for what, h, t in AHEAD_OF_FIRST:
                        if what in ("k", "v"):
                            done = [u for u in seen[2:] if BANK[u[1:]] == BANK[(what, t)]]
                            step(n, what, h, t, before=done[-1] if done else None, dn=0)
                            seen.append((0, what, t))
                        else:
                            step(n, what, h, t)

                def step(n, what, h, t, before=None, dn=0, last=False):
                    u, T = NH * n + h, n * UT + (h * NT + t)
                    m = rows(t)
                    if what == "qk":
                        if t == 0:
                            pe.wait_ge(q_in[h], AHEAD + 16 * n + 16)
                        if h == 0 and t % 4 == 0:
                            pe.wait_ge(klo_ok, AHEAD + NC * n + t // 4 + 1)
                        pe.wait_ge(sc_ok, AHEAD + T - 1)
                        for i, (kp, qp) in enumerate(((HI, HI), (LO, HI), (HI, LO))):
                            mm = pe.matmul(pqk[0:m, (h * NT + t) % 2], kT[:, kp, t * P:t * P + m], q[:, qp, h],
                                           start=(i == 0), stop=(i == 2))
                        mm.then_inc(qk_ps, 1)
                    elif what == "mt":
                        pe.wait_ge(max_ok, AHEAD + (NT - 1) * (u + 1))
                        pe.wait_ge(on_ok, AHEAD + u - 1)
                        for c in range(4):
                            mm = pe.transpose(pred[:, c * P:(c + 1) * P], mx[:, h, c * P:(c + 1) * P], ident[:])
                        mm.then_inc(mt_ps, 1)
                    elif what == "mb":
                        pe.wait_ge(diag_ok, AHEAD + u + 1)
                        pe.wait_ge(sub_ok, AHEAD + NT * u)
                        pe.matmul(pmax[:], ones[:], diag[:].rearrange("p c n -> p (c n)"),
                                  start=True, stop=True).then_inc(mb_ps, 1)
                    elif what == "pv":
                        pe.wait_ge(plo_ok, AHEAD + T + 1)
                        if t == 0:
                            pe.wait_ge(oraw_ok, AHEAD + u)
                        if h == 0 and t % 4 == 0:
                            pe.wait_ge(vlo_ok, AHEAD + NC * n + t // 4 + 1)
                        for i, (vp, pp) in enumerate(((HI, HI), (LO, HI), (HI, LO))):
                            mm = pe.matmul(ppv[:], V[0:m, vp, t], pr[0:m, pp, (h * NT + t) % NP],
                                           start=(t == 0 and i == 0), stop=(t == NT - 1 and i == 2))
                        mm.then_inc(pv_ps, 1)
                    elif what == "dt":
                        pe.wait_ge(sum_ok, AHEAD + (NT - 1) * (u + 1))
                        if last and h == 1:
                            pe.wait_ge(on_ok, AHEAD + u)
                        else:
                            pe.wait_ge(red_ok, AHEAD + u + 2)
                        for c in range(4):
                            mm = pe.transpose(pred[:, c * P:(c + 1) * P], sm[:, h, c * P:(c + 1) * P], ident[:])
                        mm.then_inc(dt_ps, 1)
                    elif what == "db":
                        pe.wait_ge(ddiag_ok, AHEAD + u + 1)
                        pe.matmul(pred[:], ones[:], diag[:].rearrange("p c n -> p (c n)"),
                                  start=True, stop=True).then_inc(db_ps, 1)
                    elif what == "k":
                        if before is not None:
                            wait_for_bank(n, dn, before)
                        pe.wait_ge(w_in, AHEAD + 16 * n + 16)
                        a, z = CH[t]
                        project_chunk(0, pkv[:, BANK["k", t], 0:z - a], a, z).then_inc(k_ps, 1)
                    elif what == "kn":
                        pe.wait_ge(ksq_ok, AHEAD + NC * n + t + 1)
                        pe.wait_ge(var_ok, AHEAD + rk_signals(n, t - 1) if t else AHEAD + n * NR)
                        for i in chunk_tiles(t):
                            mm = pe.matmul(pss[0:rows(i), i:i + 1], sq[:, t % 2, (i % 4) * P:(i % 4) * P + rows(i)],
                                           ones[:, 0:1], start=True, stop=True)
                        mm.then_inc(ss_ps, 1)
                    elif what == "v":
                        if before is not None:
                            wait_for_bank(n, dn, before)
                        pe.wait_ge(w_in, AHEAD + 16 * n + 16)
                        a, z = CH[t]
                        project_chunk(1, pkv[:, BANK["v", t], 0:z - a], a, z).then_inc(v_ps, 1)
                    elif what == "vt":
                        wait_for_bank(n, dn, before)
                        pe.wait_ge(vraw_ok, AHEAD + NC * n + t + 1)
                        for i in chunk_tiles(t):
                            mm = pe.transpose(pkv[:, BANK["vt", t], (i % 4) * P:(i % 4 + 1) * P],
                                              vraw[:, i * P:(i + 1) * P], ident[:])
                        mm.then_inc(vt_ps, 1)

                rounds(pe, prologue, step)

            @block.scalar
            def _(act):
                def prologue(b):
                    for t in range(CT):
                        m = min(P, L - t * P)
                        act.wait_ge(xt_ps, AHEAD + b * CT + t + 1)
                        act.copy(ctxT[:, HI, :, S + t * P:S + t * P + m],
                                 pkv[:, t % 2].rearrange("p (c r) -> p c r", c=KT)[:, :, 0:m]).then_inc(xhi_ok, 1)
                    for what, h, t in AHEAD_OF_FIRST:
                        step(b * KVH, what, h, t)

                def step(n, what, h, t, before=None, dn=0, last=False):
                    u, T = NH * n + h, n * UT + (h * NT + t)
                    m, s = rows(t), h * NT + t
                    if what == "copy":
                        act.wait_ge(qk_ps, AHEAD + T + 1)
                        act.wait_ge(plo_ok, AHEAD + T + 1 - UT)
                        act.wait_ge(sum_ok, AHEAD + sums(n - 1, h, t))
                        if h == 0 and t % 4 == 0:
                            act.wait_ge(rk_ok, AHEAD + rk_signals(n, t // 4))
                        act.activation(sc[0:m, s], pqk[0:m, s % 2], ACT.Copy, scale=rk[0:m, t:t + 1]).then_inc(sc_ok, 1)
                    elif what == "exp":
                        act.wait_ge(sub_ok, AHEAD + T + 1)
                        act.activation(sc[0:m, s], sc[0:m, s], ACT.Exp).then_inc(exp_ok, 1)
                    elif what == "hi":
                        act.wait_ge(exp_ok, AHEAD + T + 1)
                        act.wait_ge(pv_ps, AHEAD + T - NP + 1)
                        act.copy(pr[0:m, HI, s % NP], sc[0:m, s]).then_inc(phi_ok, 1)
                    elif what == "oraw":
                        act.wait_ge(pv_ps, AHEAD + NT * (u + 1))
                        act.wait_ge(on_ok, AHEAD + u)
                        act.copy(oraw[:], ppv[:]).then_inc(oraw_ok, 1)
                    elif what == "khi":
                        a, z = CH[t]
                        act.wait_ge(k_ps, AHEAD + NC * n + t + 1)
                        act.wait_ge(qk_ps, AHEAD + tiles(n - 1, 1, chunk_tiles(t)[-1]))
                        act.copy(kT[:, HI, a:z], pkv[:, BANK["k", t], 0:z - a]).then_inc(khi_ok, 1)
                        act.wait_ge(ss_ps, AHEAD + NC * n + t - 1)
                        act.activation(sq[:, t % 2, 0:z - a], pkv[:, BANK["k", t], 0:z - a], ACT.Square).then_inc(ksq_ok, 1)
                    elif what == "vhi":
                        a, z = CH[t]
                        act.wait_ge(v_ps, AHEAD + NC * n + t + 1)
                        act.wait_ge(vt_ps, AHEAD + NC * (n - 1) + t + 1)
                        act.copy(vraw[:, a:z], pkv[:, BANK["v", t], 0:z - a]).then_inc(vraw_ok, 1)
                    elif what == "vthi":
                        act.wait_ge(vt_ps, AHEAD + NC * n + t + 1)
                        act.wait_ge(pv_ps, AHEAD + tiles(n - 1, 1, chunk_tiles(t)[-1]))
                        w = len(chunk_tiles(t))
                        act.copy(V[:, HI, 4 * t:4 * t + w],
                                 pkv[:, BANK["vt", t], 0:w * P].rearrange("p (a n) -> p a n", n=P)).then_inc(vhi_ok, 1)

                rounds(act, prologue, step)

            @block.vector
            def _(dve):
                def prologue(b):
                    for t in range(CT):
                        m = min(P, L - t * P)
                        dve.wait_ge(xhi_ok, AHEAD + b * CT + t + 1)
                        dve.tensor_tensor(ctxT[:, LO, :, S + t * P:S + t * P + m],
                                          pkv[:, t % 2].rearrange("p (c r) -> p c r", c=KT)[:, :, 0:m],
                                          ctxT[:, HI, :, S + t * P:S + t * P + m].bitcast(F32),
                                          ALU.subtract).then_inc(xlo_ok, 1)
                    for what, h, t in AHEAD_OF_FIRST:
                        step(b * KVH, what, h, t)

                def diagonal(col):
                    return dve.tensor_tensor(diag[:], ident[:].unsqueeze(1).to_broadcast([P, 4, P]),
                                             col[:].unsqueeze(2).to_broadcast([P, 4, P]), ALU.mult)

                def step(n, what, h, t, before=None, dn=0, last=False):
                    u, T = NH * n + h, n * UT + (h * NT + t)
                    m, s = rows(t), h * NT + t
                    if what == "max":
                        dve.wait_ge(sc_ok, AHEAD + T + 1)
                        if t == 1:
                            dve.wait_ge(mt_ps, AHEAD + u - 1)
                            dve.tensor_tensor(mx[:, h], sc[:, s - 1], sc[:, s], ALU.max).then_inc(max_ok, 1)
                        else:
                            dve.wait_ge(max_ok, AHEAD + (NT - 1) * u + t - 1)
                            dve.tensor_tensor(mx[0:m, h], mx[0:m, h], sc[0:m, s], ALU.max).then_inc(max_ok, 1)
                    elif what == "red":
                        dve.wait_ge(mt_ps, AHEAD + u + 1)
                        dve.tensor_reduce(red[:], pred[:].rearrange("p (c n) -> p c n", c=4), AX.X, ALU.max).then_inc(red_ok, 1)
                        dve.wait_ge(red_ok, AHEAD + u + 1)
                        dve.wait_ge(db_ps, AHEAD + u - 1)
                        diagonal(red).then_inc(diag_ok, 1)
                    elif what == "sub":
                        if t == 0:
                            dve.wait_ge(mb_ps, AHEAD + u + 1)
                        dve.tensor_tensor(sc[0:m, s], sc[0:m, s], pmax[0:m], ALU.subtract).then_inc(sub_ok, 1)
                    elif what == "lo":
                        dve.wait_ge(phi_ok, AHEAD + T + 1)
                        dve.tensor_tensor(pr[0:m, LO, s % NP], sc[0:m, s], pr[0:m, HI, s % NP].bitcast(F32),
                                          ALU.subtract).then_inc(plo_ok, 1)
                    elif what == "dred":
                        dve.wait_ge(dt_ps, AHEAD + u + 1)
                        dve.tensor_reduce(den[:], pred[:].rearrange("p (c n) -> p c n", c=4), AX.X, ALU.add).then_inc(den_ok, 1)
                        dve.wait_ge(den_ok, AHEAD + u + 1)
                        dve.reciprocal(rden[:], den[:]).then_inc(rden_ok, 1)
                        dve.wait_ge(rden_ok, AHEAD + u + 1)
                        if last and h == 1:
                            dve.wait_ge(db_ps, AHEAD + u)
                        else:
                            dve.wait_ge(mb_ps, AHEAD + u + 2)
                        diagonal(rden).then_inc(ddiag_ok, 1)
                    elif what == "on":
                        dve.wait_ge(db_ps, AHEAD + u + 1)
                        dve.wait_ge(oraw_ok, AHEAD + u + 1)
                        dve.wait_ge(o_out, AHEAD + 16 * u)
                        dve.tensor_tensor(on[:], oraw[:], pred[:], ALU.mult).then_inc(on_ok, 1)
                    elif what == "klo":
                        a, z = CH[t]
                        dve.wait_ge(ksq_ok, AHEAD + NC * n + t + 1)
                        dve.tensor_tensor(kT[:, LO, a:z], pkv[:, BANK["k", t], 0:z - a], kT[:, HI, a:z].bitcast(F32),
                                          ALU.subtract).then_inc(klo_ok, 1)
                    elif what == "var":
                        dve.wait_ge(ss_ps, AHEAD + NC * n + t + 1)
                        dve.wait_ge(rk_ok, AHEAD + rk_signals(n - 1, t))
                        i, z = chunk_tiles(t)[0], min(chunk_tiles(t)[-1] + 1, NT - 1)
                        dve.tensor_scalar(var[:, i:z], pss[:, i:z], 1.0 / DH, EPS_RMS, ALU.mult, ALU.add).then_inc(var_ok, 1)
                        if t == NC - 1:
                            dve.tensor_scalar(var[0:LAST, NT - 1:NT], pss[0:LAST, NT - 1:NT], 1.0 / DH, EPS_RMS,
                                              ALU.mult, ALU.add).then_inc(var_ok, 1)
                    elif what == "vtlo":
                        w = len(chunk_tiles(t))
                        dve.wait_ge(vhi_ok, AHEAD + NC * n + t + 1)
                        dve.tensor_tensor(V[:, LO, 4 * t:4 * t + w],
                                          pkv[:, BANK["vt", t], 0:w * P].rearrange("p (a n) -> p a n", n=P),
                                          V[:, HI, 4 * t:4 * t + w].bitcast(F32), ALU.subtract).then_inc(vlo_ok, 1)

                rounds(dve, prologue, step)

            @block.gpsimd
            def _(pool):
                def prologue(b):
                    for what, h, t in AHEAD_OF_FIRST:
                        step(b * KVH, what, h, t)

                def step(n, what, h, t, before=None, dn=0, last=False):
                    u, T = NH * n + h, n * UT + (h * NT + t)
                    m, s = rows(t), h * NT + t
                    if what == "sum":
                        pool.wait_ge(exp_ok, AHEAD + T + 1)
                        if t == 1:
                            pool.wait_ge(dt_ps, AHEAD + u - 1)
                            pool.tensor_tensor(sm[:, h], sc[:, s - 1], sc[:, s], ALU.add).then_inc(sum_ok, 1)
                        else:
                            pool.wait_ge(sum_ok, AHEAD + (NT - 1) * u + t - 1)
                            pool.tensor_tensor(sm[0:m, h], sm[0:m, h], sc[0:m, s], ALU.add).then_inc(sum_ok, 1)
                    elif what == "pow":
                        i, z = chunk_tiles(t)[0], min(chunk_tiles(t)[-1] + 1, NT - 1)
                        pool.wait_ge(var_ok, AHEAD + rk_signals(n, t))
                        pool.wait_ge(sc_ok, AHEAD + tiles(n - 1, 1, chunk_tiles(t)[-1]))
                        pool.tensor_tensor(rk[:, i:z], var[:, i:z], mhalf[:, 0:z - i], ALU.pow).then_inc(rk_ok, 1)
                        if t == NC - 1:
                            pool.tensor_tensor(rk[0:LAST, NT - 1:NT], var[0:LAST, NT - 1:NT], mhalf[0:LAST, 0:1],
                                               ALU.pow).then_inc(rk_ok, 1)

                rounds(pool, prologue, step)


def gate_column(sp, act, g, gcol, g_in, g_ok):
    if sp is not None:
        sp.dma_start(gcol[:, 0:1], g.partition_broadcast(P)).then_inc(g_in, 16)
    if act is not None:
        act.wait_ge(g_in, 16)
        act.activation(gcol[:, 1:2], gcol[:, 0:1], ACT.Tanh).then_inc(g_ok, 1)


def project(nc, d, scr, x, Wo, g_xattn):
    B, S, D, DH, HEADS, KVH, G, QT = (d[k] for k in ("B", "S", "D", "DH", "HEADS", "KVH", "G", "QT"))
    BT = S // P
    HH = HEADS // 2
    WC = 4
    with ExitStack() as ctx:
        sb, ps, sem = tools(nc, ctx, "out")
        wo = sb("wo", [P, 2, HEADS, D], F32R)
        wraw = sb("wraw", [P, 2, WC, D])
        oraw = wraw[:].rearrange("p a b c -> p (a b c)").rearrange("p (a h s) -> p a h s", a=2, h=HH)
        o = sb("o", [P, 2, 2, HH, P], F32R)
        xin = sb("xin", [P, 2, D])
        x2 = sb("x2", [P, 2, D])
        gcol = sb("gcol", [P, 2])
        po = ps("po", [P, 2, 512])
        g_in, g_ok = sem("g_in"), sem("g_ok")
        w_in, o_in = [sem("w_in0"), sem("w_in1")], [sem("o_in0"), sem("o_in1")]
        x_in, x2_out = [sem("x_in0"), sem("x_in1")], [sem("x2_out0"), sem("x2_out1")]
        whi_ok, wlo_ok, ohi_ok, olo_ok, o_ps, x2_ok = (
            sem(n) for n in ("whi_ok", "wlo_ok", "ohi_ok", "olo_ok", "o_ps", "x2_ok"))

        wo_v = Wo.rearrange("(h p) n -> p h n", p=P)
        x_v = x.rearrange("b (t p) n -> b t p n", p=P)

        with nc.Block() as block:

            @block.sync
            def _(sp):
                gate_column(sp, None, g_xattn, gcol, g_in, g_ok)
                for i in range(HEADS // WC):
                    if i >= 2:
                        sp.wait_ge(wlo_ok, i - 1)
                    sp.dma_start(wraw[:, i % 2], wo_v[:, WC * i:WC * i + WC]).then_inc(w_in[i % 2], 16)

            @block.gpsimd
            def _(pool):
                start_ahead(pool, o_in + x_in + x2_out + [ohi_ok, olo_ok, o_ps, x2_ok])

            @block.scalar
            def _(act):
                gate_column(None, act, g_xattn, gcol, g_in, g_ok)
                for i in range(HEADS // WC):
                    act.wait_ge(w_in[i % 2], 16 * (i // 2) + 16)
                    act.copy(wo[:, HI, WC * i:WC * i + WC], wraw[:, i % 2]).then_inc(whi_ok, 1)

            @block.vector
            def _(dve):
                for i in range(HEADS // WC):
                    dve.wait_ge(whi_ok, i + 1)
                    dve.tensor_tensor(wo[:, LO, WC * i:WC * i + WC], wraw[:, i % 2],
                                      wo[:, HI, WC * i:WC * i + WC].bitcast(F32), ALU.subtract).then_inc(wlo_ok, 1)

        with nc.Block() as block:

            @block.sync
            def _(sp):
                with sp.Fori(0, B) as b:
                    for t in range(BT):
                        i = b * BT + t
                        sp.wait_ge(x2_ok, AHEAD + i - 1)
                        sp.dma_start(xin[:, t], x_v[bass.ds(b, 1), t].rearrange("o p n -> (o p) n")).then_inc(x_in[t], 16)
                        for e in range(2):
                            sp.wait_ge(olo_ok, AHEAD + 2 * i + e - 1)
                            for k in range(KVH // 2):
                                sp.dma_start(oraw[:, e, k * G:(k + 1) * G],
                                             scr["o"][bass.ds(b * KVH + (e * (KVH // 2) + k), 1), :, :, t * P:(t + 1) * P]
                                             .rearrange("o p g s -> (o p) g s")).then_inc(o_in[e], 16)
                    for t in range(BT):
                        sp.wait_ge(x2_ok, AHEAD + b * BT + t + 1)
                        sp.dma_start(scr["x2"][bass.ds((b * BT + t) * P, P)], x2[:, t]).then_inc(x2_out[t], 16)
                for t in range(2):
                    sp.wait_ge(x2_out[t], AHEAD + 16 * (QT // 2))

            @block.scalar
            def _(act):
                with act.Fori(0, B) as b:
                    for t in range(BT):
                        for e in range(2):
                            v = b * (2 * BT) + (2 * t + e)
                            act.wait_ge(o_in[e], AHEAD + (b * BT + t) * (16 * KVH // 2) + 16 * KVH // 2)
                            act.wait_ge(o_ps, AHEAD + v - 1)
                            act.copy(o[:, e, HI], oraw[:, e]).then_inc(ohi_ok, 1)

            @block.vector
            def _(dve):
                with dve.Fori(0, B) as b:
                    for t in range(BT):
                        i = b * BT + t
                        for e in range(2):
                            dve.wait_ge(ohi_ok, AHEAD + 2 * i + e + 1)
                            dve.tensor_tensor(o[:, e, LO], oraw[:, e], o[:, e, HI].bitcast(F32),
                                              ALU.subtract).then_inc(olo_ok, 1)
                        dve.wait_ge(o_ps, AHEAD + 2 * i + 2)
                        dve.wait_ge(x_in[t], AHEAD + 16 * b + 16)
                        dve.wait_ge(x2_out[t], AHEAD + 16 * b)
                        dve.scalar_tensor_tensor(out=x2[:, t], in0=po[:, t], scalar=gcol[:, 1:2], in1=xin[:, t],
                                                 op0=ALU.mult, op1=ALU.add).then_inc(x2_ok, 1)

            @block.tensor
            def _(pe):
                with pe.Fori(0, B) as b:
                    for t in range(BT):
                        i = b * BT + t
                        pe.wait_ge(x2_ok, AHEAD + i - 1)
                        for e in range(2):
                            pe.wait_ge(olo_ok, AHEAD + 2 * i + e + 1)
                            for h in range(HH):
                                for p, (op, wp) in enumerate(((HI, HI), (LO, HI), (HI, LO))):
                                    mm = pe.matmul(po[:, t], o[:, e, op, h], wo[:, wp, e * HH + h],
                                                   start=(e == 0 and h == 0 and p == 0),
                                                   stop=(e == 1 and h == HH - 1 and p == 2))
                            mm.then_inc(o_ps, 1)


def ffn(nc, d, scr, g_ffn, c1_w, c2_w, w1, w2t, out):
    S, D, KT, QT = (d[k] for k in ("S", "D", "KT", "QT"))
    RANK = c1_w.shape[0]
    INTER = w1.shape[0]
    IT = INTER // P
    BLK = 32
    CW = 448
    NCH = INTER // CW
    NB = CW // BLK
    GT = [(g, min(g + 4, IT)) for g in range(0, IT, 4)]
    assert NCH * CW == INTER and IT * P == INTER
    with ExitStack() as ctx:
        sb, ps, sem = tools(nc, ctx, "ffn")
        ident = sb("ident", [P, P])
        mhalf = sb("mhalf", [P, 1])
        rank = sb("rank", [P, NB, BLK])
        gcol = sb("gcol", [P, 2])
        stage = sb("stage", [P, 2, D])
        c1 = sb("c1", [RANK, D])
        c2 = sb("c2", [P, IT, RANK])
        c1T = sb("c1T", [P, KT, RANK])
        c2T = sb("c2T", [RANK, INTER])
        w1T = sb("w1T", [P, 2, KT, INTER], F32R)
        w2 = sb("w2", [P, 2, IT, D], F32R)
        xin = sb("xin", [P, 2, D])
        stats = sb("stats", [P, QT, 6])
        mv = sb("mv", [P, QT, 2])
        veps = sb("veps", [P, QT])
        rstd = sb("rstd", [P, QT])
        xn = sb("xn", [P, 2, D])
        xT = sb("xT", [P, 2, KT, P], F32R)
        xTf = sb("xTf", [P, KT, P])
        tT = sb("tT", [RANK, P])
        bm = sb("bm", [P, NB])
        bs = sb("bs", [P, NB])
        eq = sb("eq", [P, NB, BLK])
        score = sb("score", [P, NB, BLK])
        mask = sb("mask", [P, NCH, NB, BLK])
        hm = sb("hm", [P, INTER])
        hT = sb("hT", [P, 2, IT, P], F32R)
        y = sb("y", [P, 2, D])
        ptr = ps("ptr", [P, 2, 512])
        pt = ps("pt", [P, 512])
        pin = ps("pin", [P, 2, 512])
        ph = ps("ph", [P, 2, 512])
        py = ps("py", [P, 512])
        g_in, g_ok, id_ok, cst_ok, c_in, c_ps, c_ok = (
            sem(n) for n in ("g_in", "g_ok", "id_ok", "cst_ok", "c_in", "c_ps", "c_ok"))
        s_in = [sem("s_in0"), sem("s_in1")]
        w_ps, whi_ok, wlo_ok = sem("w_ps"), sem("whi_ok"), sem("wlo_ok")
        l_in, l_out = [sem("l_in0"), sem("l_in1")], [sem("l_out0"), sem("l_out1")]
        bn, var_ok, ve_ok, rstd_ok, ln_ok = (sem(n) for n in ("bn", "var_ok", "ve_ok", "rstd_ok", "ln_ok"))
        x_in, y_out = [sem("x_in0"), sem("x_in1")], [sem("y_out0"), sem("y_out1")]
        n_in = [sem("n_in0"), sem("n_in1")]
        names = ("xt_ps xhi_ok xf_ok xlo_ok t_ps t_ok in_ps bm_ok eq_ok score_ok bs_ok "
                 "mask_ok h_ps hm_ok ht_ps hhi_ok hlo_ok y_ps y_ok").split()
        loop_sems = [sem(n) for n in names]
        (xt_ps, xhi_ok, xf_ok, xlo_ok, t_ps, t_ok, in_ps, bm_ok, eq_ok, score_ok, bs_ok,
         mask_ok, h_ps, hm_ok, ht_ps, hhi_ok, hlo_ok, y_ps, y_ok) = loop_sems

        w1_t = w1.rearrange("(t p) n -> t p n", p=P)
        w2_t = w2t.rearrange("(t p) n -> t p n", p=P)
        out_v = out.rearrange("b s n -> (b s) n")
        NW = 2 * IT

        def normalised(sp, t):
            sp.wait_ge(ln_ok, t + 1)
            sp.dma_start(scr["xn"][t * P:(t + 1) * P], xn[:, t % 2]).then_inc(l_out[t % 2], 16)

        with nc.Block() as block:

            @block.sync
            def _(sp):
                gate_column(sp, None, g_ffn, gcol, g_in, g_ok)
                sp.dma_start(c1[:], c1_w).then_inc(c_in, 16)
                sp.dma_start(c2[:], c2_w.rearrange("(t p) r -> p t r", p=P)).then_inc(c_in, 16)
                for t in range(QT):
                    if t >= 2:
                        sp.wait_ge(ln_ok, t - 1)
                    sp.dma_start(xin[:, t % 2], scr["x2"][t * P:(t + 1) * P]).then_inc(l_in[t % 2], 16)
                    if t >= 1:
                        normalised(sp, t - 1)
                normalised(sp, QT - 1)
                for i in range(NW):
                    if i >= 2:
                        sp.wait_ge(wlo_ok, i - 1)
                    sp.dma_start(stage[:, i % 2], w1_t[i] if i < IT else w2_t[i - IT]).then_inc(s_in[i % 2], 16)
                for t in range(2):
                    sp.wait_ge(l_out[t], 16 * (QT // 2))

            @block.gpsimd
            def _(pool):
                start_ahead(pool, loop_sems + x_in + n_in + y_out)
                identity(pool, ident, id_ok)
                pool.memset(mhalf[:], -0.5).then_inc(cst_ok, 1)
                pool.wait_ge(cst_ok, 1)
                for t in range(QT):
                    pool.wait_ge(ve_ok, t + 1)
                    pool.tensor_tensor(rstd[:, t:t + 1], veps[:, t:t + 1], mhalf[:], ALU.pow).then_inc(rstd_ok, 1)
                for i in range(BLK):
                    pool.memset(rank[:, :, i:i + 1], float(BLK - i)).then_inc(cst_ok, 1)

            @block.scalar
            def _(act):
                gate_column(None, act, g_ffn, gcol, g_in, g_ok)
                for i in range(NW):
                    if i < IT:
                        act.wait_ge(w_ps, i + 1)
                        act.copy(w1T[:, HI, :, i * P:(i + 1) * P],
                                 ptr[:, i % 2].rearrange("p (c r) -> p c r", c=KT)).then_inc(whi_ok, 1)
                    else:
                        act.wait_ge(s_in[i % 2], 16 * (i // 2) + 16)
                        act.copy(w2[:, HI, i - IT], stage[:, i % 2]).then_inc(whi_ok, 1)

            @block.tensor
            def _(pe):
                pe.wait_ge(id_ok, 2)
                pe.wait_ge(c_in, 32)
                for c in range(KT):
                    mm = pe.transpose(pt[:, c * RANK:(c + 1) * RANK], c1[:, c * P:(c + 1) * P], ident[0:RANK, 0:RANK])
                mm.then_inc(c_ps, 1)
                for g, (a, z) in enumerate(GT):
                    bank = (pin[:, 0], pin[:, 1], ph[:, 0], ph[:, 1])[g]
                    for t in range(a, z):
                        mm = pe.transpose(bank[0:RANK, (t - a) * P:(t - a + 1) * P], c2[:, t], ident[:])
                    mm.then_inc(c_ps, 1)
                for i in range(IT):
                    pe.wait_ge(s_in[i % 2], 16 * (i // 2) + 16)
                    if i >= 2:
                        pe.wait_ge(wlo_ok, i - 1)
                    for c in range(KT):
                        mm = pe.transpose(ptr[:, i % 2, c * P:(c + 1) * P], stage[:, i % 2, c * P:(c + 1) * P], ident[:])
                    mm.then_inc(w_ps, 1)

            @block.vector
            def _(dve):
                for t in range(QT):
                    dve.wait_ge(l_in[t % 2], 16 * (t // 2) + 16)
                    dve.bn_stats(stats[:, t], xin[:, t % 2]).then_inc(bn, 1)
                    dve.wait_ge(bn, t + 1)
                    dve.bn_aggr(mv[:, t], stats[:, t]).then_inc(var_ok, 1)
                    dve.wait_ge(var_ok, t + 1)
                    dve.tensor_scalar(veps[:, t:t + 1], mv[:, t, 1:2], EPS_LN, None, ALU.add).then_inc(ve_ok, 1)
                    dve.wait_ge(rstd_ok, t + 1)
                    if t >= 2:
                        dve.wait_ge(l_out[t % 2], 16 * (t // 2))
                    dve.tensor_scalar(xn[:, t % 2], xin[:, t % 2], mv[:, t, 0:1], rstd[:, t:t + 1],
                                      ALU.subtract, ALU.mult).then_inc(ln_ok, 1)
                dve.wait_ge(c_ps, 1)
                dve.tensor_copy(c1T[:].rearrange("p c r -> p (c r)"), pt[:, 0:KT * RANK]).then_inc(c_ok, 1)
                for g, (a, z) in enumerate(GT):
                    bank = (pin[:, 0], pin[:, 1], ph[:, 0], ph[:, 1])[g]
                    dve.wait_ge(c_ps, g + 2)
                    dve.tensor_copy(c2T[:, a * P:z * P], bank[0:RANK, 0:(z - a) * P]).then_inc(c_ok, 1)
                for i in range(NW):
                    dve.wait_ge(whi_ok, i + 1)
                    if i < IT:
                        dve.tensor_tensor(w1T[:, LO, :, i * P:(i + 1) * P], ptr[:, i % 2].rearrange("p (c r) -> p c r", c=KT),
                                          w1T[:, HI, :, i * P:(i + 1) * P].bitcast(F32), ALU.subtract).then_inc(wlo_ok, 1)
                    else:
                        dve.tensor_tensor(w2[:, LO, i - IT], stage[:, i % 2], w2[:, HI, i - IT].bitcast(F32),
                                          ALU.subtract).then_inc(wlo_ok, 1)

        with nc.Block() as block:

            def tiles(eng, tile):
                with eng.Fori(0, QT // 2) as r:
                    for j in range(2):
                        tile(2 * r + j, r, j)

            @block.sync
            def _(sp):
                with sp.Fori(0, QT // 2) as r:
                    for j in range(2):
                        sp.wait_ge(y_ok, AHEAD + 2 * r + j - 1)
                        sp.dma_start(xn[:, j], scr["xn"][bass.ds((2 * r + j) * P, P)]).then_inc(n_in[j], 16)
                        sp.dma_start(xin[:, j], scr["x2"][bass.ds((2 * r + j) * P, P)]).then_inc(x_in[j], 16)
                    for j in range(2):
                        sp.wait_ge(y_ok, AHEAD + 2 * r + j + 1)
                        sp.dma_start(out_v[bass.ds((2 * r + j) * P, P)], y[:, j]).then_inc(y_out[j], 16)
                for j in range(2):
                    sp.wait_ge(y_out[j], AHEAD + 16 * (QT // 2))

            @block.scalar
            def _(act):
                def tile(i, r, j):
                    act.wait_ge(xt_ps, AHEAD + i + 1)
                    act.wait_ge(y_ps, AHEAD + i)
                    act.copy(xT[:, HI].rearrange("p c r -> p (c r)"), ptr[:, 0]).then_inc(xhi_ok, 1)
                    act.copy(xTf[:].rearrange("p c r -> p (c r)"), ptr[:, 0]).then_inc(xf_ok, 1)
                    act.wait_ge(t_ps, AHEAD + i + 1)
                    act.copy(tT[:], pt[0:RANK, 0:P]).then_inc(t_ok, 1)
                    for g, (a, z) in enumerate(GT):
                        act.wait_ge(ht_ps, AHEAD + i * len(GT) + g + 1)
                        act.copy(hT[:, HI, a:z].rearrange("p c r -> p (c r)"),
                                 ptr[:, (g + 1) % 2, 0:(z - a) * P]).then_inc(hhi_ok, 1)
                tiles(act, tile)

            @block.tensor
            def _(pe):
                def tile(i, r, j):
                    pe.wait_ge(n_in[j], AHEAD + 16 * r + 16)
                    for c in range(KT):
                        mm = pe.transpose(ptr[:, 0, c * P:(c + 1) * P], xn[:, j, c * P:(c + 1) * P], ident[:])
                    mm.then_inc(xt_ps, 1)
                    pe.wait_ge(xf_ok, AHEAD + i + 1)
                    for c in range(KT):
                        mm = pe.matmul(pt[0:RANK, 0:P], c1T[:, c], xTf[:, c], start=(c == 0), stop=(c == KT - 1))
                    mm.then_inc(t_ps, 1)
                    pe.wait_ge(t_ok, AHEAD + i + 1)
                    for c in range(NCH):
                        pe.wait_ge(eq_ok, AHEAD + i * NCH + c - 1)
                        pe.matmul(pin[:, c % 2, 0:CW], tT[:], c2T[:, c * CW:(c + 1) * CW],
                                  start=True, stop=True).then_inc(in_ps, 1)
                        if c == 0:
                            pe.wait_ge(xlo_ok, AHEAD + i + 1)
                        pe.wait_ge(hm_ok, AHEAD + i * NCH + c - 1)
                        for t in range(KT):
                            for p, (xp, wp) in enumerate(((HI, HI), (LO, HI), (HI, LO))):
                                mm = pe.matmul(ph[:, c % 2, 0:CW], xT[:, xp, t], w1T[:, wp, t, c * CW:(c + 1) * CW],
                                               start=(t == 0 and p == 0), stop=(t == KT - 1 and p == 2))
                        mm.then_inc(h_ps, 1)
                    for g, (a, z) in enumerate(GT):
                        pe.wait_ge(hm_ok, AHEAD + i * NCH + (z * P + CW - 1) // CW)
                        if g == 0:
                            pe.wait_ge(hlo_ok, AHEAD + i * len(GT))
                        elif g >= 1:
                            pe.wait_ge(hlo_ok, AHEAD + i * len(GT) + g - 1)
                        for t in range(a, z):
                            mm = pe.transpose(ptr[:, (g + 1) % 2, (t - a) * P:(t - a + 1) * P], hm[:, t * P:(t + 1) * P], ident[:])
                        mm.then_inc(ht_ps, 1)
                    for g, (a, z) in enumerate(GT):
                        pe.wait_ge(hlo_ok, AHEAD + i * len(GT) + g + 1)
                        if g == 0:
                            pe.wait_ge(y_ok, AHEAD + i)
                        for t in range(a, z):
                            for p, (hp, wp) in enumerate(((HI, HI), (LO, HI), (HI, LO))):
                                mm = pe.matmul(py[:], hT[:, hp, t], w2[:, wp, t],
                                               start=(t == 0 and p == 0), stop=(t == IT - 1 and p == 2))
                    mm.then_inc(y_ps, 1)
                tiles(pe, tile)

            @block.vector
            def _(dve):
                def blocks(a):
                    return a.rearrange("p (n b) -> p n b", b=BLK)

                def tile(i, r, j):
                    dve.wait_ge(xf_ok, AHEAD + i + 1)
                    dve.tensor_tensor(xT[:, LO].rearrange("p c r -> p (c r)"), ptr[:, 0],
                                      xT[:, HI].bitcast(F32).rearrange("p c r -> p (c r)"), ALU.subtract).then_inc(xlo_ok, 1)
                    for c in range(NCH):
                        u = i * NCH + c
                        dve.wait_ge(in_ps, AHEAD + u + 1)
                        inner = blocks(pin[:, c % 2, 0:CW])
                        dve.tensor_reduce(bm[:], inner, AX.X, ALU.max).then_inc(bm_ok, 1)
                        dve.wait_ge(bm_ok, AHEAD + u + 1)
                        dve.tensor_tensor(eq[:], inner, bm[:].unsqueeze(2).to_broadcast([P, NB, BLK]),
                                          ALU.is_equal).then_inc(eq_ok, 1)
                        dve.wait_ge(eq_ok, AHEAD + u + 1)
                        dve.tensor_tensor(score[:], eq[:], rank[:], ALU.mult).then_inc(score_ok, 1)
                        dve.wait_ge(score_ok, AHEAD + u + 1)
                        dve.tensor_reduce(bs[:], score[:], AX.X, ALU.max).then_inc(bs_ok, 1)
                        dve.wait_ge(bs_ok, AHEAD + u + 1)
                        dve.tensor_tensor(mask[:, c], score[:], bs[:].unsqueeze(2).to_broadcast([P, NB, BLK]),
                                          ALU.is_equal).then_inc(mask_ok, 1)
                        dve.wait_ge(mask_ok, AHEAD + u + 1)
                        dve.wait_ge(h_ps, AHEAD + u + 1)
                        if c == 0:
                            dve.wait_ge(ht_ps, AHEAD + i * len(GT))
                        dve.scalar_tensor_tensor(out=hm[:, c * CW:(c + 1) * CW], in0=ph[:, c % 2, 0:CW], scalar=0.0,
                                                 in1=mask[:, c].rearrange("p n b -> p (n b)"),
                                                 op0=ALU.max, op1=ALU.mult).then_inc(hm_ok, 1)
                    for g, (a, z) in enumerate(GT):
                        dve.wait_ge(hhi_ok, AHEAD + i * len(GT) + g + 1)
                        dve.tensor_tensor(hT[:, LO, a:z].rearrange("p c r -> p (c r)"), ptr[:, (g + 1) % 2, 0:(z - a) * P],
                                          hT[:, HI, a:z].bitcast(F32).rearrange("p c r -> p (c r)"),
                                          ALU.subtract).then_inc(hlo_ok, 1)
                    dve.wait_ge(y_ps, AHEAD + i + 1)
                    dve.wait_ge(x_in[j], AHEAD + 16 * r + 16)
                    dve.wait_ge(y_out[j], AHEAD + 16 * r)
                    dve.scalar_tensor_tensor(out=y[:, j], in0=py[:], scalar=gcol[:, 1:2], in1=xin[:, j],
                                             op0=ALU.mult, op1=ALU.add).then_inc(y_ok, 1)
                tiles(dve, tile)


_INS = ["x", "ctx_4096", "g_xattn", "g_ffn", "L0_xattn_Wq", "L0_xattn_Wk", "L0_xattn_Wv", "L0_xattn_Wo",
        "L0_xattn_q_norm_w", "L0_xattn_k_norm_w", "L0_ffn_c1_w", "L0_ffn_c2_w", "L0_ffn_w1", "L0_ffn_w2t"]


def kernel(**inputs):
    import numpy as np
    import concourse.bacc as bacc
    from concourse.bass_utils import run_bass_kernel_spmd

    nc = bacc.Bacc("TRN2", target_bir_lowering=False, num_devices=1)
    arrays, args = {}, []
    for name in _INS:
        a = np.ascontiguousarray(inputs[name])
        arrays[f"in_{name}"] = a
        args.append(nc.dram_tensor(f"in_{name}", a.shape, mybir.dt.from_np(a.dtype), kind="ExternalInput").ap())
    out = nc.dram_tensor("out_x", inputs["x"].shape, F32, kind="ExternalOutput").ap()
    program(nc, *args, out)
    r = run_bass_kernel_spmd(nc, [arrays], core_ids=[0])
    return r.results[0]["out_x"]
```

```python
from contextlib import ExitStack

import concourse.bass as bass
from concourse import mybir

F32 = mybir.dt.float32
F32R = mybir.dt.float32r
ALU = mybir.AluOpType
ACT = mybir.ActivationFunctionType
AX = mybir.AxisListType

P = 128
AHEAD = 32
HI, LO = 0, 1
EPS_LN = 1e-5
EPS_RMS = 1e-6


def passes(w, m):
    return ((w[HI], m[HI]), (w[LO], m[HI]), (w[HI], m[LO]))


def program(nc, x, ctx_4096, g_xattn, g_ffn, Wq, Wk, Wv, Wo, q_norm_w, k_norm_w, c1_w, c2_w, w1, w2t, out):
    B, S, D = x.shape
    L = ctx_4096.shape[1]
    DH = q_norm_w.shape[0]
    HEADS = Wq.shape[1] // DH
    KVH = Wk.shape[1] // DH
    G = HEADS // KVH
    KT = D // P
    QT = B * S // P
    dims = dict(B=B, S=S, D=D, L=L, DH=DH, HEADS=HEADS, KVH=KVH, G=G, KT=KT, QT=QT)

    scratch = dict(
        lat=nc.dram_tensor("lat_scr", [B, P, 2, KT, S], F32, kind="Internal").ap(),
        q=nc.dram_tensor("q_scr", [B * KVH, P, 2, G, S], F32, kind="Internal").ap(),
        kv=nc.dram_tensor("kv_scr", [KVH, P, 2, 2, KT, DH], F32, kind="Internal").ap(),
        o=nc.dram_tensor("o_scr", [B * KVH, P, G, S], F32, kind="Internal").ap(),
        x2=nc.dram_tensor("x2_scr", [QT * P, D], F32, kind="Internal").ap(),
        xn=nc.dram_tensor("xn_scr", [QT * P, D], F32, kind="Internal").ap(),
    )
    prepare(nc, dims, scratch, x, Wq, Wk, Wv, q_norm_w, k_norm_w)
    attend(nc, dims, scratch, ctx_4096)
    project(nc, dims, scratch, x, Wo, g_xattn)
    ffn(nc, dims, scratch, g_ffn, c1_w, c2_w, w1, w2t, out)


def tools(nc, ctx, tag):
    def sb(name, shape, dt=F32):
        return ctx.enter_context(nc.sbuf_tensor(f"{tag}_{name}", shape, dt))

    def ps(name, shape):
        return ctx.enter_context(nc.psum_tensor(f"{tag}_{name}", shape, F32))

    def sem(name):
        return ctx.enter_context(nc.semaphore(f"{tag}_{name}"))
    return sb, ps, sem


def start_ahead(pool, sems):
    for s in sems:
        pool.sem_inc(s, AHEAD)


def pipeline(eng, units, width, steps, emit, first=()):
    def window(w):
        found = [(place % width, place // width, what) for place, *what in steps if 0 <= w - place // width < units]
        found += [(place % width, place // width, what) for place, *what in first if w == place // width]
        return [(int(late), what) for _, late, what in sorted(found, key=lambda f: f[0])]

    w, end = int(min(p // width for p, *_ in steps)), units + int(max(p // width for p, *_ in steps))
    while w < end:
        todo, z = window(w), w + 1
        while z < end and window(z) == todo:
            z += 1
        last = max(late for late, _ in todo)
        if z - w > 1:
            with eng.Fori(w - last, z - last) as n:
                for late, what in todo:
                    emit(n + (last - late), *what)
        else:
            for late, what in todo:
                emit(w - late, *what)
        w = z


def identity(pool, ident, sem):
    pool.memset(ident[:], 0.0).then_inc(sem, 1)
    pool.wait_ge(sem, 1)
    pool.affine_select(out=ident[:], in_=ident[:], compare_op=ALU.not_equal, fill=1.0, base=0,
                       pattern=[[-1, P]], channel_multiplier=1).then_inc(sem, 1)



def prepare(nc, d, scr, x, Wq, Wk, Wv, q_norm_w, k_norm_w):
    B, S, D, DH, KVH, G, KT, QT = (d[k] for k in ("B", "S", "D", "DH", "KVH", "G", "KT", "QT"))
    N = G * DH
    SCALE = float(DH) ** -0.5
    BT = S // P
    NJ = 2
    UT = NJ * QT
    with ExitStack() as ctx:
        sb, ps, sem = tools(nc, ctx, "pre")
        ident = sb("ident", [P, P])
        mhalf = sb("mhalf", [P, QT])
        wcol = sb("wcol", [P, 4])
        xin = sb("xin", [P, QT, D])
        stats = sb("stats", [P, QT, 6])
        mv = sb("mv", [P, QT, 2])
        veps = sb("veps", [P, QT])
        rstd = sb("rstd", [P, QT])
        xn = sb("xn", [P, 2, D])
        xT = sb("xT", [P, 2, KT, QT * P], F32R)
        wq_raw = sb("wq_raw", [P, NJ, KT, N])
        wq = sb("wq", [P, NJ, 2, KT, N], F32R)
        kv_raw = sb("kv_raw", [P, NJ, 2, KT, DH])
        kv = sb("kv", [P, NJ, 2, 2, KT, DH], F32R)
        sq = sb("sq", [P, 2, N])
        ss = sb("ss", [P, 2, G])
        ms = sb("ms", [P, 2, G])
        rq = sb("rq", [P, 2, G])
        qn = sb("qn", [P, 2, N])
        qT = sb("qT", [P, 4, 2, N], F32R)
        ptr = ps("ptr", [P, 2, 512])
        pq = ps("pq", [P, 4, 512])

        w_in, lat_out, id_ok, half_ok, w_ok = (sem(n) for n in ("w_in", "lat_out", "id_ok", "half_ok", "w_ok"))
        x_in = [sem(f"x_in{t}") for t in range(QT // 2)]
        bn, var_ok, ve_ok, rstd_ok, xn_ok, xt_ps, xhi_ok, xlo_ok = (
            sem(n) for n in ("bn", "var_ok", "ve_ok", "rstd_ok", "xn_ok", "xt_ps", "xhi_ok", "xlo_ok"))
        wq_in = [sem("wq_in0"), sem("wq_in1")]
        kv_in = [sem("kv_in0"), sem("kv_in1")]
        kv_out = [sem("kv_out0"), sem("kv_out1")]
        q_out = [sem(f"q_out{i}") for i in range(4)]
        wqhi_ok, wqlo_ok, kvhi_ok, kvlo_ok = (sem(n) for n in ("wqhi_ok", "wqlo_ok", "kvhi_ok", "kvlo_ok"))
        q_ps, sq_ok, ss_ok, ms_ok, rq_ok, qn_ok, qt_ps, qhi_ok, qlo_ok = (
            sem(n) for n in ("q_ps", "sq_ok", "ss_ok", "ms_ok", "rq_ok", "qn_ok", "qt_ps", "qhi_ok", "qlo_ok"))

        x_t = x.rearrange("b (t p) n -> (b t) p n", p=P)
        wq_v = Wq.rearrange("(t p) n -> p t n", p=P)
        wk_v = Wk.rearrange("(t p) n -> p t n", p=P)
        wv_v = Wv.rearrange("(t p) n -> p t n", p=P)

        steps = []
        for j in range(NJ):
            o = j * QT
            steps += [(o - 12, "load", j, 0), (o - 5.5, "whi", j, 0), (o - 4.5, "wlo", j, 0), (o - 3.5, "kvhi", j, 0),
                      (o - 3.3, "kvlo", j, 0), (o - 3, "kvst", j, 0)]
            for t in range(QT):
                p = o + t
                steps += [(p, "q", j, t), (p + .9, "sq", j, t), (p + 1.1, "ss", j, t), (p + 1.2, "pow", j, t),
                          (p + 1.9, "qn", j, t), (p + 2.7, "qt", j, t), (p + 2.8, "qhi", j, t), (p + 3.2, "qlo", j, t),
                          (p + 3.3, "qst", j, t)]
        steps.sort()

        with nc.Block() as block:

            @block.gpsimd
            def _(pool):
                start_ahead(pool, wq_in + kv_in + kv_out + q_out + [wqhi_ok, wqlo_ok, kvhi_ok, kvlo_ok,
                            q_ps, sq_ok, ss_ok, ms_ok, rq_ok, qn_ok, qt_ps, qhi_ok, qlo_ok])

        with nc.Block() as block:

            def run(eng, emit):
                pipeline(eng, KVH // NJ, UT, steps, emit)

            @block.sync
            def _(sp):
                for t in range(QT // 2):
                    sp.dma_start(xin[:, 2 * t:2 * t + 2], x_t[2 * t:2 * t + 2].rearrange("t p n -> p t n")).then_inc(x_in[t], 16)
                sp.dma_start(wcol[:, 0:1], q_norm_w.rearrange("(p o) -> p o", o=1)).then_inc(w_in, 16)
                sp.dma_start(wcol[:, 1:2], k_norm_w.rearrange("(p o) -> p o", o=1)).then_inc(w_in, 16)

                def step(n, what, j, t):
                    k, v = NJ * n + j, n * UT + (j * QT + t)
                    if what == "load":
                        sp.wait_ge(wqlo_ok, AHEAD + k - 1)
                        sp.wait_ge(kvlo_ok, AHEAD + k - 1)
                        sp.dma_start(wq_raw[:, j], wq_v[:, :, bass.ds(k * N, N)]).then_inc(wq_in[j], 16)
                        sp.dma_start(kv_raw[:, j, 0], wk_v[:, :, bass.ds(k * DH, DH)]).then_inc(kv_in[j], 16)
                        sp.dma_start(kv_raw[:, j, 1], wv_v[:, :, bass.ds(k * DH, DH)]).then_inc(kv_in[j], 16)
                    elif what == "kvst":
                        sp.wait_ge(kvlo_ok, AHEAD + k + 1)
                        sp.dma_start(scr["kv"][bass.ds(k, 1)].rearrange("o p a c t n -> (o p) (a c t n)"),
                                     kv[:, j].bitcast(F32).rearrange("p a c t n -> p (a c t n)")).then_inc(kv_out[j], 16)
                    elif what == "qst":
                        sp.wait_ge(qlo_ok, AHEAD + v + 1)
                        row = scr["q"][bass.ds(k + (t // BT) * KVH, 1)].rearrange("o p c g s -> (o p) c g s")
                        for c in range(2):
                            sp.dma_start(row[:, c, :, (t % BT) * P:(t % BT + 1) * P],
                                         qT[:, t % 4, c].bitcast(F32).rearrange("p (g s) -> p g s", g=G)
                                         ).then_inc(q_out[t % 4], 16)
                run(sp, step)
                for b in range(B):
                    sp.dma_start(scr["lat"][b], xT[:, :, :, b * S:(b + 1) * S].bitcast(F32)).then_inc(lat_out, 16)
                sp.wait_ge(lat_out, 16 * B)
                for j in range(NJ):
                    sp.wait_ge(kv_out[j], AHEAD + 16 * (KVH // NJ))
                for i in range(4):
                    sp.wait_ge(q_out[i], AHEAD + 32 * (KVH * QT // 4))

            @block.gpsimd
            def _(pool):
                identity(pool, ident, id_ok)
                pool.memset(mhalf[:], -0.5).then_inc(half_ok, 1)
                pool.wait_ge(half_ok, 1)
                pool.wait_ge(ve_ok, QT)
                pool.tensor_tensor(rstd[:], veps[:], mhalf[:], ALU.pow).then_inc(rstd_ok, 1)

                def step(n, what, j, t):
                    if what == "pow":
                        pool.wait_ge(ms_ok, AHEAD + n * UT + (j * QT + t + 1))
                        pool.tensor_tensor(rq[:, t % 2], ms[:, t % 2], mhalf[:, 0:G], ALU.pow).then_inc(rq_ok, 1)
                run(pool, step)

            @block.scalar
            def _(act):
                for t in range(QT):
                    act.wait_ge(xt_ps, t + 1)
                    act.copy(xT[:, HI, :, t * P:(t + 1) * P],
                             ptr[:, t % 2].rearrange("p (c r) -> p c r", c=KT)).then_inc(xhi_ok, 1)

                def step(n, what, j, t):
                    k, v = NJ * n + j, n * UT + (j * QT + t)
                    if what == "whi":
                        act.wait_ge(wq_in[j], AHEAD + 16 * n + 16)
                        act.wait_ge(q_ps, AHEAD + (k - 1) * QT)
                        act.copy(wq[:, j, HI], wq_raw[:, j]).then_inc(wqhi_ok, 1)
                    elif what == "kvhi":
                        act.wait_ge(kv_in[j], AHEAD + 32 * n + 32)
                        act.wait_ge(kv_out[j], AHEAD + 16 * n)
                        for a in range(2):
                            act.copy(kv[:, j, a, HI], kv_raw[:, j, a]).then_inc(kvhi_ok, 1)
                    elif what == "sq":
                        act.wait_ge(q_ps, AHEAD + v + 1)
                        act.wait_ge(ss_ok, AHEAD + v - 1)
                        act.activation(sq[:, t % 2], pq[:, t % 4], ACT.Square).then_inc(sq_ok, 1)
                    elif what == "qhi":
                        act.wait_ge(qt_ps, AHEAD + v + 1)
                        act.wait_ge(q_out[t % 4], AHEAD + 32 * (k * (QT // 4) + t // 4))
                        act.activation(qT[:, t % 4, HI], ptr[:, t % 2], ACT.Copy, scale=wcol[:, 3:4]).then_inc(qhi_ok, 1)
                act.wait_ge(w_ok, 2)
                run(act, step)

            @block.tensor
            def _(pe):
                pe.wait_ge(id_ok, 2)
                for t in range(QT):
                    pe.wait_ge(xn_ok, t + 1)
                    if t >= 2:
                        pe.wait_ge(xlo_ok, t - 1)
                    for c in range(KT):
                        last = pe.transpose(ptr[:, t % 2, c * P:(c + 1) * P], xn[:, t % 2, c * P:(c + 1) * P], ident[:])
                    last.then_inc(xt_ps, 1)
                pe.wait_ge(xlo_ok, QT)

                def step(n, what, j, t):
                    k, v = NJ * n + j, n * UT + (j * QT + t)
                    if what == "q":
                        if t == 0:
                            pe.wait_ge(wqlo_ok, AHEAD + k + 1)
                        pe.wait_ge(qn_ok, AHEAD + v - 3)
                        i = 0
                        for c in range(KT):
                            for xp, wp in ((HI, HI), (LO, HI), (HI, LO)):
                                mm = pe.matmul(pq[:, t % 4], xT[:, xp, c, t * P:(t + 1) * P], wq[:, j, wp, c],
                                               start=(i == 0), stop=(i == 3 * KT - 1))
                                i += 1
                        mm.then_inc(q_ps, 1)
                    elif what == "qt":
                        pe.wait_ge(qn_ok, AHEAD + v + 1)
                        pe.wait_ge(qlo_ok, AHEAD + v - 1)
                        for g in range(G):
                            mm = pe.transpose(ptr[:, t % 2, g * P:(g + 1) * P], qn[:, t % 2, g * DH:(g + 1) * DH], ident[:])
                        mm.then_inc(qt_ps, 1)
                run(pe, step)

            @block.vector
            def _(dve):
                for t in range(QT):
                    dve.wait_ge(x_in[t // 2], 16)
                    dve.bn_stats(stats[:, t], xin[:, t]).then_inc(bn, 1)
                for t in range(QT):
                    dve.wait_ge(bn, t + 1)
                    dve.bn_aggr(mv[:, t], stats[:, t]).then_inc(var_ok, 1)
                for t in range(QT):
                    dve.wait_ge(var_ok, t + 1)
                    dve.tensor_scalar(veps[:, t:t + 1], mv[:, t, 1:2], EPS_LN, None, ALU.add).then_inc(ve_ok, 1)
                dve.wait_ge(rstd_ok, 1)
                for t in range(QT + 1):
                    if t < QT:
                        if t >= 2:
                            dve.wait_ge(xt_ps, t - 1)
                        dve.tensor_scalar(xn[:, t % 2], xin[:, t], mv[:, t, 0:1], rstd[:, t:t + 1],
                                          ALU.subtract, ALU.mult).then_inc(xn_ok, 1)
                    if t >= 1:
                        v = t - 1
                        dve.wait_ge(xhi_ok, v + 1)
                        dve.tensor_tensor(xT[:, LO, :, v * P:(v + 1) * P],
                                          ptr[:, v % 2].rearrange("p (c r) -> p c r", c=KT),
                                          xT[:, HI, :, v * P:(v + 1) * P].bitcast(F32),
                                          ALU.subtract).then_inc(xlo_ok, 1)
                dve.wait_ge(w_in, 32)
                dve.tensor_tensor(wcol[:, 2:3], wcol[:, 0:1], wcol[:, 1:2], ALU.mult).then_inc(w_ok, 1)
                dve.wait_ge(w_ok, 1)
                dve.tensor_scalar(wcol[:, 3:4], wcol[:, 2:3], SCALE, None, ALU.mult).then_inc(w_ok, 1)
                dve.wait_ge(w_ok, 2)

                def step(n, what, j, t):
                    k, v, s = NJ * n + j, n * UT + (j * QT + t), t % 2
                    if what == "wlo":
                        dve.wait_ge(wqhi_ok, AHEAD + k + 1)
                        dve.tensor_tensor(wq[:, j, LO], wq_raw[:, j], wq[:, j, HI].bitcast(F32),
                                          ALU.subtract).then_inc(wqlo_ok, 1)
                    elif what == "kvlo":
                        dve.wait_ge(kvhi_ok, AHEAD + 2 * k + 2)
                        dve.tensor_tensor(kv[:, j, :, LO], kv_raw[:, j], kv[:, j, :, HI].bitcast(F32),
                                          ALU.subtract).then_inc(kvlo_ok, 1)
                    elif what == "ss":
                        dve.wait_ge(sq_ok, AHEAD + v + 1)
                        dve.tensor_reduce(ss[:, s], sq[:, s].rearrange("p (g n) -> p g n", g=G),
                                          AX.X, ALU.add).then_inc(ss_ok, 1)
                        dve.wait_ge(ss_ok, AHEAD + v + 1)
                        dve.tensor_scalar(ms[:, s], ss[:, s], 1.0 / DH, EPS_RMS, ALU.mult, ALU.add).then_inc(ms_ok, 1)
                    elif what == "qn":
                        dve.wait_ge(rq_ok, AHEAD + v + 1)
                        dve.wait_ge(qt_ps, AHEAD + v - 1)
                        dve.tensor_tensor(qn[:, s].rearrange("p (g n) -> p g n", g=G),
                                          pq[:, t % 4].rearrange("p (g n) -> p g n", g=G),
                                          rq[:, s].unsqueeze(2).to_broadcast([P, G, DH]), ALU.mult).then_inc(qn_ok, 1)
                    elif what == "qlo":
                        dve.wait_ge(qhi_ok, AHEAD + v + 1)
                        dve.scalar_tensor_tensor(out=qT[:, t % 4, LO], in0=ptr[:, s], scalar=wcol[:, 3:4],
                                                 in1=qT[:, t % 4, HI].bitcast(F32), op0=ALU.mult,
                                                 op1=ALU.subtract).then_inc(qlo_ok, 1)
                run(dve, step)


def attend(nc, d, scr, ctx_4096):
    B, S, D, L, DH, KVH, G, KT = (d[k] for k in ("B", "S", "D", "L", "DH", "KVH", "G", "KT"))
    KV = S + L
    NT = -(-KV // P)
    LAST = KV - (NT - 1) * P
    KVP = KV + KV % 2
    NH = 2
    HALF = G * S // NH
    UT = NH * NT
    CH = [(c, min(c + 512, KVP)) for c in range(0, KVP, 512)]
    NC = len(CH)
    CT = -(-L // P)
    NP = 3
    NR = NC + 1
    assert UT % NP == 0 and UT % 2 == 0 and HALF == 512 and NC == 4 and NT > 4 * (NC - 1) + 1 and CT <= NT

    def rows(t):
        return P if t < NT - 1 else LAST

    def chunk_tiles(c):
        return range(4 * c, min(4 * c + 4, NT))

    with ExitStack() as ctx:
        sb, ps, sem = tools(nc, ctx, "att")
        ident = sb("ident", [P, P])
        ones = sb("ones", [P, P])
        mhalf = sb("mhalf", [P, 4])
        ctxT = sb("ctxT", [P, 2, KT, KVP], F32R)
        wkv = sb("wkv", [P, 2, 2, KT, DH], F32R)
        kT = sb("kT", [P, 2, KVP], F32R)
        vraw = sb("vraw", [P, NT * P])
        V = sb("V", [P, 2, NT, DH], F32R)
        sq = sb("sq", [P, 2, 512])
        var = sb("var", [P, NT])
        rk = sb("rk", [P, NT])
        q = sb("q", [P, 2, NH, HALF], F32R)
        sc = sb("sc", [P, UT, HALF])
        pr = sb("pr", [P, 2, NP, HALF], F32R)
        mx = sb("mx", [P, NH, HALF])
        sm = sb("sm", [P, NH, HALF])
        red = sb("red", [P, 4])
        den = sb("den", [P, 4])
        rden = sb("rden", [P, 4])
        diag = sb("diag", [P, 4, P])
        oraw = sb("oraw", [P, HALF])
        on = sb("on", [P, HALF])
        pqk = ps("pqk", [P, 2, 512])
        ppv = ps("ppv", [P, 512])
        pkv = ps("pkv", [P, 2, 512])
        pss = ps("pss", [P, 512])
        pred = ps("pred", [P, 512])
        pmax = ps("pmax", [P, 512])

        x_in, lat_in, w_in, o_out = sem("x_in"), sem("lat_in"), sem("w_in"), sem("o_out")
        q_in = [sem("q_in0"), sem("q_in1")]
        id_ok, cst_ok = sem("id_ok"), sem("cst_ok")
        names = ("xt_ps xhi_ok xlo_ok k_ps v_ps khi_ok klo_ok ksq_ok vraw_ok vt_ps vhi_ok vlo_ok ss_ps var_ok rk_ok "
                 "qk_ps sc_ok max_ok mt_ps red_ok diag_ok mb_ps sub_ok exp_ok phi_ok plo_ok sum_ok pv_ps oraw_ok "
                 "dt_ps den_ok rden_ok ddiag_ok db_ps on_ok").split()
        loop_sems = [sem(n) for n in names]
        (xt_ps, xhi_ok, xlo_ok, k_ps, v_ps, khi_ok, klo_ok, ksq_ok, vraw_ok, vt_ps, vhi_ok, vlo_ok, ss_ps, var_ok, rk_ok,
         qk_ps, sc_ok, max_ok, mt_ps, red_ok, diag_ok, mb_ps, sub_ok, exp_ok, phi_ok, plo_ok, sum_ok, pv_ps, oraw_ok,
         dt_ps, den_ok, rden_ok, ddiag_ok, db_ps, on_ok) = loop_sems

        LAG = 22.5
        steps = []
        for h in range(NH):
            for t in range(NT):
                p = h * NT + t
                steps += [(p, "qk", h, t), (p + .3, "copy", h, t)]
                steps += [(p + LAG - 3.8, "sub", h, t), (p + LAG - 2.8, "exp", h, t), (p + LAG - 2, "hi", h, t),
                          (p + LAG - 1.2, "lo", h, t), (p + LAG, "pv", h, t)]
                if t >= 1:
                    steps += [(p + 1, "max", h, t), (p + LAG - 1.5, "sum", h, t)]
            e = (h + 1) * NT
            steps += [(e + 1.5, "mt", h, 0), (e + 1.6, "red", h, 0), (e + 3, "mb", h, 0)]
            f = e + LAG
            steps += [(f - .6, "oraw", h, 0), (f + 1.5, "dt", h, 0), (f + 1.6, "dred", h, 0), (f + 3.3, "db", h, 0),
                      (f + 3.4, "on", h, 0), (f + 3.5, "st", h, 0)]
            steps += [(h * NT - NT + .1, "ldq", h, 0)]
        for c, (k, v, vt) in enumerate(((-10.7, -13, 11.5), (-6.7, -7.7, 15.5), (-2.7, -4.5, 19.5), (.5, 7.3, 22.7))):
            steps += [(k, "k", 0, c), (k + 1.2, "khi", 0, c), (k + 1.6, "klo", 0, c), (k + 2.2, "kn", 0, c),
                      (k + 2.3, "var", 0, c), (k + 2.4, "pow", 0, c)]
            steps += [(v, "v", 0, c), (v + 1.2, "vhi", 0, c)]
            steps += [(vt, "vt", 0, c), (vt + .3, "vthi", 0, c), (vt + .6, "vtlo", 0, c)]
        steps += [(-20.5, "ldw", 0, 0)]
        steps.sort()

        def window(own, before, after):
            w = []
            for p, what, h, t in steps:
                if own and 0 <= p < UT:
                    w.append((p, 0, what, h, t))
                if before and p >= UT:
                    w.append((p - UT, -1, what, h, t))
                if after and p < 0:
                    w.append((p + UT, 1, what, h, t))
            return [x[1:] for x in sorted(w)]

        FIRST, MIDDLE, LAST_ONE, TAIL = window(1, 0, 1), window(1, 1, 1), window(1, 1, 0), window(0, 1, 0)
        AHEAD_OF_FIRST = [(what, h, t) for p, what, h, t in steps if p < 0]

        USES = [(dn, what, c) for dn, what, _, c in MIDDLE if what in ("k", "v", "vt")]
        BANK = {(what, c): i % 2 for i, (_, what, c) in enumerate(USES)}
        assert len(USES) == 3 * NC

        def bank_before(seen, what, c):
            return next(u for u in reversed(seen) if BANK[u[1:]] == BANK[(what, c)])

        def rounds(eng, prologue, step):
            def run(n, steps_of, last):
                seen = [(dn - 1, w, c) for dn, w, c in USES]
                for dn, what, h, t in steps_of:
                    if what in ("k", "v", "vt"):
                        step(n + dn, what, h, t, before=bank_before(seen, what, t), dn=dn)
                        seen.append((dn, what, t))
                    else:
                        step(n + dn, what, h, t, last=last)

            with eng.Fori(0, B) as b:
                prologue(b)
                run(b * KVH, FIRST, False)
                with eng.Fori(1, KVH - 1) as r:
                    run(b * KVH + r, MIDDLE, False)
                run(b * KVH + (KVH - 1), LAST_ONE, False)
                run(b * KVH + KVH, TAIL, True)

        def sums(n, h, t):
            return n * (NH * (NT - 1)) + (h * (NT - 1) + max(t, 1))

        def tiles(n, h, t):
            return n * UT + (h * NT + t + 1)

        def rk_signals(n, c):
            return n * NR + (c + 1 if c < NC - 1 else NR)

        with nc.Block() as block:

            @block.gpsimd
            def _(pool):
                start_ahead(pool, loop_sems + [x_in, lat_in, w_in, o_out] + q_in)
                identity(pool, ident, id_ok)
                pool.memset(mhalf[:], -0.5).then_inc(cst_ok, 1)

            @block.vector
            def _(dve):
                dve.memset(ones[:], 1.0).then_inc(cst_ok, 1)
                dve.memset(vraw[:, KVP:], 0.0).then_inc(cst_ok, 1)
                dve.memset(ctxT[:, :, :, KV:KVP].bitcast(F32), 0.0).then_inc(cst_ok, 1)

        with nc.Block() as block:

            @block.sync
            def _(sp):
                def head(n, b):
                    return n - b * KVH

                with sp.Fori(0, B) as b:
                    n0 = b * KVH

                    def step(n, k, what, h):
                        if what == "ldw":
                            sp.wait_ge(k_ps, AHEAD + NC * n)
                            sp.wait_ge(v_ps, AHEAD + NC * n)
                            sp.dma_start(wkv[:].bitcast(F32).rearrange("p a c t n -> p (a c t n)"),
                                         scr["kv"][bass.ds(k, 1)].rearrange("o p a c t n -> (o p) (a c t n)")
                                         ).then_inc(w_in, 16)
                        elif what == "ldq":
                            sp.wait_ge(qk_ps, AHEAD + (n - 1) * UT + (h + 1) * NT)
                            sp.dma_start(q[:, :, h].bitcast(F32),
                                         scr["q"][bass.ds(n, 1), :, :, h * G // NH:(h + 1) * G // NH]
                                         .rearrange("o p c g s -> (o p) c (g s)")).then_inc(q_in[h], 16)
                        elif what == "st":
                            sp.wait_ge(on_ok, AHEAD + NH * n + h + 1)
                            sp.dma_start(scr["o"][bass.ds(n, 1), :, h * G // NH:(h + 1) * G // NH]
                                         .rearrange("o p g s -> (o p) (g s)"), on[:]).then_inc(o_out, 16)

                    step(n0, 0, "ldw", 0)
                    sp.wait_ge(plo_ok, AHEAD + n0 * UT - NT)
                    sp.wait_ge(sum_ok, AHEAD + sums(n0 - 1, 0, NT - 1))
                    full = L // P
                    sp.dma_start(sc[:, 0:full], ctx_4096[bass.ds(b, 1), 0:full * P]
                                 .rearrange("o (t p) n -> (o p) t n", p=P)).then_inc(x_in, 16)
                    sp.dma_start(sc[0:L - full * P, full], ctx_4096[bass.ds(b, 1), full * P:L]
                                 .rearrange("o p n -> (o p) n")).then_inc(x_in, 16)
                    sp.dma_start(ctxT[:, :, :, 0:S].bitcast(F32),
                                 scr["lat"][bass.ds(b, 1)].rearrange("o p c t s -> (o p) c t s")).then_inc(lat_in, 16)
                    step(n0, 0, "ldq", 0)

                    def run(n, k, steps_of):
                        for dn, what, h, t in steps_of:
                            step(n + dn, k + dn, what, h)

                    run(n0, 0, FIRST)
                    with sp.Fori(1, KVH - 1) as r:
                        run(n0 + r, r, MIDDLE)
                    run(n0 + (KVH - 1), KVH - 1, LAST_ONE)
                    run(n0 + KVH, KVH, TAIL)
                sp.wait_ge(o_out, AHEAD + 16 * NH * B * KVH)

            @block.tensor
            def _(pe):
                def project_chunk(which, bank, a, z):
                    i = 0
                    for t in range(KT):
                        for wp, xp in ((HI, HI), (LO, HI), (HI, LO)):
                            last = pe.matmul(bank, wkv[:, which, wp, t], ctxT[:, xp, t, a:z],
                                             start=(i == 0), stop=(i == 3 * KT - 1))
                            i += 1
                    return last

                def wait_for_bank(n, dn, before):
                    bn, what, c = before
                    pe.wait_ge({"k": klo_ok, "v": vraw_ok, "vt": vlo_ok}[what], AHEAD + NC * (n - dn + bn) + c + 1)

                def prologue(b):
                    n = b * KVH
                    pe.wait_ge(x_in, AHEAD + 32 * b + 32)
                    pe.wait_ge(vlo_ok, AHEAD + NC * n)
                    pe.wait_ge(vraw_ok, AHEAD + NC * n)
                    pe.wait_ge(klo_ok, AHEAD + NC * n)
                    for t in range(CT):
                        m = min(P, L - t * P)
                        if t >= 2:
                            pe.wait_ge(xlo_ok, AHEAD + b * CT + t - 1)
                        for c in range(KT):
                            last = pe.transpose(pkv[:, t % 2, c * P:c * P + m], sc[0:m, t, c * P:(c + 1) * P],
                                                ident[0:m, 0:m])
                        last.then_inc(xt_ps, 1)
                    pe.wait_ge(xlo_ok, AHEAD + b * CT + CT)
                    pe.wait_ge(lat_in, AHEAD + 16 * b + 16)
                    seen = [(0, "k", 0), (0, "k", 1)]
                    for what, h, t in AHEAD_OF_FIRST:
                        if what in ("k", "v"):
                            done = [u for u in seen[2:] if BANK[u[1:]] == BANK[(what, t)]]
                            step(n, what, h, t, before=done[-1] if done else None, dn=0)
                            seen.append((0, what, t))
                        else:
                            step(n, what, h, t)

                def step(n, what, h, t, before=None, dn=0, last=False):
                    u, T = NH * n + h, n * UT + (h * NT + t)
                    m = rows(t)
                    if what == "qk":
                        if t == 0:
                            pe.wait_ge(q_in[h], AHEAD + 16 * n + 16)
                        if h == 0 and t % 4 == 0:
                            pe.wait_ge(klo_ok, AHEAD + NC * n + t // 4 + 1)
                        pe.wait_ge(sc_ok, AHEAD + T - 1)
                        for i, (kp, qp) in enumerate(((HI, HI), (LO, HI), (HI, LO))):
                            mm = pe.matmul(pqk[0:m, (h * NT + t) % 2], kT[:, kp, t * P:t * P + m], q[:, qp, h],
                                           start=(i == 0), stop=(i == 2))
                        mm.then_inc(qk_ps, 1)
                    elif what == "mt":
                        pe.wait_ge(max_ok, AHEAD + (NT - 1) * (u + 1))
                        pe.wait_ge(on_ok, AHEAD + u - 1)
                        for c in range(4):
                            mm = pe.transpose(pred[:, c * P:(c + 1) * P], mx[:, h, c * P:(c + 1) * P], ident[:])
                        mm.then_inc(mt_ps, 1)
                    elif what == "mb":
                        pe.wait_ge(diag_ok, AHEAD + u + 1)
                        pe.wait_ge(sub_ok, AHEAD + NT * u)
                        pe.matmul(pmax[:], ones[:], diag[:].rearrange("p c n -> p (c n)"),
                                  start=True, stop=True).then_inc(mb_ps, 1)
                    elif what == "pv":
                        pe.wait_ge(plo_ok, AHEAD + T + 1)
                        if t == 0:
                            pe.wait_ge(oraw_ok, AHEAD + u)
                        if h == 0 and t % 4 == 0:
                            pe.wait_ge(vlo_ok, AHEAD + NC * n + t // 4 + 1)
                        for i, (vp, pp) in enumerate(((HI, HI), (LO, HI), (HI, LO))):
                            mm = pe.matmul(ppv[:], V[0:m, vp, t], pr[0:m, pp, (h * NT + t) % NP],
                                           start=(t == 0 and i == 0), stop=(t == NT - 1 and i == 2))
                        mm.then_inc(pv_ps, 1)
                    elif what == "dt":
                        pe.wait_ge(sum_ok, AHEAD + (NT - 1) * (u + 1))
                        if last and h == 1:
                            pe.wait_ge(on_ok, AHEAD + u)
                        else:
                            pe.wait_ge(red_ok, AHEAD + u + 2)
                        for c in range(4):
                            mm = pe.transpose(pred[:, c * P:(c + 1) * P], sm[:, h, c * P:(c + 1) * P], ident[:])
                        mm.then_inc(dt_ps, 1)
                    elif what == "db":
                        pe.wait_ge(ddiag_ok, AHEAD + u + 1)
                        pe.matmul(pred[:], ones[:], diag[:].rearrange("p c n -> p (c n)"),
                                  start=True, stop=True).then_inc(db_ps, 1)
                    elif what == "k":
                        if before is not None:
                            wait_for_bank(n, dn, before)
                        pe.wait_ge(w_in, AHEAD + 16 * n + 16)
                        a, z = CH[t]
                        project_chunk(0, pkv[:, BANK["k", t], 0:z - a], a, z).then_inc(k_ps, 1)
                    elif what == "kn":
                        pe.wait_ge(ksq_ok, AHEAD + NC * n + t + 1)
                        pe.wait_ge(var_ok, AHEAD + rk_signals(n, t - 1) if t else AHEAD + n * NR)
                        for i in chunk_tiles(t):
                            mm = pe.matmul(pss[0:rows(i), i:i + 1], sq[:, t % 2, (i % 4) * P:(i % 4) * P + rows(i)],
                                           ones[:, 0:1], start=True, stop=True)
                        mm.then_inc(ss_ps, 1)
                    elif what == "v":
                        if before is not None:
                            wait_for_bank(n, dn, before)
                        pe.wait_ge(w_in, AHEAD + 16 * n + 16)
                        a, z = CH[t]
                        project_chunk(1, pkv[:, BANK["v", t], 0:z - a], a, z).then_inc(v_ps, 1)
                    elif what == "vt":
                        wait_for_bank(n, dn, before)
                        pe.wait_ge(vraw_ok, AHEAD + NC * n + t + 1)
                        for i in chunk_tiles(t):
                            mm = pe.transpose(pkv[:, BANK["vt", t], (i % 4) * P:(i % 4 + 1) * P],
                                              vraw[:, i * P:(i + 1) * P], ident[:])
                        mm.then_inc(vt_ps, 1)

                rounds(pe, prologue, step)

            @block.scalar
            def _(act):
                def prologue(b):
                    for t in range(CT):
                        m = min(P, L - t * P)
                        act.wait_ge(xt_ps, AHEAD + b * CT + t + 1)
                        act.copy(ctxT[:, HI, :, S + t * P:S + t * P + m],
                                 pkv[:, t % 2].rearrange("p (c r) -> p c r", c=KT)[:, :, 0:m]).then_inc(xhi_ok, 1)
                    for what, h, t in AHEAD_OF_FIRST:
                        step(b * KVH, what, h, t)

                def step(n, what, h, t, before=None, dn=0, last=False):
                    u, T = NH * n + h, n * UT + (h * NT + t)
                    m, s = rows(t), h * NT + t
                    if what == "copy":
                        act.wait_ge(qk_ps, AHEAD + T + 1)
                        act.wait_ge(plo_ok, AHEAD + T + 1 - UT)
                        act.wait_ge(sum_ok, AHEAD + sums(n - 1, h, t))
                        if h == 0 and t % 4 == 0:
                            act.wait_ge(rk_ok, AHEAD + rk_signals(n, t // 4))
                        act.activation(sc[0:m, s], pqk[0:m, s % 2], ACT.Copy, scale=rk[0:m, t:t + 1]).then_inc(sc_ok, 1)
                    elif what == "exp":
                        act.wait_ge(sub_ok, AHEAD + T + 1)
                        act.activation(sc[0:m, s], sc[0:m, s], ACT.Exp).then_inc(exp_ok, 1)
                    elif what == "hi":
                        act.wait_ge(exp_ok, AHEAD + T + 1)
                        act.wait_ge(pv_ps, AHEAD + T - NP + 1)
                        act.copy(pr[0:m, HI, s % NP], sc[0:m, s]).then_inc(phi_ok, 1)
                    elif what == "oraw":
                        act.wait_ge(pv_ps, AHEAD + NT * (u + 1))
                        act.wait_ge(on_ok, AHEAD + u)
                        act.copy(oraw[:], ppv[:]).then_inc(oraw_ok, 1)
                    elif what == "khi":
                        a, z = CH[t]
                        act.wait_ge(k_ps, AHEAD + NC * n + t + 1)
                        act.wait_ge(qk_ps, AHEAD + tiles(n - 1, 1, chunk_tiles(t)[-1]))
                        act.copy(kT[:, HI, a:z], pkv[:, BANK["k", t], 0:z - a]).then_inc(khi_ok, 1)
                        act.wait_ge(ss_ps, AHEAD + NC * n + t - 1)
                        act.activation(sq[:, t % 2, 0:z - a], pkv[:, BANK["k", t], 0:z - a], ACT.Square).then_inc(ksq_ok, 1)
                    elif what == "vhi":
                        a, z = CH[t]
                        act.wait_ge(v_ps, AHEAD + NC * n + t + 1)
                        act.wait_ge(vt_ps, AHEAD + NC * (n - 1) + t + 1)
                        act.copy(vraw[:, a:z], pkv[:, BANK["v", t], 0:z - a]).then_inc(vraw_ok, 1)
                    elif what == "vthi":
                        act.wait_ge(vt_ps, AHEAD + NC * n + t + 1)
                        act.wait_ge(pv_ps, AHEAD + tiles(n - 1, 1, chunk_tiles(t)[-1]))
                        w = len(chunk_tiles(t))
                        act.copy(V[:, HI, 4 * t:4 * t + w],
                                 pkv[:, BANK["vt", t], 0:w * P].rearrange("p (a n) -> p a n", n=P)).then_inc(vhi_ok, 1)

                rounds(act, prologue, step)

            @block.vector
            def _(dve):
                def prologue(b):
                    for t in range(CT):
                        m = min(P, L - t * P)
                        dve.wait_ge(xhi_ok, AHEAD + b * CT + t + 1)
                        dve.tensor_tensor(ctxT[:, LO, :, S + t * P:S + t * P + m],
                                          pkv[:, t % 2].rearrange("p (c r) -> p c r", c=KT)[:, :, 0:m],
                                          ctxT[:, HI, :, S + t * P:S + t * P + m].bitcast(F32),
                                          ALU.subtract).then_inc(xlo_ok, 1)
                    for what, h, t in AHEAD_OF_FIRST:
                        step(b * KVH, what, h, t)

                def diagonal(col):
                    return dve.tensor_tensor(diag[:], ident[:].unsqueeze(1).to_broadcast([P, 4, P]),
                                             col[:].unsqueeze(2).to_broadcast([P, 4, P]), ALU.mult)

                def step(n, what, h, t, before=None, dn=0, last=False):
                    u, T = NH * n + h, n * UT + (h * NT + t)
                    m, s = rows(t), h * NT + t
                    if what == "max":
                        dve.wait_ge(sc_ok, AHEAD + T + 1)
                        if t == 1:
                            dve.wait_ge(mt_ps, AHEAD + u - 1)
                            dve.tensor_tensor(mx[:, h], sc[:, s - 1], sc[:, s], ALU.max).then_inc(max_ok, 1)
                        else:
                            dve.wait_ge(max_ok, AHEAD + (NT - 1) * u + t - 1)
                            dve.tensor_tensor(mx[0:m, h], mx[0:m, h], sc[0:m, s], ALU.max).then_inc(max_ok, 1)
                    elif what == "red":
                        dve.wait_ge(mt_ps, AHEAD + u + 1)
                        dve.tensor_reduce(red[:], pred[:].rearrange("p (c n) -> p c n", c=4), AX.X, ALU.max).then_inc(red_ok, 1)
                        dve.wait_ge(red_ok, AHEAD + u + 1)
                        dve.wait_ge(db_ps, AHEAD + u - 1)
                        diagonal(red).then_inc(diag_ok, 1)
                    elif what == "sub":
                        if t == 0:
                            dve.wait_ge(mb_ps, AHEAD + u + 1)
                        dve.tensor_tensor(sc[0:m, s], sc[0:m, s], pmax[0:m], ALU.subtract).then_inc(sub_ok, 1)
                    elif what == "lo":
                        dve.wait_ge(phi_ok, AHEAD + T + 1)
                        dve.tensor_tensor(pr[0:m, LO, s % NP], sc[0:m, s], pr[0:m, HI, s % NP].bitcast(F32),
                                          ALU.subtract).then_inc(plo_ok, 1)
                    elif what == "dred":
                        dve.wait_ge(dt_ps, AHEAD + u + 1)
                        dve.tensor_reduce(den[:], pred[:].rearrange("p (c n) -> p c n", c=4), AX.X, ALU.add).then_inc(den_ok, 1)
                        dve.wait_ge(den_ok, AHEAD + u + 1)
                        dve.reciprocal(rden[:], den[:]).then_inc(rden_ok, 1)
                        dve.wait_ge(rden_ok, AHEAD + u + 1)
                        if last and h == 1:
                            dve.wait_ge(db_ps, AHEAD + u)
                        else:
                            dve.wait_ge(mb_ps, AHEAD + u + 2)
                        diagonal(rden).then_inc(ddiag_ok, 1)
                    elif what == "on":
                        dve.wait_ge(db_ps, AHEAD + u + 1)
                        dve.wait_ge(oraw_ok, AHEAD + u + 1)
                        dve.wait_ge(o_out, AHEAD + 16 * u)
                        dve.tensor_tensor(on[:], oraw[:], pred[:], ALU.mult).then_inc(on_ok, 1)
                    elif what == "klo":
                        a, z = CH[t]
                        dve.wait_ge(ksq_ok, AHEAD + NC * n + t + 1)
                        dve.tensor_tensor(kT[:, LO, a:z], pkv[:, BANK["k", t], 0:z - a], kT[:, HI, a:z].bitcast(F32),
                                          ALU.subtract).then_inc(klo_ok, 1)
                    elif what == "var":
                        dve.wait_ge(ss_ps, AHEAD + NC * n + t + 1)
                        dve.wait_ge(rk_ok, AHEAD + rk_signals(n - 1, t))
                        i, z = chunk_tiles(t)[0], min(chunk_tiles(t)[-1] + 1, NT - 1)
                        dve.tensor_scalar(var[:, i:z], pss[:, i:z], 1.0 / DH, EPS_RMS, ALU.mult, ALU.add).then_inc(var_ok, 1)
                        if t == NC - 1:
                            dve.tensor_scalar(var[0:LAST, NT - 1:NT], pss[0:LAST, NT - 1:NT], 1.0 / DH, EPS_RMS,
                                              ALU.mult, ALU.add).then_inc(var_ok, 1)
                    elif what == "vtlo":
                        w = len(chunk_tiles(t))
                        dve.wait_ge(vhi_ok, AHEAD + NC * n + t + 1)
                        dve.tensor_tensor(V[:, LO, 4 * t:4 * t + w],
                                          pkv[:, BANK["vt", t], 0:w * P].rearrange("p (a n) -> p a n", n=P),
                                          V[:, HI, 4 * t:4 * t + w].bitcast(F32), ALU.subtract).then_inc(vlo_ok, 1)

                rounds(dve, prologue, step)

            @block.gpsimd
            def _(pool):
                def prologue(b):
                    for what, h, t in AHEAD_OF_FIRST:
                        step(b * KVH, what, h, t)

                def step(n, what, h, t, before=None, dn=0, last=False):
                    u, T = NH * n + h, n * UT + (h * NT + t)
                    m, s = rows(t), h * NT + t
                    if what == "sum":
                        pool.wait_ge(exp_ok, AHEAD + T + 1)
                        if t == 1:
                            pool.wait_ge(dt_ps, AHEAD + u - 1)
                            pool.tensor_tensor(sm[:, h], sc[:, s - 1], sc[:, s], ALU.add).then_inc(sum_ok, 1)
                        else:
                            pool.wait_ge(sum_ok, AHEAD + (NT - 1) * u + t - 1)
                            pool.tensor_tensor(sm[0:m, h], sm[0:m, h], sc[0:m, s], ALU.add).then_inc(sum_ok, 1)
                    elif what == "pow":
                        i, z = chunk_tiles(t)[0], min(chunk_tiles(t)[-1] + 1, NT - 1)
                        pool.wait_ge(var_ok, AHEAD + rk_signals(n, t))
                        pool.wait_ge(sc_ok, AHEAD + tiles(n - 1, 1, chunk_tiles(t)[-1]))
                        pool.tensor_tensor(rk[:, i:z], var[:, i:z], mhalf[:, 0:z - i], ALU.pow).then_inc(rk_ok, 1)
                        if t == NC - 1:
                            pool.tensor_tensor(rk[0:LAST, NT - 1:NT], var[0:LAST, NT - 1:NT], mhalf[0:LAST, 0:1],
                                               ALU.pow).then_inc(rk_ok, 1)

                rounds(pool, prologue, step)


def gate_column(sp, act, g, gcol, g_in, g_ok):
    if sp is not None:
        sp.dma_start(gcol[:, 0:1], g.partition_broadcast(P)).then_inc(g_in, 16)
    if act is not None:
        act.wait_ge(g_in, 16)
        act.activation(gcol[:, 1:2], gcol[:, 0:1], ACT.Tanh).then_inc(g_ok, 1)


def project(nc, d, scr, x, Wo, g_xattn):
    B, S, D, DH, HEADS, KVH, G, QT = (d[k] for k in ("B", "S", "D", "DH", "HEADS", "KVH", "G", "QT"))
    BT = S // P
    WC = 4
    HC = 8
    NE = HEADS // HC
    NV = NE * BT
    SL = 4
    with ExitStack() as ctx:
        sb, ps, sem = tools(nc, ctx, "out")
        wo = sb("wo", [P, 2, HEADS, D], F32R)
        wraw = sb("wraw", [P, 2, WC, D])
        oraw = sb("oraw", [P, SL, HC, P])
        o = sb("o", [P, SL, 2, HC, P], F32R)
        xin = sb("xin", [P, BT, D])
        x2 = sb("x2", [P, BT, D])
        gcol = sb("gcol", [P, 2])
        po = ps("po", [P, BT, 512])
        g_in, g_ok = sem("g_in"), sem("g_ok")
        w_in = [sem("w_in0"), sem("w_in1")]
        o_in = [sem(f"o_in{i}") for i in range(SL)]
        x_in, x2_out = [sem("x_in0"), sem("x_in1")], [sem("x2_out0"), sem("x2_out1")]
        whi_ok, wlo_ok, ohi_ok, olo_ok, o_ps, x2_ok = (
            sem(n) for n in ("whi_ok", "wlo_ok", "ohi_ok", "olo_ok", "o_ps", "x2_ok"))

        wo_v = Wo.rearrange("(h p) n -> p h n", p=P)
        x_v = x.rearrange("b (t p) n -> b t p n", p=P)

        with nc.Block() as block:

            @block.gpsimd
            def _(pool):
                start_ahead(pool, o_in + x_in + x2_out + [ohi_ok, olo_ok, o_ps, x2_ok])

        with nc.Block() as block:

            def batches(eng, batch):
                batch(0, True)
                with eng.Fori(1, B) as b:
                    batch(b, False)

            @block.sync
            def _(sp):
                gate_column(sp, None, g_xattn, gcol, g_in, g_ok)

                steps = [(2 * v - 6, "load", v // BT, v % BT) for v in range(NV)]
                steps += [(-1.5, "x", 0, t) for t in range(BT)] + [(2 * NV + 1 + t, "store", 0, t) for t in range(BT)]

                def step(b, what, e, t):
                    v = e * BT + t
                    if what == "load":
                        sp.wait_ge(olo_ok, AHEAD + b * NV + (v + 1) - SL)
                        for k in range(HC // G):
                            sp.dma_start(oraw[:, v % SL, k * G:(k + 1) * G],
                                         scr["o"][bass.ds(b * KVH + (e * (HC // G) + k), 1), :, :, t * P:(t + 1) * P]
                                         .rearrange("o p g s -> (o p) g s")).then_inc(o_in[v % SL], 16)
                    elif what == "x":
                        sp.wait_ge(x2_ok, AHEAD + b * BT + t - 1)
                        sp.dma_start(xin[:, t], x_v[bass.ds(b, 1), t].rearrange("o p n -> (o p) n")).then_inc(x_in[t], 16)
                    elif what == "store":
                        sp.wait_ge(x2_ok, AHEAD + b * BT + t + 1)
                        sp.dma_start(scr["x2"][bass.ds((b * BT + t) * P, P)], x2[:, t]).then_inc(x2_out[t], 16)
                pipeline(sp, B, 2 * NV, steps, step)
                for t in range(BT):
                    sp.wait_ge(x2_out[t], AHEAD + 16 * B)

            @block.gpsimd
            def _(pool):
                for i in range(HEADS // WC):
                    if i >= 2:
                        pool.wait_ge(wlo_ok, i - 1)
                    pool.dma_start(wraw[:, i % 2], wo_v[:, WC * i:WC * i + WC]).then_inc(w_in[i % 2], 16)

            @block.scalar
            def _(act):
                gate_column(None, act, g_xattn, gcol, g_in, g_ok)

                def batch(b, first):
                    for e in range(NE):
                        for t in range(BT):
                            v = e * BT + t
                            act.wait_ge(o_in[v % SL], AHEAD + (b * (NV // SL) + v // SL + 1) * (16 * HC // G))
                            act.wait_ge(o_ps, AHEAD + b * NV + (v + 1) - SL)
                            act.copy(o[:, v % SL, HI], oraw[:, v % SL]).then_inc(ohi_ok, 1)
                            if first:
                                act.wait_ge(w_in[v % 2], 16 * (v // 2) + 16)
                                act.copy(wo[:, HI, WC * v:WC * v + WC], wraw[:, v % 2]).then_inc(whi_ok, 1)
                batches(act, batch)

            @block.vector
            def _(dve):
                def batch(b, first):
                    for e in range(NE):
                        for t in range(BT):
                            v = e * BT + t
                            dve.wait_ge(ohi_ok, AHEAD + b * NV + v + 1)
                            dve.tensor_tensor(o[:, v % SL, LO], oraw[:, v % SL], o[:, v % SL, HI].bitcast(F32),
                                              ALU.subtract).then_inc(olo_ok, 1)
                            if first:
                                dve.wait_ge(whi_ok, v + 1)
                                dve.tensor_tensor(wo[:, LO, WC * v:WC * v + WC], wraw[:, v % 2],
                                                  wo[:, HI, WC * v:WC * v + WC].bitcast(F32), ALU.subtract).then_inc(wlo_ok, 1)
                    for t in range(BT):
                        dve.wait_ge(o_ps, AHEAD + b * NV + NV - BT + t + 1)
                        dve.wait_ge(x_in[t], AHEAD + 16 * b + 16)
                        dve.wait_ge(x2_out[t], AHEAD + 16 * b)
                        dve.scalar_tensor_tensor(out=x2[:, t], in0=po[:, t], scalar=gcol[:, 1:2], in1=xin[:, t],
                                                 op0=ALU.mult, op1=ALU.add).then_inc(x2_ok, 1)
                dve.wait_ge(g_ok, 1)
                batches(dve, batch)

            @block.tensor
            def _(pe):
                with pe.Fori(0, B) as b:
                    for e in range(NE):
                        for t in range(BT):
                            v = e * BT + t
                            if e == 0:
                                pe.wait_ge(x2_ok, AHEAD + b * BT + t - 1)
                            pe.wait_ge(olo_ok, AHEAD + b * NV + v + 1)
                            for h in range(HC):
                                if h % WC == 0:
                                    pe.wait_ge(wlo_ok, (e * HC + h) // WC + 1)
                                for p, (op, wp) in enumerate(((HI, HI), (LO, HI), (HI, LO))):
                                    mm = pe.matmul(po[:, t], o[:, v % SL, op, h], wo[:, wp, e * HC + h],
                                                   start=(e == 0 and h == 0 and p == 0),
                                                   stop=(e == NE - 1 and h == HC - 1 and p == 2))
                            mm.then_inc(o_ps, 1)


def ffn(nc, d, scr, g_ffn, c1_w, c2_w, w1, w2t, out):
    S, D, KT, QT = (d[k] for k in ("S", "D", "KT", "QT"))
    RANK = c1_w.shape[0]
    INTER = w1.shape[0]
    IT = INTER // P
    BLK = 32
    CW = 448
    NCH = INTER // CW
    NB = CW // BLK
    NS = 4
    NW = 2 * IT
    HB = (0, 1, 0, 1)
    GT = [(g, min(g + 4, IT)) for g in range(0, IT, 4)]
    assert NCH * CW == INTER and IT * P == INTER
    with ExitStack() as ctx:
        sb, ps, sem = tools(nc, ctx, "ffn")
        ident = sb("ident", [P, P])
        mhalf = sb("mhalf", [P, QT])
        rank = sb("rank", [P, NB, BLK])
        gcol = sb("gcol", [P, 2])
        stage = sb("stage", [P, NS, D])
        c1 = sb("c1", [RANK, D])
        c2 = sb("c2", [P, IT, RANK])
        c1T = sb("c1T", [P, KT, RANK])
        c2T = sb("c2T", [RANK, INTER])
        w1T = sb("w1T", [P, 2, KT, INTER], F32R)
        w2 = sb("w2", [P, 2, IT, D], F32R)
        xall = sb("xall", [P, QT, D])
        xin = sb("xin", [P, 2, D])
        stats = sb("stats", [P, QT, 6])
        mv = sb("mv", [P, QT, 2])
        veps = sb("veps", [P, QT])
        rstd = sb("rstd", [P, QT])
        xn = sb("xn", [P, 2, D])
        xT = sb("xT", [P, 2, 2, KT, P], F32R)
        xTf = sb("xTf", [P, KT, P])
        tT = sb("tT", [RANK, P])
        bm = sb("bm", [P, NB])
        bs = sb("bs", [P, NB])
        eq = sb("eq", [P, NB, BLK])
        score = sb("score", [P, NB, BLK])
        mask = sb("mask", [P, NCH, NB, BLK])
        hm = sb("hm", [P, INTER])
        hT = sb("hT", [P, 2, IT, P], F32R)
        ptr = ps("ptr", [P, 2, 512])
        pt = ps("pt", [P, 512])
        pin = ps("pin", [P, 2, 512])
        ph = ps("ph", [P, 2, 512])
        py = ps("py", [P, 512])
        g_in, g_ok, id_ok, cst_ok, c_in, c_ps, c_ok = (
            sem(n) for n in ("g_in", "g_ok", "id_ok", "cst_ok", "c_in", "c_ps", "c_ok"))
        s_in = [sem(f"s_in{i}") for i in range(NS)]
        w_ps, whi_ok, wlo_ok = sem("w_ps"), sem("whi_ok"), sem("wlo_ok")
        l_in, l_out = [sem(f"l_in{t}") for t in range(QT // 2)], sem("l_out")
        bn, var_ok, ve_ok, rstd_ok, ln_ok = (sem(n) for n in ("bn", "var_ok", "ve_ok", "rstd_ok", "ln_ok"))
        x_in, y_out = [sem("x_in0"), sem("x_in1")], [sem("y_out0"), sem("y_out1")]
        n_in = [sem("n_in0"), sem("n_in1")]
        names = ("xt_ps xhi_ok xf_ok xlo_ok t_ps t_ok in_ps bm_ok eq_ok score_ok bs_ok "
                 "mask_ok h_ps hm_ok ht_ps hhi_ok hlo_ok y_ps y_ok").split()
        loop_sems = [sem(n) for n in names]
        (xt_ps, xhi_ok, xf_ok, xlo_ok, t_ps, t_ok, in_ps, bm_ok, eq_ok, score_ok, bs_ok,
         mask_ok, h_ps, hm_ok, ht_ps, hhi_ok, hlo_ok, y_ps, y_ok) = loop_sems

        w1_t = w1.rearrange("(t p) n -> t p n", p=P)
        w2_t = w2t.rearrange("(t p) n -> t p n", p=P)
        out_v = out.rearrange("b s n -> (b s) n")

        def w_bank(i):
            return (ptr[:, 0], ptr[:, 1], py[:])[i % 3]

        def load_weights(eng, i):
            eng.dma_start(stage[:, i % NS], w1_t[i] if i < IT else w2_t[i - IT]).then_inc(s_in[i % NS], 16)

        with nc.Block() as block:

            @block.sync
            def _(sp):
                gate_column(sp, None, g_ffn, gcol, g_in, g_ok)
                sp.dma_start(c1[:], c1_w).then_inc(c_in, 16)
                sp.dma_start(c2[:], c2_w.rearrange("(t p) r -> p t r", p=P)).then_inc(c_in, 16)
                for t in range(QT // 2):
                    sp.dma_start(xall[:, 2 * t:2 * t + 2],
                                 scr["x2"][2 * t * P:(2 * t + 2) * P].rearrange("(t p) n -> p t n", p=P)).then_inc(l_in[t], 16)
                for t in range(QT):
                    sp.wait_ge(ln_ok, t + 1)
                    sp.dma_start(scr["xn"][t * P:(t + 1) * P], xall[:, t]).then_inc(l_out, 16)
                sp.wait_ge(l_out, 16 * QT)

            @block.gpsimd
            def _(pool):
                start_ahead(pool, loop_sems + x_in + n_in + y_out)
                identity(pool, ident, id_ok)
                pool.memset(mhalf[:], -0.5).then_inc(cst_ok, 1)
                pool.wait_ge(cst_ok, 1)
                pool.wait_ge(ve_ok, QT)
                pool.tensor_tensor(rstd[:], veps[:], mhalf[:], ALU.pow).then_inc(rstd_ok, 1)
                for i in range(BLK):
                    pool.memset(rank[:, :, i:i + 1], float(BLK - i)).then_inc(cst_ok, 1)

            @block.scalar
            def _(act):
                for i in range(NS):
                    load_weights(act, i)
                gate_column(None, act, g_ffn, gcol, g_in, g_ok)
                for i in range(IT):
                    act.wait_ge(w_ps, i + 1)
                    load_weights(act, i + NS)
                    act.copy(w1T[:, HI, :, i * P:(i + 1) * P],
                             w_bank(i).rearrange("p (c r) -> p c r", c=KT)).then_inc(whi_ok, 1)

            @block.tensor
            def _(pe):
                pe.wait_ge(id_ok, 2)
                pe.wait_ge(c_in, 32)
                for c in range(KT):
                    mm = pe.transpose(pt[:, c * RANK:(c + 1) * RANK], c1[:, c * P:(c + 1) * P], ident[0:RANK, 0:RANK])
                mm.then_inc(c_ps, 1)
                for g, (a, z) in enumerate(GT):
                    bank = (pin[:, 0], pin[:, 1], ph[:, 0], ph[:, 1])[g]
                    for t in range(a, z):
                        mm = pe.transpose(bank[0:RANK, (t - a) * P:(t - a + 1) * P], c2[:, t], ident[:])
                    mm.then_inc(c_ps, 1)
                for i in range(IT):
                    pe.wait_ge(s_in[i % NS], 16 * (i // NS) + 16)
                    if i >= 3:
                        pe.wait_ge(wlo_ok, i - 2)
                    for c in range(KT):
                        mm = pe.transpose(w_bank(i)[:, c * P:(c + 1) * P], stage[:, i % NS, c * P:(c + 1) * P], ident[:])
                    mm.then_inc(w_ps, 1)

            @block.vector
            def _(dve):
                for t in range(QT):
                    dve.wait_ge(l_in[t // 2], 16)
                    dve.bn_stats(stats[:, t], xall[:, t]).then_inc(bn, 1)
                for t in range(QT):
                    dve.wait_ge(bn, t + 1)
                    dve.bn_aggr(mv[:, t], stats[:, t]).then_inc(var_ok, 1)
                for t in range(QT):
                    dve.wait_ge(var_ok, t + 1)
                    dve.tensor_scalar(veps[:, t:t + 1], mv[:, t, 1:2], EPS_LN, None, ALU.add).then_inc(ve_ok, 1)
                dve.wait_ge(c_ps, 1)
                dve.tensor_copy(c1T[:].rearrange("p c r -> p (c r)"), pt[:, 0:KT * RANK]).then_inc(c_ok, 1)
                for g, (a, z) in enumerate(GT):
                    bank = (pin[:, 0], pin[:, 1], ph[:, 0], ph[:, 1])[g]
                    dve.wait_ge(c_ps, g + 2)
                    dve.tensor_copy(c2T[:, a * P:z * P], bank[0:RANK, 0:(z - a) * P]).then_inc(c_ok, 1)
                dve.wait_ge(rstd_ok, 1)
                for t in range(QT):
                    dve.tensor_scalar(xall[:, t], xall[:, t], mv[:, t, 0:1], rstd[:, t:t + 1],
                                      ALU.subtract, ALU.mult).then_inc(ln_ok, 1)
                for i in range(IT):
                    dve.wait_ge(whi_ok, i + 1)
                    dve.tensor_tensor(w1T[:, LO, :, i * P:(i + 1) * P], w_bank(i).rearrange("p (c r) -> p c r", c=KT),
                                      w1T[:, HI, :, i * P:(i + 1) * P].bitcast(F32), ALU.subtract).then_inc(wlo_ok, 1)

        T = 27
        tile_steps = [(-57, "load"), (-20, "xload"), (26.5, "store"),
                      (-26.7, "xt"), (-21.9, "c1"), (-19.3, "inner", 0), (-14, "inner", 1), (-10, "inner", 2), (-7, "inner", 3),
                      (-26.5, "xcopy"), (-24.2, "xlo"), (-21.8, "tcopy"),
                      (-15.8, "mask", 0), (-12, "mask", 1), (-8.9, "mask", 2), (-5, "mask", 3),
                      (0.2, "h", 0), (2.7, "h", 1), (5.2, "h", 2), (7.8, "h", 3),
                      (2.6, "hm", 0), (5.1, "hm", 1), (7.7, "hm", 2), (10.2, "hm", 3),
                      (7.75, "ht", 0), (10.5, "ht", 1), (14.0, "ht", 2), (16.9, "ht", 3),
                      (9.0, "hsplit", 0), (11.0, "hsplit", 1), (14.9, "hsplit", 2), (17.9, "hsplit", 3),
                      (11.1, "out", 0), (14.2, "out", 1), (17.2, "out", 2), (20.2, "out", 3), (26, "y")]
        first_steps = [(3.0 + t, "w2", 0, t) for t in range(IT)]
        steps = sorted((p + j * T, what[0], j, *(what[1:] or (0,))) for j in range(2) for p, *what in tile_steps)

        with nc.Block() as block:

            @block.sync
            def _(sp):
                def step(r, what, j, c):
                    i = 2 * r + j
                    if what == "w2":
                        if c + NS < IT:
                            sp.wait_ge(wlo_ok, IT + c + 1)
                            load_weights(sp, IT + c + NS)
                    elif what == "load":
                        sp.wait_ge(xt_ps, AHEAD + i - 1)
                        sp.dma_start(xn[:, j], scr["xn"][bass.ds(i * P, P)]).then_inc(n_in[j], 16)
                    elif what == "xload":
                        sp.wait_ge(y_out[j], AHEAD + 16 * r)
                        sp.dma_start(xin[:, j], scr["x2"][bass.ds(i * P, P)]).then_inc(x_in[j], 16)
                    elif what == "store":
                        sp.wait_ge(y_ok, AHEAD + i + 1)
                        sp.dma_start(out_v[bass.ds(i * P, P)], xin[:, j]).then_inc(y_out[j], 16)
                pipeline(sp, QT // 2, 2 * T, steps, step, first_steps)
                for j in range(2):
                    sp.wait_ge(y_out[j], AHEAD + 16 * (QT // 2))

            @block.scalar
            def _(act):
                def step(r, what, j, c):
                    i = 2 * r + j
                    if what == "w2":
                        k = IT + c
                        act.wait_ge(s_in[k % NS], 16 * (k // NS) + 16)
                        act.copy(w2[:, HI, c], stage[:, k % NS]).then_inc(whi_ok, 1)
                    elif what == "xcopy":
                        act.wait_ge(xt_ps, AHEAD + i + 1)
                        act.wait_ge(h_ps, AHEAD + (i - 1) * NCH)
                        act.copy(xT[:, j, HI].rearrange("p c r -> p (c r)"), pt[:]).then_inc(xhi_ok, 1)
                        act.wait_ge(t_ps, AHEAD + i)
                        act.copy(xTf[:].rearrange("p c r -> p (c r)"), pt[:]).then_inc(xf_ok, 1)
                    elif what == "tcopy":
                        act.wait_ge(t_ps, AHEAD + i + 1)
                        act.wait_ge(in_ps, AHEAD + i * NCH)
                        act.copy(tT[:], pin[0:RANK, 1, 0:P]).then_inc(t_ok, 1)
                    elif what == "hsplit":
                        a, z = GT[c]
                        act.wait_ge(ht_ps, AHEAD + i * len(GT) + c + 1)
                        act.wait_ge(y_ps, AHEAD + i)
                        act.copy(hT[:, HI, a:z].rearrange("p c r -> p (c r)"),
                                 ptr[:, HB[c], 0:(z - a) * P]).then_inc(hhi_ok, 1)
                pipeline(act, QT // 2, 2 * T, steps, step, first_steps)

            @block.tensor
            def _(pe):
                def step(r, what, j, c):
                    i = 2 * r + j
                    if what == "xt":
                        pe.wait_ge(n_in[j], AHEAD + 16 * r + 16)
                        pe.wait_ge(xlo_ok, AHEAD + i)
                        for k in range(KT):
                            mm = pe.transpose(pt[:, k * P:(k + 1) * P], xn[:, j, k * P:(k + 1) * P], ident[:])
                        mm.then_inc(xt_ps, 1)
                    elif what == "c1":
                        pe.wait_ge(xf_ok, AHEAD + i + 1)
                        pe.wait_ge(eq_ok, AHEAD + i * NCH)
                        for k in range(KT):
                            mm = pe.matmul(pin[0:RANK, 1, 0:P], c1T[:, k], xTf[:, k], start=(k == 0), stop=(k == KT - 1))
                        mm.then_inc(t_ps, 1)
                    elif what == "inner":
                        pe.wait_ge(t_ok, AHEAD + i + 1)
                        pe.wait_ge(eq_ok, AHEAD + i * NCH + c - 1)
                        pe.matmul(pin[:, c % 2, 0:CW], tT[:], c2T[:, c * CW:(c + 1) * CW],
                                  start=True, stop=True).then_inc(in_ps, 1)
                    elif what == "h":
                        pe.wait_ge(xlo_ok, AHEAD + i + 1)
                        pe.wait_ge(hm_ok, AHEAD + i * NCH + c - 1)
                        for t in range(KT):
                            for p, (xp, wp) in enumerate(((HI, HI), (LO, HI), (HI, LO))):
                                mm = pe.matmul(ph[:, c % 2, 0:CW], xT[:, j, xp, t], w1T[:, wp, t, c * CW:(c + 1) * CW],
                                               start=(t == 0 and p == 0), stop=(t == KT - 1 and p == 2))
                        mm.then_inc(h_ps, 1)
                    elif what == "ht":
                        a, z = GT[c]
                        pe.wait_ge(hm_ok, AHEAD + i * NCH + (z * P + CW - 1) // CW)
                        pe.wait_ge(hlo_ok, AHEAD + i * len(GT) + c - 1)
                        for t in range(a, z):
                            mm = pe.transpose(ptr[:, HB[c], (t - a) * P:(t - a + 1) * P], hm[:, t * P:(t + 1) * P], ident[:])
                        mm.then_inc(ht_ps, 1)
                    elif what == "out":
                        a, z = GT[c]
                        pe.wait_ge(hlo_ok, AHEAD + i * len(GT) + c + 1)
                        pe.wait_ge(wlo_ok, IT + z)
                        if c == 0:
                            pe.wait_ge(y_ok, AHEAD + i)
                        for t in range(a, z):
                            for p, (hp, wp) in enumerate(((HI, HI), (LO, HI), (HI, LO))):
                                mm = pe.matmul(py[:], hT[:, hp, t], w2[:, wp, t],
                                               start=(t == 0 and p == 0), stop=(t == IT - 1 and p == 2))
                        if c == len(GT) - 1:
                            mm.then_inc(y_ps, 1)
                pipeline(pe, QT // 2, 2 * T, steps, step)

            @block.vector
            def _(dve):
                def blocks(a):
                    return a.rearrange("p (n b) -> p n b", b=BLK)

                def step(r, what, j, c):
                    i = 2 * r + j
                    u = i * NCH + c
                    if what == "w2":
                        k = IT + c
                        dve.wait_ge(whi_ok, k + 1)
                        dve.tensor_tensor(w2[:, LO, c], stage[:, k % NS], w2[:, HI, c].bitcast(F32),
                                          ALU.subtract).then_inc(wlo_ok, 1)
                    elif what == "xlo":
                        dve.wait_ge(xf_ok, AHEAD + i + 1)
                        dve.tensor_tensor(xT[:, j, LO].rearrange("p c r -> p (c r)"), pt[:],
                                          xT[:, j, HI].bitcast(F32).rearrange("p c r -> p (c r)"), ALU.subtract).then_inc(xlo_ok, 1)
                    elif what == "mask":
                        dve.wait_ge(in_ps, AHEAD + u + 1)
                        inner = blocks(pin[:, c % 2, 0:CW])
                        dve.tensor_reduce(bm[:], inner, AX.X, ALU.max).then_inc(bm_ok, 1)
                        dve.wait_ge(bm_ok, AHEAD + u + 1)
                        dve.tensor_tensor(eq[:], inner, bm[:].unsqueeze(2).to_broadcast([P, NB, BLK]),
                                          ALU.is_equal).then_inc(eq_ok, 1)
                        dve.wait_ge(eq_ok, AHEAD + u + 1)
                        dve.tensor_tensor(score[:], eq[:], rank[:], ALU.mult).then_inc(score_ok, 1)
                        dve.wait_ge(score_ok, AHEAD + u + 1)
                        dve.tensor_reduce(bs[:], score[:], AX.X, ALU.max).then_inc(bs_ok, 1)
                        dve.wait_ge(bs_ok, AHEAD + u + 1)
                        dve.wait_ge(hm_ok, AHEAD + u + 1 - NCH)
                        dve.tensor_tensor(mask[:, c], score[:], bs[:].unsqueeze(2).to_broadcast([P, NB, BLK]),
                                          ALU.is_equal).then_inc(mask_ok, 1)
                    elif what == "hm":
                        dve.wait_ge(mask_ok, AHEAD + u + 1)
                        dve.wait_ge(h_ps, AHEAD + u + 1)
                        dve.wait_ge(ht_ps, AHEAD + i * len(GT))
                        dve.scalar_tensor_tensor(out=hm[:, c * CW:(c + 1) * CW], in0=ph[:, c % 2, 0:CW], scalar=0.0,
                                                 in1=mask[:, c].rearrange("p n b -> p (n b)"),
                                                 op0=ALU.max, op1=ALU.mult).then_inc(hm_ok, 1)
                    elif what == "hsplit":
                        a, z = GT[c]
                        dve.wait_ge(hhi_ok, AHEAD + i * len(GT) + c + 1)
                        dve.tensor_tensor(hT[:, LO, a:z].rearrange("p c r -> p (c r)"), ptr[:, HB[c], 0:(z - a) * P],
                                          hT[:, HI, a:z].bitcast(F32).rearrange("p c r -> p (c r)"),
                                          ALU.subtract).then_inc(hlo_ok, 1)
                    elif what == "y":
                        dve.wait_ge(y_ps, AHEAD + i + 1)
                        dve.wait_ge(x_in[j], AHEAD + 16 * r + 16)
                        dve.scalar_tensor_tensor(out=xin[:, j], in0=py[:], scalar=gcol[:, 1:2], in1=xin[:, j],
                                                 op0=ALU.mult, op1=ALU.add).then_inc(y_ok, 1)
                pipeline(dve, QT // 2, 2 * T, steps, step, first_steps)


_INS = ["x", "ctx_4096", "g_xattn", "g_ffn", "L0_xattn_Wq", "L0_xattn_Wk", "L0_xattn_Wv", "L0_xattn_Wo",
        "L0_xattn_q_norm_w", "L0_xattn_k_norm_w", "L0_ffn_c1_w", "L0_ffn_c2_w", "L0_ffn_w1", "L0_ffn_w2t"]


def kernel(**inputs):
    import numpy as np
    import concourse.bacc as bacc
    from concourse.bass_utils import run_bass_kernel_spmd

    nc = bacc.Bacc("TRN2", target_bir_lowering=False, num_devices=1)
    arrays, args = {}, []
    for name in _INS:
        a = np.ascontiguousarray(inputs[name])
        arrays[f"in_{name}"] = a
        args.append(nc.dram_tensor(f"in_{name}", a.shape, mybir.dt.from_np(a.dtype), kind="ExternalInput").ap())
    out = nc.dram_tensor("out_x", inputs["x"].shape, F32, kind="ExternalOutput").ap()
    program(nc, *args, out)
    r = run_bass_kernel_spmd(nc, [arrays], core_ids=[0])
    return r.results[0]["out_x"]
```

```python
from contextlib import ExitStack

import concourse.bass as bass
from concourse import mybir

F32 = mybir.dt.float32
F32R = mybir.dt.float32r
ALU = mybir.AluOpType
ACT = mybir.ActivationFunctionType
AX = mybir.AxisListType

P = 128
AHEAD = 32
HI, LO = 0, 1
EPS_LN = 1e-5
EPS_RMS = 1e-6


def passes(w, m):
    return ((w[HI], m[HI]), (w[LO], m[HI]), (w[HI], m[LO]))


def program(nc, x, ctx_4096, g_xattn, g_ffn, Wq, Wk, Wv, Wo, q_norm_w, k_norm_w, c1_w, c2_w, w1, w2t, out):
    B, S, D = x.shape
    L = ctx_4096.shape[1]
    DH = q_norm_w.shape[0]
    HEADS = Wq.shape[1] // DH
    KVH = Wk.shape[1] // DH
    G = HEADS // KVH
    KT = D // P
    QT = B * S // P
    dims = dict(B=B, S=S, D=D, L=L, DH=DH, HEADS=HEADS, KVH=KVH, G=G, KT=KT, QT=QT)

    scratch = dict(
        lat=nc.dram_tensor("lat_scr", [B, P, 2, KT, S], F32, kind="Internal").ap(),
        q=nc.dram_tensor("q_scr", [B * KVH, P, 2, G, S], F32, kind="Internal").ap(),
        kv=nc.dram_tensor("kv_scr", [KVH, P, 2, 2, KT, DH], F32, kind="Internal").ap(),
        o=nc.dram_tensor("o_scr", [B * KVH, P, G, S], F32, kind="Internal").ap(),
        x2=nc.dram_tensor("x2_scr", [QT * P, D], F32, kind="Internal").ap(),
        xn=nc.dram_tensor("xn_scr", [QT * P, D], F32, kind="Internal").ap(),
    )
    prepare(nc, dims, scratch, x, Wq, Wk, Wv, q_norm_w, k_norm_w)
    attend(nc, dims, scratch, ctx_4096)
    project(nc, dims, scratch, x, Wo, g_xattn)
    ffn(nc, dims, scratch, g_ffn, c1_w, c2_w, w1, w2t, out)


def tools(nc, ctx, tag):
    def sb(name, shape, dt=F32):
        return ctx.enter_context(nc.sbuf_tensor(f"{tag}_{name}", shape, dt))

    def ps(name, shape):
        return ctx.enter_context(nc.psum_tensor(f"{tag}_{name}", shape, F32))

    def sem(name):
        return ctx.enter_context(nc.semaphore(f"{tag}_{name}"))
    return sb, ps, sem


def start_ahead(pool, sems):
    for s in sems:
        pool.sem_inc(s, AHEAD)


def pipeline(eng, units, width, steps, emit, first=()):
    def window(w):
        found = [(place % width, place // width, what) for place, *what in steps if 0 <= w - place // width < units]
        found += [(place % width, place // width, what) for place, *what in first if w == place // width]
        return [(int(late), what) for _, late, what in sorted(found, key=lambda f: f[0])]

    w, end = int(min(p // width for p, *_ in steps)), units + int(max(p // width for p, *_ in steps))
    while w < end:
        todo, z = window(w), w + 1
        while z < end and window(z) == todo:
            z += 1
        last = max(late for late, _ in todo)
        if z - w > 1:
            with eng.Fori(w - last, z - last) as n:
                for late, what in todo:
                    emit(n + (last - late), *what)
        else:
            for late, what in todo:
                emit(w - late, *what)
        w = z


def identity(pool, ident, sem):
    pool.memset(ident[:], 0.0).then_inc(sem, 1)
    pool.wait_ge(sem, 1)
    pool.affine_select(out=ident[:], in_=ident[:], compare_op=ALU.not_equal, fill=1.0, base=0,
                       pattern=[[-1, P]], channel_multiplier=1).then_inc(sem, 1)



def prepare(nc, d, scr, x, Wq, Wk, Wv, q_norm_w, k_norm_w):
    B, S, D, DH, KVH, G, KT, QT = (d[k] for k in ("B", "S", "D", "DH", "KVH", "G", "KT", "QT"))
    N = G * DH
    SCALE = float(DH) ** -0.5
    BT = S // P
    NJ = 2
    UT = NJ * QT
    with ExitStack() as ctx:
        sb, ps, sem = tools(nc, ctx, "pre")
        ident = sb("ident", [P, P])
        mhalf = sb("mhalf", [P, QT])
        wcol = sb("wcol", [P, 4])
        xin = sb("xin", [P, QT, D])
        stats = sb("stats", [P, QT, 6])
        mv = sb("mv", [P, QT, 2])
        veps = sb("veps", [P, QT])
        rstd = sb("rstd", [P, QT])
        xn = sb("xn", [P, 2, D])
        xT = sb("xT", [P, 2, KT, QT * P], F32R)
        wq_raw = sb("wq_raw", [P, NJ, KT, N])
        wq = sb("wq", [P, NJ, 2, KT, N], F32R)
        kv_raw = sb("kv_raw", [P, NJ, 2, KT, DH])
        kv = sb("kv", [P, NJ, 2, 2, KT, DH], F32R)
        sq = sb("sq", [P, 2, N])
        ss = sb("ss", [P, 2, G])
        ms = sb("ms", [P, 2, G])
        rq = sb("rq", [P, 2, G])
        qn = sb("qn", [P, 2, N])
        qT = sb("qT", [P, 4, 2, N], F32R)
        ptr = ps("ptr", [P, 2, 512])
        pq = ps("pq", [P, 4, 512])

        w_in, lat_out, id_ok, half_ok, w_ok = (sem(n) for n in ("w_in", "lat_out", "id_ok", "half_ok", "w_ok"))
        x_in = [sem(f"x_in{t}") for t in range(QT // 2)]
        bn, var_ok, ve_ok, rstd_ok, xn_ok, xt_ps, xhi_ok, xlo_ok = (
            sem(n) for n in ("bn", "var_ok", "ve_ok", "rstd_ok", "xn_ok", "xt_ps", "xhi_ok", "xlo_ok"))
        wq_in = [sem("wq_in0"), sem("wq_in1")]
        kv_in = [sem("kv_in0"), sem("kv_in1")]
        kv_out = [sem("kv_out0"), sem("kv_out1")]
        q_out = [sem(f"q_out{i}") for i in range(4)]
        wqhi_ok, wqlo_ok, kvhi_ok, kvlo_ok = (sem(n) for n in ("wqhi_ok", "wqlo_ok", "kvhi_ok", "kvlo_ok"))
        q_ps, sq_ok, ss_ok, ms_ok, rq_ok, qn_ok, qt_ps, qhi_ok, qlo_ok = (
            sem(n) for n in ("q_ps", "sq_ok", "ss_ok", "ms_ok", "rq_ok", "qn_ok", "qt_ps", "qhi_ok", "qlo_ok"))

        x_t = x.rearrange("b (t p) n -> (b t) p n", p=P)
        wq_v = Wq.rearrange("(t p) n -> p t n", p=P)
        wk_v = Wk.rearrange("(t p) n -> p t n", p=P)
        wv_v = Wv.rearrange("(t p) n -> p t n", p=P)

        steps = []
        for j in range(NJ):
            o = j * QT
            steps += [(o - 12, "load", j, 0), (o - 5.5, "whi", j, 0), (o - 4.5, "wlo", j, 0), (o - 3.5, "kvhi", j, 0),
                      (o - 3.3, "kvlo", j, 0), (o - 3, "kvst", j, 0)]
            for t in range(QT):
                p = o + t
                steps += [(p, "q", j, t), (p + .9, "sq", j, t), (p + 1.1, "ss", j, t), (p + 1.2, "pow", j, t),
                          (p + 1.9, "qn", j, t), (p + 2.7, "qt", j, t), (p + 2.8, "qhi", j, t), (p + 3.2, "qlo", j, t),
                          (p + 3.3, "qst", j, t)]
        steps.sort()

        with nc.Block() as block:

            @block.gpsimd
            def _(pool):
                start_ahead(pool, wq_in + kv_in + kv_out + q_out + [wqhi_ok, wqlo_ok, kvhi_ok, kvlo_ok,
                            q_ps, sq_ok, ss_ok, ms_ok, rq_ok, qn_ok, qt_ps, qhi_ok, qlo_ok])

        with nc.Block() as block:

            def run(eng, emit, first=()):
                pipeline(eng, KVH // NJ, UT, steps, emit, first)

            @block.sync
            def _(sp):
                for t in range(QT // 2):
                    sp.dma_start(xin[:, 2 * t:2 * t + 2], x_t[2 * t:2 * t + 2].rearrange("t p n -> p t n")).then_inc(x_in[t], 16)
                sp.dma_start(wcol[:, 0:1], q_norm_w.rearrange("(p o) -> p o", o=1)).then_inc(w_in, 16)
                sp.dma_start(wcol[:, 1:2], k_norm_w.rearrange("(p o) -> p o", o=1)).then_inc(w_in, 16)

                def step(n, what, j, t):
                    k, v = NJ * n + j, n * UT + (j * QT + t)
                    if what == "lat":
                        sp.wait_ge(xlo_ok, QT)
                        sp.dma_start(scr["lat"][t], xT[:, :, :, t * S:(t + 1) * S].bitcast(F32)).then_inc(lat_out, 16)
                    elif what == "load":
                        sp.wait_ge(wqlo_ok, AHEAD + k - 1)
                        sp.wait_ge(kvlo_ok, AHEAD + k - 1)
                        sp.dma_start(wq_raw[:, j], wq_v[:, :, bass.ds(k * N, N)]).then_inc(wq_in[j], 16)
                        sp.dma_start(kv_raw[:, j, 0], wk_v[:, :, bass.ds(k * DH, DH)]).then_inc(kv_in[j], 16)
                        sp.dma_start(kv_raw[:, j, 1], wv_v[:, :, bass.ds(k * DH, DH)]).then_inc(kv_in[j], 16)
                    elif what == "kvst":
                        sp.wait_ge(kvlo_ok, AHEAD + k + 1)
                        sp.dma_start(scr["kv"][bass.ds(k, 1)].rearrange("o p a c t n -> (o p) (a c t n)"),
                                     kv[:, j].bitcast(F32).rearrange("p a c t n -> p (a c t n)")).then_inc(kv_out[j], 16)
                    elif what == "qst":
                        sp.wait_ge(qlo_ok, AHEAD + v + 1)
                        row = scr["q"][bass.ds(k + (t // BT) * KVH, 1)].rearrange("o p c g s -> (o p) c g s")
                        for c in range(2):
                            sp.dma_start(row[:, c, :, (t % BT) * P:(t % BT + 1) * P],
                                         qT[:, t % 4, c].bitcast(F32).rearrange("p (g s) -> p g s", g=G)
                                         ).then_inc(q_out[t % 4], 16)
                run(sp, step, [(1.5 + 3 * b, "lat", 0, b) for b in range(B)])
                sp.wait_ge(lat_out, 16 * B)
                for j in range(NJ):
                    sp.wait_ge(kv_out[j], AHEAD + 16 * (KVH // NJ))
                for i in range(4):
                    sp.wait_ge(q_out[i], AHEAD + 32 * (KVH * QT // 4))

            @block.gpsimd
            def _(pool):
                identity(pool, ident, id_ok)
                pool.memset(mhalf[:], -0.5).then_inc(half_ok, 1)
                pool.wait_ge(half_ok, 1)
                pool.wait_ge(ve_ok, QT)
                pool.tensor_tensor(rstd[:], veps[:], mhalf[:], ALU.pow).then_inc(rstd_ok, 1)

                def step(n, what, j, t):
                    if what == "pow":
                        pool.wait_ge(ms_ok, AHEAD + n * UT + (j * QT + t + 1))
                        pool.tensor_tensor(rq[:, t % 2], ms[:, t % 2], mhalf[:, 0:G], ALU.pow).then_inc(rq_ok, 1)
                run(pool, step)

            @block.scalar
            def _(act):
                for t in range(QT):
                    act.wait_ge(xt_ps, t + 1)
                    act.copy(xT[:, HI, :, t * P:(t + 1) * P],
                             ptr[:, t % 2].rearrange("p (c r) -> p c r", c=KT)).then_inc(xhi_ok, 1)

                def step(n, what, j, t):
                    k, v = NJ * n + j, n * UT + (j * QT + t)
                    if what == "whi":
                        act.wait_ge(wq_in[j], AHEAD + 16 * n + 16)
                        act.wait_ge(q_ps, AHEAD + (k - 1) * QT)
                        act.copy(wq[:, j, HI], wq_raw[:, j]).then_inc(wqhi_ok, 1)
                    elif what == "kvhi":
                        act.wait_ge(kv_in[j], AHEAD + 32 * n + 32)
                        act.wait_ge(kv_out[j], AHEAD + 16 * n)
                        for a in range(2):
                            act.copy(kv[:, j, a, HI], kv_raw[:, j, a]).then_inc(kvhi_ok, 1)
                    elif what == "sq":
                        act.wait_ge(q_ps, AHEAD + v + 1)
                        act.wait_ge(ss_ok, AHEAD + v - 1)
                        act.activation(sq[:, t % 2], pq[:, t % 4], ACT.Square).then_inc(sq_ok, 1)
                    elif what == "qhi":
                        act.wait_ge(qt_ps, AHEAD + v + 1)
                        act.wait_ge(q_out[t % 4], AHEAD + 32 * (k * (QT // 4) + t // 4))
                        act.activation(qT[:, t % 4, HI], ptr[:, t % 2], ACT.Copy, scale=wcol[:, 3:4]).then_inc(qhi_ok, 1)
                act.wait_ge(w_ok, 2)
                run(act, step)

            @block.tensor
            def _(pe):
                pe.wait_ge(id_ok, 2)
                for t in range(QT):
                    pe.wait_ge(xn_ok, t + 1)
                    if t >= 2:
                        pe.wait_ge(xlo_ok, t - 1)
                    for c in range(KT):
                        last = pe.transpose(ptr[:, t % 2, c * P:(c + 1) * P], xn[:, t % 2, c * P:(c + 1) * P], ident[:])
                    last.then_inc(xt_ps, 1)
                pe.wait_ge(xlo_ok, QT)

                def step(n, what, j, t):
                    k, v = NJ * n + j, n * UT + (j * QT + t)
                    if what == "q":
                        if t == 0:
                            pe.wait_ge(wqlo_ok, AHEAD + k + 1)
                        pe.wait_ge(qn_ok, AHEAD + v - 3)
                        i = 0
                        for c in range(KT):
                            for xp, wp in ((HI, HI), (LO, HI), (HI, LO)):
                                mm = pe.matmul(pq[:, t % 4], xT[:, xp, c, t * P:(t + 1) * P], wq[:, j, wp, c],
                                               start=(i == 0), stop=(i == 3 * KT - 1))
                                i += 1
                        mm.then_inc(q_ps, 1)
                    elif what == "qt":
                        pe.wait_ge(qn_ok, AHEAD + v + 1)
                        pe.wait_ge(qlo_ok, AHEAD + v - 1)
                        for g in range(G):
                            mm = pe.transpose(ptr[:, t % 2, g * P:(g + 1) * P], qn[:, t % 2, g * DH:(g + 1) * DH], ident[:])
                        mm.then_inc(qt_ps, 1)
                run(pe, step)

            @block.vector
            def _(dve):
                for t in range(QT):
                    dve.wait_ge(x_in[t // 2], 16)
                    dve.bn_stats(stats[:, t], xin[:, t]).then_inc(bn, 1)
                for t in range(QT):
                    dve.wait_ge(bn, t + 1)
                    dve.bn_aggr(mv[:, t], stats[:, t]).then_inc(var_ok, 1)
                for t in range(QT):
                    dve.wait_ge(var_ok, t + 1)
                    dve.tensor_scalar(veps[:, t:t + 1], mv[:, t, 1:2], EPS_LN, None, ALU.add).then_inc(ve_ok, 1)
                dve.wait_ge(rstd_ok, 1)
                for t in range(QT + 1):
                    if t < QT:
                        if t >= 2:
                            dve.wait_ge(xt_ps, t - 1)
                        dve.tensor_scalar(xn[:, t % 2], xin[:, t], mv[:, t, 0:1], rstd[:, t:t + 1],
                                          ALU.subtract, ALU.mult).then_inc(xn_ok, 1)
                    if t >= 1:
                        v = t - 1
                        dve.wait_ge(xhi_ok, v + 1)
                        dve.tensor_tensor(xT[:, LO, :, v * P:(v + 1) * P],
                                          ptr[:, v % 2].rearrange("p (c r) -> p c r", c=KT),
                                          xT[:, HI, :, v * P:(v + 1) * P].bitcast(F32),
                                          ALU.subtract).then_inc(xlo_ok, 1)
                dve.wait_ge(w_in, 32)
                dve.tensor_tensor(wcol[:, 2:3], wcol[:, 0:1], wcol[:, 1:2], ALU.mult).then_inc(w_ok, 1)
                dve.wait_ge(w_ok, 1)
                dve.tensor_scalar(wcol[:, 3:4], wcol[:, 2:3], SCALE, None, ALU.mult).then_inc(w_ok, 1)
                dve.wait_ge(w_ok, 2)

                def step(n, what, j, t):
                    k, v, s = NJ * n + j, n * UT + (j * QT + t), t % 2
                    if what == "wlo":
                        dve.wait_ge(wqhi_ok, AHEAD + k + 1)
                        dve.tensor_tensor(wq[:, j, LO], wq_raw[:, j], wq[:, j, HI].bitcast(F32),
                                          ALU.subtract).then_inc(wqlo_ok, 1)
                    elif what == "kvlo":
                        dve.wait_ge(kvhi_ok, AHEAD + 2 * k + 2)
                        dve.tensor_tensor(kv[:, j, :, LO], kv_raw[:, j], kv[:, j, :, HI].bitcast(F32),
                                          ALU.subtract).then_inc(kvlo_ok, 1)
                    elif what == "ss":
                        dve.wait_ge(sq_ok, AHEAD + v + 1)
                        dve.tensor_reduce(ss[:, s], sq[:, s].rearrange("p (g n) -> p g n", g=G),
                                          AX.X, ALU.add).then_inc(ss_ok, 1)
                        dve.wait_ge(ss_ok, AHEAD + v + 1)
                        dve.tensor_scalar(ms[:, s], ss[:, s], 1.0 / DH, EPS_RMS, ALU.mult, ALU.add).then_inc(ms_ok, 1)
                    elif what == "qn":
                        dve.wait_ge(rq_ok, AHEAD + v + 1)
                        dve.wait_ge(qt_ps, AHEAD + v - 1)
                        dve.tensor_tensor(qn[:, s].rearrange("p (g n) -> p g n", g=G),
                                          pq[:, t % 4].rearrange("p (g n) -> p g n", g=G),
                                          rq[:, s].unsqueeze(2).to_broadcast([P, G, DH]), ALU.mult).then_inc(qn_ok, 1)
                    elif what == "qlo":
                        dve.wait_ge(qhi_ok, AHEAD + v + 1)
                        dve.scalar_tensor_tensor(out=qT[:, t % 4, LO], in0=ptr[:, s], scalar=wcol[:, 3:4],
                                                 in1=qT[:, t % 4, HI].bitcast(F32), op0=ALU.mult,
                                                 op1=ALU.subtract).then_inc(qlo_ok, 1)
                run(dve, step)


def attend(nc, d, scr, ctx_4096):
    B, S, D, L, DH, KVH, G, KT = (d[k] for k in ("B", "S", "D", "L", "DH", "KVH", "G", "KT"))
    KV = S + L
    NT = -(-KV // P)
    LAST = KV - (NT - 1) * P
    KVP = KV + KV % 2
    NH = 2
    HALF = G * S // NH
    UT = NH * NT
    CH = [(c, min(c + 512, KVP)) for c in range(0, KVP, 512)]
    NC = len(CH)
    CT = -(-L // P)
    PARTS = 3
    NP = 3
    NR = NC + 1
    assert NT % 2 == 1 and UT % NP == 0 and UT % 2 == 0 and HALF == 512 and NC == 4 and NT > 4 * (NC - 1) + 1 and CT <= NT

    def rows(t):
        return P if t < NT - 1 else LAST

    def chunk_tiles(c):
        return range(4 * c, min(4 * c + 4, NT))

    with ExitStack() as ctx:
        sb, ps, sem = tools(nc, ctx, "att")
        ident = sb("ident", [P, P])
        ones = sb("ones", [P, P])
        mhalf = sb("mhalf", [P, 4])
        ctxT = sb("ctxT", [P, 2, KT, KVP], F32R)
        wkv = sb("wkv", [P, 2, 2, KT, DH], F32R)
        kT = sb("kT", [P, 2, KVP], F32R)
        vraw = sb("vraw", [P, NT * P])
        V = sb("V", [P, 2, NT, DH], F32R)
        sq = sb("sq", [P, 2, 512])
        var = sb("var", [P, NT])
        rk = sb("rk", [P, NT])
        q = sb("q", [P, 2, NH, HALF], F32R)
        sc = sb("sc", [P, UT, HALF])
        pr = sb("pr", [P, 2, NP, HALF], F32R)
        mx = sb("mx", [P, NH, HALF])
        sm = sb("sm", [P, NH, HALF])
        red = sb("red", [P, 4])
        den = sb("den", [P, 4])
        rden = sb("rden", [P, 4])
        diag = sb("diag", [P, 4, P])
        oraw = sb("oraw", [P, HALF])
        on = sb("on", [P, HALF])
        pqk = ps("pqk", [P, 2, 512])
        ppv = ps("ppv", [P, 512])
        pkv = ps("pkv", [P, 2, 512])
        pss = ps("pss", [P, 512])
        pred = ps("pred", [P, 512])
        pmax = ps("pmax", [P, 512])

        lat_in, w_in, o_out = sem("lat_in"), sem("w_in"), sem("o_out")
        x_in = [sem(f"x_in{i}") for i in range(4)]
        q_in = [sem("q_in0"), sem("q_in1")]
        id_ok, cst_ok = sem("id_ok"), sem("cst_ok")
        names = ("xt_ps xhi_ok xlo_ok k_ps v_ps khi_ok klo_ok ksq_ok vraw_ok vt_ps vhi_ok vlo_ok ss_ps var_ok rk_ok "
                 "qk_ps sc_ok max_ok mt_ps red_ok diag_ok mb_ps sub_ok exp_ok phi_ok plo_ok sum_ok pv_ps oraw_ok "
                 "dt_ps den_ok rden_ok ddiag_ok db_ps on_ok").split()
        loop_sems = [sem(n) for n in names]
        (xt_ps, xhi_ok, xlo_ok, k_ps, v_ps, khi_ok, klo_ok, ksq_ok, vraw_ok, vt_ps, vhi_ok, vlo_ok, ss_ps, var_ok, rk_ok,
         qk_ps, sc_ok, max_ok, mt_ps, red_ok, diag_ok, mb_ps, sub_ok, exp_ok, phi_ok, plo_ok, sum_ok, pv_ps, oraw_ok,
         dt_ps, den_ok, rden_ok, ddiag_ok, db_ps, on_ok) = loop_sems

        LAG = 21.5
        steps = []
        for h in range(NH):
            for t in range(NT):
                p = h * NT + t
                steps += [(p, "qk", h, t), (p + 0.39, "copy", h, t)]
                if t % 2 == 0:
                    steps += [(p + LAG - 4.3, "sub", h, t)]
                steps += [(p + LAG - 3.14, "exp", h, t), (p + LAG - 2.3, "hi", h, t),
                          (p + LAG - 1.63, "lo", h, t), (p + LAG, "pv", h, t)]
                if t >= 1:
                    steps += [(p + 1.18, "max", h, t), (p + LAG - 1.5, "sum", h, t)]
            e = (h + 1) * NT
            steps += [(e + 1.59, "mt", h, 0), (e + 1.47, "red", h, 0), (e + 3, "mb", h, 0)]
            f = e + LAG
            steps += [(f - 0.6, "oraw", h, 0), (f + 0.67, "dt", h, 0), (f + 1.83, "dred", h, 0), (f + 3.76, "db", h, 0),
                      (f + 4.21, "on", h, 0), (f + 4.31, "st", h, 0)]
            steps += [(h * NT - NT + .1, "ldq", h, 0)]
        for c, (k, v, vt) in enumerate(((-12.7, 1, 10.6), (-9, 4, 15.5), (-3.21, 6.63, 20.25), (-1.5, 11.35, 24.37))):
            for i in range(PARTS):
                steps += [(k + i * 0.82, "k", i, c), (v + i * 0.82, "v", i, c)]
            k, v = k + (PARTS - 1) * 0.82, v + (PARTS - 1) * 0.82
            steps += [(k + 0.9, "khi", 0, c), (k + 1.03, "klo", 0, c), (k + 3.5, "kn", 0, c),
                      (k + 3.6, "var", 0, c), (k + 3.7, "pow", 0, c)]
            steps += [(v + 0.9, "vhi", 0, c)]
            steps += [(vt, "vt", 0, c), (vt + 0.76, "vthi", 0, c), (vt + 1.64, "vtlo", 0, c)]
        steps += [(-17, "ldw", 0, 0)]
        steps.sort()

        XP = [(x, min(x + 3, CT)) for x in range(0, CT - 1, 3)][:-1]
        XP += [(XP[-1][1], CT)]
        assert len(XP) == len(x_in)
        context = [(0.26 + i * 0.99 + d, what, 0, i) for i in range(CT)
                   for d, what in ((0, "xt"), (0.26, "xhi"), (0.6, "xlo"))]
        loads = [(12.89, "ldw", 0, 0), (12.89 + .1, "ldlat", 0, 0)]
        loads += [(z - 1 + LAG - 1.5 + .1, "ldx", 0, i) for i, (a, z) in enumerate(XP)]

        def window(*parts):
            w = [(p + shift, dn, what, h, t) for dn, shift, part in parts for p, what, h, t in part]
            return [x[1:] for x in sorted(w, key=lambda x: x[0])]

        early = [x for x in steps if x[0] < 0]
        own = [x for x in steps if 0 <= x[0] < UT]
        late = [x for x in steps if x[0] >= UT]
        in_last = [x for x in loads if x[0] < UT]
        in_boundary = [x for x in loads if x[0] >= UT]
        start_early = [x for x in early if x[1] != "ldw"]
        START = window((0, -2 * UT, loads), (0, 0, context), (0, UT - 3.33, start_early))
        FIRST = window((0, 0, own), (1, UT, early))
        MIDDLE = window((-1, -UT, late), (0, 0, own), (1, UT, early))
        LAST_ONE = window((-1, -UT, late), (0, 0, own))
        LAST_LOADS = window((-1, -UT, late), (0, 0, own), (1, 0, in_last))
        BOUNDARY = window((-1, -UT, late), (0, -UT, in_boundary), (0, 0, context), (0, UT - 3.33, start_early))
        TAIL = window((-1, -UT, late))

        USES = [(dn, what, c) for dn, what, h, c in MIDDLE if what in ("k", "v", "vt") and h == 0]
        BANK = {(what, c): i % 2 for i, (_, what, c) in enumerate(USES)}
        assert len(USES) == 3 * NC
        BANK.update({("xt", i): i % 2 for i in range(CT)})

        def uses(steps_of):
            return [(dn, what, c) for dn, what, h, c in steps_of if (what, c) in BANK and h == 0]

        def bank_before(seen, what, c):
            return next((u for u in reversed(seen) if BANK[u[1:]] == BANK[(what, c)]), None)

        def rounds(eng, step):
            def run(n, steps_of, earlier, xb=None, last=False, head=0, fresh=False):
                seen = [(dn - back, what, c) for back, w in earlier for dn, what, c in uses(w)]
                for dn, what, h, t in steps_of:
                    if (what, t) in BANK and h == 0:
                        step(n + dn, what, h, t, before=bank_before(seen, what, t), dn=dn, xb=xb, fresh=fresh)
                        seen.append((dn, what, t))
                    else:
                        step(n + dn, what, h, t, last=last, xb=xb, dn=dn, head=head)

            def batch(b, loads_of_next):
                n = b * KVH
                run(n, FIRST, [(0, BOUNDARY)], xb=b, fresh=True)
                with eng.Fori(1, KVH - 1) as r:
                    run(n + r, MIDDLE, [(1, MIDDLE)], head=r)
                run(n + (KVH - 1), loads_of_next or LAST_ONE, [(1, MIDDLE)], xb=b + 1, head=-1)

            run(0, START, [], xb=0, fresh=True)
            with eng.Fori(0, B - 1) as b:
                batch(b, LAST_LOADS)
                run(b * KVH + KVH, BOUNDARY, [(2, MIDDLE), (1, LAST_ONE)], xb=b + 1, last=True, fresh=True)
            batch(B - 1, None)
            run(B * KVH, TAIL, [], last=True)

        def sums(n, h, t):
            return n * UT + (h * NT + max(t, 1) + 1)

        def tiles(n, h, t):
            return n * UT + (h * NT + t + 1)

        def rk_signals(n, c):
            return n * NR + (c + 1 if c < NC - 1 else NR)

        with nc.Block() as block:

            @block.gpsimd
            def _(pool):
                start_ahead(pool, loop_sems + [lat_in, w_in, o_out] + x_in + q_in)
                identity(pool, ident, id_ok)
                pool.memset(mhalf[:], -0.5).then_inc(cst_ok, 1)

            @block.vector
            def _(dve):
                dve.memset(ones[:], 1.0).then_inc(cst_ok, 1)
                dve.memset(vraw[:, KVP:], 0.0).then_inc(cst_ok, 1)
                dve.memset(ctxT[:, :, :, KV:KVP].bitcast(F32), 0.0).then_inc(cst_ok, 1)

        with nc.Block() as block:

            @block.sync
            def _(sp):
                def step(n, what, h, t, before=None, dn=0, last=False, xb=None, head=0, fresh=False):
                    if what == "ldw":
                        k = head + dn
                        sp.wait_ge(k_ps, AHEAD + NC * n)
                        sp.wait_ge(v_ps, AHEAD + NC * n)
                        sp.dma_start(wkv[:].bitcast(F32).rearrange("p a c t n -> p (a c t n)"),
                                     scr["kv"][bass.ds(k, 1)].rearrange("o p a c t n -> (o p) (a c t n)")
                                     ).then_inc(w_in, 16)
                    elif what == "ldlat":
                        sp.dma_start(ctxT[:, :, :, 0:S].bitcast(F32),
                                     scr["lat"][bass.ds(xb, 1)].rearrange("o p c t s -> (o p) c t s")).then_inc(lat_in, 16)
                    elif what == "ldx":
                        a, z = XP[t]
                        used = AHEAD + xb * (KVH * UT) - UT + z
                        sp.wait_ge(plo_ok, used)
                        sp.wait_ge(sum_ok, used)
                        full = min(z, L // P)
                        sp.dma_start(sc[:, a:full], ctx_4096[bass.ds(xb, 1), a * P:full * P]
                                     .rearrange("o (t p) n -> (o p) t n", p=P)).then_inc(x_in[t], 16)
                        if full < z:
                            sp.dma_start(sc[0:L - full * P, full], ctx_4096[bass.ds(xb, 1), full * P:L]
                                         .rearrange("o p n -> (o p) n")).then_inc(x_in[t], 16)
                    elif what == "ldq":
                        sp.wait_ge(qk_ps, AHEAD + (n - 1) * UT + (h + 1) * NT)
                        sp.dma_start(q[:, :, h].bitcast(F32),
                                     scr["q"][bass.ds(n, 1), :, :, h * G // NH:(h + 1) * G // NH]
                                     .rearrange("o p c g s -> (o p) c (g s)")).then_inc(q_in[h], 16)
                    elif what == "st":
                        sp.wait_ge(on_ok, AHEAD + NH * n + h + 1)
                        sp.dma_start(scr["o"][bass.ds(n, 1), :, h * G // NH:(h + 1) * G // NH]
                                     .rearrange("o p g s -> (o p) (g s)"), on[:]).then_inc(o_out, 16)

                rounds(sp, step)
                sp.wait_ge(o_out, AHEAD + 16 * NH * B * KVH)

            @block.tensor
            def _(pe):
                def project_chunk(which, bank, a, z, part, done):
                    terms = [(t, wp, xp) for t in range(KT) for wp, xp in ((HI, HI), (LO, HI), (HI, LO))]
                    n = len(terms) // PARTS
                    for i in range(part * n, part * n + n):
                        t, wp, xp = terms[i]
                        mm = pe.matmul(bank, wkv[:, which, wp, t], ctxT[:, xp, t, a:z],
                                       start=(i == 0), stop=(i == len(terms) - 1))
                    if part == PARTS - 1:
                        mm.then_inc(done, 1)

                def wait_for_bank(n, dn, before, xb):
                    if before is not None:
                        bn, what, c = before
                        if what == "xt":
                            pe.wait_ge(xlo_ok, AHEAD + xb * CT + c + 1)
                        else:
                            pe.wait_ge({"k": klo_ok, "v": vraw_ok, "vt": vlo_ok}[what], AHEAD + NC * (n - dn + bn) + c + 1)

                def wait_for_inputs(n, c, xb):
                    pe.wait_ge(w_in, AHEAD + 16 * n + 16)
                    if xb is not None:
                        pe.wait_ge(lat_in, AHEAD + 16 * xb + 16)
                        pe.wait_ge(xlo_ok, AHEAD + xb * CT + min(CT, -(-(CH[c][1] - S) // P)))

                def step(n, what, h, t, before=None, dn=0, last=False, xb=None, head=0, fresh=False):
                    u, T = NH * n + h, n * UT + (h * NT + t)
                    m = rows(t)
                    if what == "qk":
                        if t == 0:
                            pe.wait_ge(q_in[h], AHEAD + 16 * n + 16)
                        if h == 0 and t % 4 == 0:
                            pe.wait_ge(klo_ok, AHEAD + NC * n + t // 4 + 1)
                        pe.wait_ge(sc_ok, AHEAD + T - 1)
                        for i, (kp, qp) in enumerate(((HI, HI), (LO, HI), (HI, LO))):
                            mm = pe.matmul(pqk[0:m, (h * NT + t) % 2], kT[:, kp, t * P:t * P + m], q[:, qp, h],
                                           start=(i == 0), stop=(i == 2))
                        mm.then_inc(qk_ps, 1)
                    elif what == "mt":
                        pe.wait_ge(max_ok, AHEAD + (NT - 1) * (u + 1))
                        pe.wait_ge(on_ok, AHEAD + u - 1)
                        for c in range(4):
                            mm = pe.transpose(pred[:, c * P:(c + 1) * P], mx[:, h, c * P:(c + 1) * P], ident[:])
                        mm.then_inc(mt_ps, 1)
                    elif what == "mb":
                        pe.wait_ge(diag_ok, AHEAD + u + 1)
                        pe.wait_ge(sub_ok, AHEAD + NT * u)
                        pe.matmul(pmax[:], ones[:], diag[:].rearrange("p c n -> p (c n)"),
                                  start=True, stop=True).then_inc(mb_ps, 1)
                    elif what == "pv":
                        pe.wait_ge(plo_ok, AHEAD + T + 1)
                        if t == 0:
                            pe.wait_ge(oraw_ok, AHEAD + u)
                        if h == 0 and t % 4 == 0:
                            pe.wait_ge(vlo_ok, AHEAD + NC * n + t // 4 + 1)
                        for i, (vp, pp) in enumerate(((HI, HI), (LO, HI), (HI, LO))):
                            mm = pe.matmul(ppv[:], V[0:m, vp, t], pr[0:m, pp, (h * NT + t) % NP],
                                           start=(t == 0 and i == 0), stop=(t == NT - 1 and i == 2))
                        mm.then_inc(pv_ps, 1)
                    elif what == "dt":
                        pe.wait_ge(sum_ok, AHEAD + NT * (u + 1))
                        if last and h == 1:
                            pe.wait_ge(on_ok, AHEAD + u)
                        else:
                            pe.wait_ge(red_ok, AHEAD + u + 2)
                        for c in range(4):
                            mm = pe.transpose(pred[:, c * P:(c + 1) * P], sm[:, h, c * P:(c + 1) * P], ident[:])
                        mm.then_inc(dt_ps, 1)
                    elif what == "db":
                        pe.wait_ge(ddiag_ok, AHEAD + u + 1)
                        pe.matmul(pred[:], ones[:], diag[:].rearrange("p c n -> p (c n)"),
                                  start=True, stop=True).then_inc(db_ps, 1)
                    elif what == "xt":
                        wait_for_bank(n, dn, before, xb)
                        piece = next(i for i, (a, z) in enumerate(XP) if a <= t < z)
                        per = 16 * (1 + (piece == len(XP) - 1))
                        pe.wait_ge(x_in[piece], AHEAD + per * xb + per)
                        w = min(P, L - t * P)
                        for c in range(KT):
                            mm = pe.transpose(pkv[:, BANK["xt", t], c * P:c * P + w], sc[0:w, t, c * P:(c + 1) * P],
                                              ident[0:w, 0:w])
                        mm.then_inc(xt_ps, 1)
                    elif what == "k":
                        if h == 0:
                            wait_for_bank(n, dn, before, xb)
                            wait_for_inputs(n, t, xb if fresh and dn == 0 else None)
                        a, z = CH[t]
                        project_chunk(0, pkv[:, BANK["k", t], 0:z - a], a, z, h, k_ps)
                    elif what == "kn":
                        pe.wait_ge(ksq_ok, AHEAD + NC * n + t + 1)
                        pe.wait_ge(var_ok, AHEAD + rk_signals(n, t - 1) if t else AHEAD + n * NR)
                        for i in chunk_tiles(t):
                            mm = pe.matmul(pss[0:rows(i), i:i + 1], sq[:, t % 2, (i % 4) * P:(i % 4) * P + rows(i)],
                                           ones[:, 0:1], start=True, stop=True)
                        mm.then_inc(ss_ps, 1)
                    elif what == "v":
                        if h == 0:
                            wait_for_bank(n, dn, before, xb)
                            wait_for_inputs(n, t, xb if fresh and dn == 0 else None)
                        a, z = CH[t]
                        project_chunk(1, pkv[:, BANK["v", t], 0:z - a], a, z, h, v_ps)
                    elif what == "vt":
                        wait_for_bank(n, dn, before, xb)
                        pe.wait_ge(vraw_ok, AHEAD + NC * n + t + 1)
                        for i in chunk_tiles(t):
                            mm = pe.transpose(pkv[:, BANK["vt", t], (i % 4) * P:(i % 4 + 1) * P],
                                              vraw[:, i * P:(i + 1) * P], ident[:])
                        mm.then_inc(vt_ps, 1)

                rounds(pe, step)

            @block.scalar
            def _(act):
                def step(n, what, h, t, before=None, dn=0, last=False, xb=None, head=0, fresh=False):
                    u, T = NH * n + h, n * UT + (h * NT + t)
                    m, s = rows(t), h * NT + t
                    if what == "xhi":
                        w = min(P, L - t * P)
                        act.wait_ge(xt_ps, AHEAD + xb * CT + t + 1)
                        act.copy(ctxT[:, HI, :, S + t * P:S + t * P + w],
                                 pkv[:, BANK["xt", t]].rearrange("p (c r) -> p c r", c=KT)[:, :, 0:w]).then_inc(xhi_ok, 1)
                    elif what == "copy":
                        act.wait_ge(qk_ps, AHEAD + T + 1)
                        act.wait_ge(plo_ok, AHEAD + T + 1 - UT)
                        act.wait_ge(sum_ok, AHEAD + sums(n - 1, h, t))
                        if h == 0 and t % 4 == 0:
                            act.wait_ge(rk_ok, AHEAD + rk_signals(n, t // 4))
                        act.activation(sc[0:m, s], pqk[0:m, s % 2], ACT.Copy, scale=rk[0:m, t:t + 1]).then_inc(sc_ok, 1)
                    elif what == "exp":
                        act.wait_ge(sub_ok, AHEAD + T + 1)
                        act.activation(sc[0:m, s], sc[0:m, s], ACT.Exp).then_inc(exp_ok, 1)
                    elif what == "hi":
                        act.wait_ge(exp_ok, AHEAD + T + 1)
                        act.wait_ge(pv_ps, AHEAD + T - NP + 1)
                        act.copy(pr[0:m, HI, s % NP], sc[0:m, s]).then_inc(phi_ok, 1)
                    elif what == "oraw":
                        act.wait_ge(pv_ps, AHEAD + NT * (u + 1))
                        act.wait_ge(on_ok, AHEAD + u)
                        act.copy(oraw[:], ppv[:]).then_inc(oraw_ok, 1)
                    elif what == "khi":
                        a, z = CH[t]
                        act.wait_ge(k_ps, AHEAD + NC * n + t + 1)
                        act.wait_ge(qk_ps, AHEAD + tiles(n - 1, 1, chunk_tiles(t)[-1]))
                        act.copy(kT[:, HI, a:z], pkv[:, BANK["k", t], 0:z - a]).then_inc(khi_ok, 1)
                        act.wait_ge(ss_ps, AHEAD + NC * n + t - 1)
                        act.activation(sq[:, t % 2, 0:z - a], pkv[:, BANK["k", t], 0:z - a], ACT.Square).then_inc(ksq_ok, 1)
                    elif what == "vhi":
                        a, z = CH[t]
                        act.wait_ge(v_ps, AHEAD + NC * n + t + 1)
                        act.wait_ge(vt_ps, AHEAD + NC * (n - 1) + t + 1)
                        act.copy(vraw[:, a:z], pkv[:, BANK["v", t], 0:z - a]).then_inc(vraw_ok, 1)
                    elif what == "vthi":
                        act.wait_ge(vt_ps, AHEAD + NC * n + t + 1)
                        act.wait_ge(pv_ps, AHEAD + tiles(n - 1, 1, chunk_tiles(t)[-1]))
                        w = len(chunk_tiles(t))
                        act.copy(V[:, HI, 4 * t:4 * t + w],
                                 pkv[:, BANK["vt", t], 0:w * P].rearrange("p (a n) -> p a n", n=P)).then_inc(vhi_ok, 1)

                rounds(act, step)

            @block.vector
            def _(dve):
                def diagonal(col):
                    return dve.tensor_tensor(diag[:], ident[:].unsqueeze(1).to_broadcast([P, 4, P]),
                                             col[:].unsqueeze(2).to_broadcast([P, 4, P]), ALU.mult)

                def step(n, what, h, t, before=None, dn=0, last=False, xb=None, head=0, fresh=False):
                    u, T = NH * n + h, n * UT + (h * NT + t)
                    m, s = rows(t), h * NT + t
                    if what == "xlo":
                        w = min(P, L - t * P)
                        dve.wait_ge(xhi_ok, AHEAD + xb * CT + t + 1)
                        dve.tensor_tensor(ctxT[:, LO, :, S + t * P:S + t * P + w],
                                          pkv[:, BANK["xt", t]].rearrange("p (c r) -> p c r", c=KT)[:, :, 0:w],
                                          ctxT[:, HI, :, S + t * P:S + t * P + w].bitcast(F32),
                                          ALU.subtract).then_inc(xlo_ok, 1)
                    elif what == "max":
                        dve.wait_ge(sc_ok, AHEAD + T + 1)
                        if t == 1:
                            dve.wait_ge(mt_ps, AHEAD + u - 1)
                            dve.tensor_tensor(mx[:, h], sc[:, s - 1], sc[:, s], ALU.max).then_inc(max_ok, 1)
                        else:
                            dve.wait_ge(max_ok, AHEAD + (NT - 1) * u + t - 1)
                            dve.tensor_tensor(mx[0:m, h], mx[0:m, h], sc[0:m, s], ALU.max).then_inc(max_ok, 1)
                    elif what == "red":
                        dve.wait_ge(mt_ps, AHEAD + u + 1)
                        dve.tensor_reduce(red[:], pred[:].rearrange("p (c n) -> p c n", c=4), AX.X, ALU.max).then_inc(red_ok, 1)
                        dve.wait_ge(red_ok, AHEAD + u + 1)
                        dve.wait_ge(db_ps, AHEAD + u - 1)
                        diagonal(red).then_inc(diag_ok, 1)
                    elif what == "sub":
                        if t == 0:
                            dve.wait_ge(mb_ps, AHEAD + u + 1)
                        w = min(2, NT - t)
                        dve.tensor_tensor(sc[0:m, s:s + w], sc[0:m, s:s + w],
                                          pmax[0:m].unsqueeze(1).to_broadcast([m, w, HALF]), ALU.subtract).then_inc(sub_ok, w)
                    elif what == "lo":
                        dve.wait_ge(phi_ok, AHEAD + T + 1)
                        dve.tensor_tensor(pr[0:m, LO, s % NP], sc[0:m, s], pr[0:m, HI, s % NP].bitcast(F32),
                                          ALU.subtract).then_inc(plo_ok, 1)
                    elif what == "dred":
                        dve.wait_ge(dt_ps, AHEAD + u + 1)
                        dve.tensor_reduce(den[:], pred[:].rearrange("p (c n) -> p c n", c=4), AX.X, ALU.add).then_inc(den_ok, 1)
                        dve.wait_ge(den_ok, AHEAD + u + 1)
                        dve.reciprocal(rden[:], den[:]).then_inc(rden_ok, 1)
                        dve.wait_ge(rden_ok, AHEAD + u + 1)
                        if last and h == 1:
                            dve.wait_ge(db_ps, AHEAD + u)
                        else:
                            dve.wait_ge(mb_ps, AHEAD + u + 2)
                        diagonal(rden).then_inc(ddiag_ok, 1)
                    elif what == "on":
                        dve.wait_ge(db_ps, AHEAD + u + 1)
                        dve.wait_ge(oraw_ok, AHEAD + u + 1)
                        dve.wait_ge(o_out, AHEAD + 16 * u)
                        dve.tensor_tensor(on[:], oraw[:], pred[:], ALU.mult).then_inc(on_ok, 1)
                    elif what == "klo":
                        a, z = CH[t]
                        dve.wait_ge(ksq_ok, AHEAD + NC * n + t + 1)
                        dve.tensor_tensor(kT[:, LO, a:z], pkv[:, BANK["k", t], 0:z - a], kT[:, HI, a:z].bitcast(F32),
                                          ALU.subtract).then_inc(klo_ok, 1)
                    elif what == "var":
                        dve.wait_ge(ss_ps, AHEAD + NC * n + t + 1)
                        dve.wait_ge(rk_ok, AHEAD + rk_signals(n - 1, t))
                        i, z = chunk_tiles(t)[0], min(chunk_tiles(t)[-1] + 1, NT - 1)
                        dve.tensor_scalar(var[:, i:z], pss[:, i:z], 1.0 / DH, EPS_RMS, ALU.mult, ALU.add).then_inc(var_ok, 1)
                        if t == NC - 1:
                            dve.tensor_scalar(var[0:LAST, NT - 1:NT], pss[0:LAST, NT - 1:NT], 1.0 / DH, EPS_RMS,
                                              ALU.mult, ALU.add).then_inc(var_ok, 1)
                    elif what == "vtlo":
                        w = len(chunk_tiles(t))
                        dve.wait_ge(vhi_ok, AHEAD + NC * n + t + 1)
                        dve.tensor_tensor(V[:, LO, 4 * t:4 * t + w],
                                          pkv[:, BANK["vt", t], 0:w * P].rearrange("p (a n) -> p a n", n=P),
                                          V[:, HI, 4 * t:4 * t + w].bitcast(F32), ALU.subtract).then_inc(vlo_ok, 1)

                rounds(dve, step)

            @block.gpsimd
            def _(pool):
                def step(n, what, h, t, before=None, dn=0, last=False, xb=None, head=0, fresh=False):
                    u, T = NH * n + h, n * UT + (h * NT + t)
                    m, s = rows(t), h * NT + t
                    if what == "sum":
                        pool.wait_ge(exp_ok, AHEAD + T + 1)
                        if t == 1:
                            pool.wait_ge(dt_ps, AHEAD + u - 1)
                            pool.tensor_tensor(sm[:, h], sc[:, s - 1], sc[:, s], ALU.add).then_inc(sum_ok, 2)
                        else:
                            pool.wait_ge(sum_ok, AHEAD + T)
                            pool.tensor_tensor(sm[0:m, h], sm[0:m, h], sc[0:m, s], ALU.add).then_inc(sum_ok, 1)
                    elif what == "pow":
                        i, z = chunk_tiles(t)[0], min(chunk_tiles(t)[-1] + 1, NT - 1)
                        pool.wait_ge(var_ok, AHEAD + rk_signals(n, t))
                        pool.wait_ge(sc_ok, AHEAD + tiles(n - 1, 1, chunk_tiles(t)[-1]))
                        pool.tensor_tensor(rk[:, i:z], var[:, i:z], mhalf[:, 0:z - i], ALU.pow).then_inc(rk_ok, 1)
                        if t == NC - 1:
                            pool.tensor_tensor(rk[0:LAST, NT - 1:NT], var[0:LAST, NT - 1:NT], mhalf[0:LAST, 0:1],
                                               ALU.pow).then_inc(rk_ok, 1)

                rounds(pool, step)


def gate_column(sp, act, g, gcol, g_in, g_ok):
    if sp is not None:
        sp.dma_start(gcol[:, 0:1], g.partition_broadcast(P)).then_inc(g_in, 16)
    if act is not None:
        act.wait_ge(g_in, 16)
        act.activation(gcol[:, 1:2], gcol[:, 0:1], ACT.Tanh).then_inc(g_ok, 1)


def project(nc, d, scr, x, Wo, g_xattn):
    B, S, D, DH, HEADS, KVH, G, QT = (d[k] for k in ("B", "S", "D", "DH", "HEADS", "KVH", "G", "QT"))
    BT = S // P
    WC = 4
    HC = 8
    NE = HEADS // HC
    NV = NE * BT
    SL = 4
    with ExitStack() as ctx:
        sb, ps, sem = tools(nc, ctx, "out")
        wo = sb("wo", [P, 2, HEADS, D], F32R)
        wraw = sb("wraw", [P, 2, WC, D])
        oraw = sb("oraw", [P, SL, HC, P])
        o = sb("o", [P, SL, 2, HC, P], F32R)
        xin = sb("xin", [P, BT, D])
        x2 = sb("x2", [P, BT, D])
        gcol = sb("gcol", [P, 2])
        po = ps("po", [P, BT, 512])
        g_in, g_ok = sem("g_in"), sem("g_ok")
        w_in = [sem("w_in0"), sem("w_in1")]
        o_in = [sem(f"o_in{i}") for i in range(SL)]
        x_in, x2_out = [sem("x_in0"), sem("x_in1")], [sem("x2_out0"), sem("x2_out1")]
        whi_ok, wlo_ok, ohi_ok, olo_ok, o_ps, x2_ok = (
            sem(n) for n in ("whi_ok", "wlo_ok", "ohi_ok", "olo_ok", "o_ps", "x2_ok"))

        wo_v = Wo.rearrange("(h p) n -> p h n", p=P)
        x_v = x.rearrange("b (t p) n -> b t p n", p=P)

        with nc.Block() as block:

            @block.gpsimd
            def _(pool):
                start_ahead(pool, o_in + x_in + x2_out + [ohi_ok, olo_ok, o_ps, x2_ok])

        with nc.Block() as block:

            def batches(eng, batch):
                batch(0, True)
                with eng.Fori(1, B) as b:
                    batch(b, False)

            @block.sync
            def _(sp):
                gate_column(sp, None, g_xattn, gcol, g_in, g_ok)

                steps = [(2 * v - 6, "load", v // BT, v % BT) for v in range(NV)]
                steps += [(-1.5, "x", 0, t) for t in range(BT)] + [(2 * NV + 1 + t, "store", 0, t) for t in range(BT)]

                def step(b, what, e, t):
                    v = e * BT + t
                    if what == "load":
                        sp.wait_ge(olo_ok, AHEAD + b * NV + (v + 1) - SL)
                        for k in range(HC // G):
                            sp.dma_start(oraw[:, v % SL, k * G:(k + 1) * G],
                                         scr["o"][bass.ds(b * KVH + (e * (HC // G) + k), 1), :, :, t * P:(t + 1) * P]
                                         .rearrange("o p g s -> (o p) g s")).then_inc(o_in[v % SL], 16)
                    elif what == "x":
                        sp.wait_ge(x2_ok, AHEAD + b * BT + t - 1)
                        sp.dma_start(xin[:, t], x_v[bass.ds(b, 1), t].rearrange("o p n -> (o p) n")).then_inc(x_in[t], 16)
                    elif what == "store":
                        sp.wait_ge(x2_ok, AHEAD + b * BT + t + 1)
                        sp.dma_start(scr["x2"][bass.ds((b * BT + t) * P, P)], x2[:, t]).then_inc(x2_out[t], 16)
                pipeline(sp, B, 2 * NV, steps, step)
                for t in range(BT):
                    sp.wait_ge(x2_out[t], AHEAD + 16 * B)

            @block.gpsimd
            def _(pool):
                for i in range(HEADS // WC):
                    if i >= 2:
                        pool.wait_ge(wlo_ok, i - 1)
                    pool.dma_start(wraw[:, i % 2], wo_v[:, WC * i:WC * i + WC]).then_inc(w_in[i % 2], 16)

            @block.scalar
            def _(act):
                gate_column(None, act, g_xattn, gcol, g_in, g_ok)

                def batch(b, first):
                    for e in range(NE):
                        for t in range(BT):
                            v = e * BT + t
                            act.wait_ge(o_in[v % SL], AHEAD + (b * (NV // SL) + v // SL + 1) * (16 * HC // G))
                            act.wait_ge(o_ps, AHEAD + b * NV + (v + 1) - SL)
                            act.copy(o[:, v % SL, HI], oraw[:, v % SL]).then_inc(ohi_ok, 1)
                            if first:
                                act.wait_ge(w_in[v % 2], 16 * (v // 2) + 16)
                                act.copy(wo[:, HI, WC * v:WC * v + WC], wraw[:, v % 2]).then_inc(whi_ok, 1)
                batches(act, batch)

            @block.vector
            def _(dve):
                def batch(b, first):
                    for e in range(NE):
                        for t in range(BT):
                            v = e * BT + t
                            dve.wait_ge(ohi_ok, AHEAD + b * NV + v + 1)
                            dve.tensor_tensor(o[:, v % SL, LO], oraw[:, v % SL], o[:, v % SL, HI].bitcast(F32),
                                              ALU.subtract).then_inc(olo_ok, 1)
                            if first:
                                dve.wait_ge(whi_ok, v + 1)
                                dve.tensor_tensor(wo[:, LO, WC * v:WC * v + WC], wraw[:, v % 2],
                                                  wo[:, HI, WC * v:WC * v + WC].bitcast(F32), ALU.subtract).then_inc(wlo_ok, 1)
                    for t in range(BT):
                        dve.wait_ge(o_ps, AHEAD + b * NV + NV - BT + t + 1)
                        dve.wait_ge(x_in[t], AHEAD + 16 * b + 16)
                        dve.wait_ge(x2_out[t], AHEAD + 16 * b)
                        dve.scalar_tensor_tensor(out=x2[:, t], in0=po[:, t], scalar=gcol[:, 1:2], in1=xin[:, t],
                                                 op0=ALU.mult, op1=ALU.add).then_inc(x2_ok, 1)
                dve.wait_ge(g_ok, 1)
                batches(dve, batch)

            @block.tensor
            def _(pe):
                with pe.Fori(0, B) as b:
                    for e in range(NE):
                        for t in range(BT):
                            v = e * BT + t
                            if e == 0:
                                pe.wait_ge(x2_ok, AHEAD + b * BT + t - 1)
                            pe.wait_ge(olo_ok, AHEAD + b * NV + v + 1)
                            for h in range(HC):
                                if h % WC == 0:
                                    pe.wait_ge(wlo_ok, (e * HC + h) // WC + 1)
                                for p, (op, wp) in enumerate(((HI, HI), (LO, HI), (HI, LO))):
                                    mm = pe.matmul(po[:, t], o[:, v % SL, op, h], wo[:, wp, e * HC + h],
                                                   start=(e == 0 and h == 0 and p == 0),
                                                   stop=(e == NE - 1 and h == HC - 1 and p == 2))
                            mm.then_inc(o_ps, 1)


def ffn(nc, d, scr, g_ffn, c1_w, c2_w, w1, w2t, out):
    S, D, KT, QT = (d[k] for k in ("S", "D", "KT", "QT"))
    RANK = c1_w.shape[0]
    INTER = w1.shape[0]
    IT = INTER // P
    BLK = 32
    CW = 448
    NCH = INTER // CW
    NB = CW // BLK
    NS = 4
    NW = 2 * IT
    HB = (0, 1, 0, 1)
    GT = [(g, min(g + 4, IT)) for g in range(0, IT, 4)]
    assert NCH * CW == INTER and IT * P == INTER
    with ExitStack() as ctx:
        sb, ps, sem = tools(nc, ctx, "ffn")
        ident = sb("ident", [P, P])
        mhalf = sb("mhalf", [P, QT])
        rank = sb("rank", [P, NB, BLK])
        gcol = sb("gcol", [P, 2])
        stage = sb("stage", [P, NS, D])
        c1 = sb("c1", [RANK, D])
        c2 = sb("c2", [P, IT, RANK])
        c1T = sb("c1T", [P, KT, RANK])
        c2T = sb("c2T", [RANK, INTER])
        w1T = sb("w1T", [P, 2, KT, INTER], F32R)
        w2 = sb("w2", [P, 2, IT, D], F32R)
        xall = sb("xall", [P, QT, D])
        xin = sb("xin", [P, 2, D])
        stats = sb("stats", [P, QT, 6])
        mv = sb("mv", [P, QT, 2])
        veps = sb("veps", [P, QT])
        rstd = sb("rstd", [P, QT])
        xn = sb("xn", [P, 2, D])
        xT = sb("xT", [P, 2, 2, KT, P], F32R)
        xTf = sb("xTf", [P, KT, P])
        tT = sb("tT", [RANK, P])
        bm = sb("bm", [P, NB])
        bs = sb("bs", [P, NB])
        eq = sb("eq", [P, NB, BLK])
        score = sb("score", [P, NB, BLK])
        mask = sb("mask", [P, NCH, NB, BLK])
        hm = sb("hm", [P, INTER])
        hT = sb("hT", [P, 2, IT, P], F32R)
        ptr = ps("ptr", [P, 2, 512])
        pt = ps("pt", [P, 512])
        pin = ps("pin", [P, 2, 512])
        ph = ps("ph", [P, 2, 512])
        py = ps("py", [P, 512])
        g_in, g_ok, id_ok, cst_ok, c_in, c_ps, c_ok = (
            sem(n) for n in ("g_in", "g_ok", "id_ok", "cst_ok", "c_in", "c_ps", "c_ok"))
        s_in = [sem(f"s_in{i}") for i in range(NS)]
        w_ps, whi_ok, wlo_ok = sem("w_ps"), sem("whi_ok"), sem("wlo_ok")
        l_in, l_out = [sem(f"l_in{t}") for t in range(QT // 2)], sem("l_out")
        bn, var_ok, ve_ok, rstd_ok, ln_ok = (sem(n) for n in ("bn", "var_ok", "ve_ok", "rstd_ok", "ln_ok"))
        x_in, y_out = [sem("x_in0"), sem("x_in1")], [sem("y_out0"), sem("y_out1")]
        n_in = [sem("n_in0"), sem("n_in1")]
        names = ("xt_ps xhi_ok xf_ok xlo_ok t_ps t_ok in_ps bm_ok eq_ok score_ok bs_ok "
                 "mask_ok h_ps hm_ok ht_ps hhi_ok hlo_ok y_ps y_ok").split()
        loop_sems = [sem(n) for n in names]
        (xt_ps, xhi_ok, xf_ok, xlo_ok, t_ps, t_ok, in_ps, bm_ok, eq_ok, score_ok, bs_ok,
         mask_ok, h_ps, hm_ok, ht_ps, hhi_ok, hlo_ok, y_ps, y_ok) = loop_sems

        w1_t = w1.rearrange("(t p) n -> t p n", p=P)
        w2_t = w2t.rearrange("(t p) n -> t p n", p=P)
        out_v = out.rearrange("b s n -> (b s) n")

        def w_bank(i):
            return (ptr[:, 0], ptr[:, 1], py[:])[i % 3]

        def load_weights(eng, i):
            eng.dma_start(stage[:, i % NS], w1_t[i] if i < IT else w2_t[i - IT]).then_inc(s_in[i % NS], 16)

        with nc.Block() as block:

            @block.sync
            def _(sp):
                gate_column(sp, None, g_ffn, gcol, g_in, g_ok)
                sp.dma_start(c1[:], c1_w).then_inc(c_in, 16)
                sp.dma_start(c2[:], c2_w.rearrange("(t p) r -> p t r", p=P)).then_inc(c_in, 16)
                for t in range(QT // 2):
                    sp.dma_start(xall[:, 2 * t:2 * t + 2],
                                 scr["x2"][2 * t * P:(2 * t + 2) * P].rearrange("(t p) n -> p t n", p=P)).then_inc(l_in[t], 16)
                for t in range(QT):
                    sp.wait_ge(ln_ok, t + 1)
                    sp.dma_start(scr["xn"][t * P:(t + 1) * P], xall[:, t]).then_inc(l_out, 16)
                sp.wait_ge(l_out, 16 * QT)

            @block.gpsimd
            def _(pool):
                start_ahead(pool, loop_sems + x_in + n_in + y_out)
                identity(pool, ident, id_ok)
                pool.memset(mhalf[:], -0.5).then_inc(cst_ok, 1)
                pool.wait_ge(cst_ok, 1)
                pool.wait_ge(ve_ok, QT)
                pool.tensor_tensor(rstd[:], veps[:], mhalf[:], ALU.pow).then_inc(rstd_ok, 1)
                for i in range(BLK):
                    pool.memset(rank[:, :, i:i + 1], float(BLK - i)).then_inc(cst_ok, 1)

            @block.scalar
            def _(act):
                for i in range(NS):
                    load_weights(act, i)
                gate_column(None, act, g_ffn, gcol, g_in, g_ok)
                for i in range(IT):
                    act.wait_ge(w_ps, i + 1)
                    load_weights(act, i + NS)
                    act.copy(w1T[:, HI, :, i * P:(i + 1) * P],
                             w_bank(i).rearrange("p (c r) -> p c r", c=KT)).then_inc(whi_ok, 1)

            @block.tensor
            def _(pe):
                pe.wait_ge(id_ok, 2)
                pe.wait_ge(c_in, 32)
                for c in range(KT):
                    mm = pe.transpose(pt[:, c * RANK:(c + 1) * RANK], c1[:, c * P:(c + 1) * P], ident[0:RANK, 0:RANK])
                mm.then_inc(c_ps, 1)
                for g, (a, z) in enumerate(GT):
                    bank = (pin[:, 0], pin[:, 1], ph[:, 0], ph[:, 1])[g]
                    for t in range(a, z):
                        mm = pe.transpose(bank[0:RANK, (t - a) * P:(t - a + 1) * P], c2[:, t], ident[:])
                    mm.then_inc(c_ps, 1)
                for i in range(IT):
                    pe.wait_ge(s_in[i % NS], 16 * (i // NS) + 16)
                    if i >= 3:
                        pe.wait_ge(wlo_ok, i - 2)
                    for c in range(KT):
                        mm = pe.transpose(w_bank(i)[:, c * P:(c + 1) * P], stage[:, i % NS, c * P:(c + 1) * P], ident[:])
                    mm.then_inc(w_ps, 1)

            @block.vector
            def _(dve):
                for t in range(QT):
                    dve.wait_ge(l_in[t // 2], 16)
                    dve.bn_stats(stats[:, t], xall[:, t]).then_inc(bn, 1)
                for t in range(QT):
                    dve.wait_ge(bn, t + 1)
                    dve.bn_aggr(mv[:, t], stats[:, t]).then_inc(var_ok, 1)
                for t in range(QT):
                    dve.wait_ge(var_ok, t + 1)
                    dve.tensor_scalar(veps[:, t:t + 1], mv[:, t, 1:2], EPS_LN, None, ALU.add).then_inc(ve_ok, 1)
                dve.wait_ge(c_ps, 1)
                dve.tensor_copy(c1T[:].rearrange("p c r -> p (c r)"), pt[:, 0:KT * RANK]).then_inc(c_ok, 1)
                for g, (a, z) in enumerate(GT):
                    bank = (pin[:, 0], pin[:, 1], ph[:, 0], ph[:, 1])[g]
                    dve.wait_ge(c_ps, g + 2)
                    dve.tensor_copy(c2T[:, a * P:z * P], bank[0:RANK, 0:(z - a) * P]).then_inc(c_ok, 1)
                dve.wait_ge(rstd_ok, 1)
                for t in range(QT):
                    dve.tensor_scalar(xall[:, t], xall[:, t], mv[:, t, 0:1], rstd[:, t:t + 1],
                                      ALU.subtract, ALU.mult).then_inc(ln_ok, 1)
                for i in range(IT):
                    dve.wait_ge(whi_ok, i + 1)
                    dve.tensor_tensor(w1T[:, LO, :, i * P:(i + 1) * P], w_bank(i).rearrange("p (c r) -> p c r", c=KT),
                                      w1T[:, HI, :, i * P:(i + 1) * P].bitcast(F32), ALU.subtract).then_inc(wlo_ok, 1)

        T = 27
        tile_steps = [(-57, "load"), (-20, "xload"), (26.5, "store"),
                      (-26.7, "xt"), (-21.9, "c1"), (-19.3, "inner", 0), (-14, "inner", 1), (-10, "inner", 2), (-7, "inner", 3),
                      (-26.5, "xcopy"), (-24.2, "xlo"), (-21.8, "tcopy"),
                      (-15.8, "mask", 0), (-12, "mask", 1), (-8.9, "mask", 2), (-5, "mask", 3),
                      (0.2, "h", 0), (2.7, "h", 1), (5.2, "h", 2), (7.8, "h", 3),
                      (2.6, "hm", 0), (5.1, "hm", 1), (7.7, "hm", 2), (10.2, "hm", 3),
                      (7.75, "ht", 0), (10.5, "ht", 1), (14.0, "ht", 2), (16.9, "ht", 3),
                      (9.0, "hsplit", 0), (11.0, "hsplit", 1), (14.9, "hsplit", 2), (17.9, "hsplit", 3),
                      (11.1, "out", 0), (14.2, "out", 1), (17.2, "out", 2), (20.2, "out", 3), (26, "y")]
        first_steps = [(3.0 + t, "w2", 0, t) for t in range(IT)]
        steps = sorted((p + j * T, what[0], j, *(what[1:] or (0,))) for j in range(2) for p, *what in tile_steps)

        with nc.Block() as block:

            @block.sync
            def _(sp):
                def step(r, what, j, c):
                    i = 2 * r + j
                    if what == "w2":
                        if c + NS < IT:
                            sp.wait_ge(wlo_ok, IT + c + 1)
                            load_weights(sp, IT + c + NS)
                    elif what == "load":
                        sp.wait_ge(xt_ps, AHEAD + i - 1)
                        sp.dma_start(xn[:, j], scr["xn"][bass.ds(i * P, P)]).then_inc(n_in[j], 16)
                    elif what == "xload":
                        sp.wait_ge(y_out[j], AHEAD + 16 * r)
                        sp.dma_start(xin[:, j], scr["x2"][bass.ds(i * P, P)]).then_inc(x_in[j], 16)
                    elif what == "store":
                        sp.wait_ge(y_ok, AHEAD + i + 1)
                        sp.dma_start(out_v[bass.ds(i * P, P)], xin[:, j]).then_inc(y_out[j], 16)
                pipeline(sp, QT // 2, 2 * T, steps, step, first_steps)
                for j in range(2):
                    sp.wait_ge(y_out[j], AHEAD + 16 * (QT // 2))

            @block.scalar
            def _(act):
                def step(r, what, j, c):
                    i = 2 * r + j
                    if what == "w2":
                        k = IT + c
                        act.wait_ge(s_in[k % NS], 16 * (k // NS) + 16)
                        act.copy(w2[:, HI, c], stage[:, k % NS]).then_inc(whi_ok, 1)
                    elif what == "xcopy":
                        act.wait_ge(xt_ps, AHEAD + i + 1)
                        act.wait_ge(h_ps, AHEAD + (i - 1) * NCH)
                        act.copy(xT[:, j, HI].rearrange("p c r -> p (c r)"), pt[:]).then_inc(xhi_ok, 1)
                        act.wait_ge(t_ps, AHEAD + i)
                        act.copy(xTf[:].rearrange("p c r -> p (c r)"), pt[:]).then_inc(xf_ok, 1)
                    elif what == "tcopy":
                        act.wait_ge(t_ps, AHEAD + i + 1)
                        act.wait_ge(in_ps, AHEAD + i * NCH)
                        act.copy(tT[:], pin[0:RANK, 1, 0:P]).then_inc(t_ok, 1)
                    elif what == "hsplit":
                        a, z = GT[c]
                        act.wait_ge(ht_ps, AHEAD + i * len(GT) + c + 1)
                        act.wait_ge(y_ps, AHEAD + i)
                        act.copy(hT[:, HI, a:z].rearrange("p c r -> p (c r)"),
                                 ptr[:, HB[c], 0:(z - a) * P]).then_inc(hhi_ok, 1)
                pipeline(act, QT // 2, 2 * T, steps, step, first_steps)

            @block.tensor
            def _(pe):
                def step(r, what, j, c):
                    i = 2 * r + j
                    if what == "xt":
                        pe.wait_ge(n_in[j], AHEAD + 16 * r + 16)
                        pe.wait_ge(xlo_ok, AHEAD + i)
                        for k in range(KT):
                            mm = pe.transpose(pt[:, k * P:(k + 1) * P], xn[:, j, k * P:(k + 1) * P], ident[:])
                        mm.then_inc(xt_ps, 1)
                    elif what == "c1":
                        pe.wait_ge(xf_ok, AHEAD + i + 1)
                        pe.wait_ge(eq_ok, AHEAD + i * NCH)
                        for k in range(KT):
                            mm = pe.matmul(pin[0:RANK, 1, 0:P], c1T[:, k], xTf[:, k], start=(k == 0), stop=(k == KT - 1))
                        mm.then_inc(t_ps, 1)
                    elif what == "inner":
                        pe.wait_ge(t_ok, AHEAD + i + 1)
                        pe.wait_ge(eq_ok, AHEAD + i * NCH + c - 1)
                        pe.matmul(pin[:, c % 2, 0:CW], tT[:], c2T[:, c * CW:(c + 1) * CW],
                                  start=True, stop=True).then_inc(in_ps, 1)
                    elif what == "h":
                        pe.wait_ge(xlo_ok, AHEAD + i + 1)
                        pe.wait_ge(hm_ok, AHEAD + i * NCH + c - 1)
                        for t in range(KT):
                            for p, (xp, wp) in enumerate(((HI, HI), (LO, HI), (HI, LO))):
                                mm = pe.matmul(ph[:, c % 2, 0:CW], xT[:, j, xp, t], w1T[:, wp, t, c * CW:(c + 1) * CW],
                                               start=(t == 0 and p == 0), stop=(t == KT - 1 and p == 2))
                        mm.then_inc(h_ps, 1)
                    elif what == "ht":
                        a, z = GT[c]
                        pe.wait_ge(hm_ok, AHEAD + i * NCH + (z * P + CW - 1) // CW)
                        pe.wait_ge(hlo_ok, AHEAD + i * len(GT) + c - 1)
                        for t in range(a, z):
                            mm = pe.transpose(ptr[:, HB[c], (t - a) * P:(t - a + 1) * P], hm[:, t * P:(t + 1) * P], ident[:])
                        mm.then_inc(ht_ps, 1)
                    elif what == "out":
                        a, z = GT[c]
                        pe.wait_ge(hlo_ok, AHEAD + i * len(GT) + c + 1)
                        pe.wait_ge(wlo_ok, IT + z)
                        if c == 0:
                            pe.wait_ge(y_ok, AHEAD + i)
                        for t in range(a, z):
                            for p, (hp, wp) in enumerate(((HI, HI), (LO, HI), (HI, LO))):
                                mm = pe.matmul(py[:], hT[:, hp, t], w2[:, wp, t],
                                               start=(t == 0 and p == 0), stop=(t == IT - 1 and p == 2))
                        if c == len(GT) - 1:
                            mm.then_inc(y_ps, 1)
                pipeline(pe, QT // 2, 2 * T, steps, step)

            @block.vector
            def _(dve):
                def blocks(a):
                    return a.rearrange("p (n b) -> p n b", b=BLK)

                def step(r, what, j, c):
                    i = 2 * r + j
                    u = i * NCH + c
                    if what == "w2":
                        k = IT + c
                        dve.wait_ge(whi_ok, k + 1)
                        dve.tensor_tensor(w2[:, LO, c], stage[:, k % NS], w2[:, HI, c].bitcast(F32),
                                          ALU.subtract).then_inc(wlo_ok, 1)
                    elif what == "xlo":
                        dve.wait_ge(xf_ok, AHEAD + i + 1)
                        dve.tensor_tensor(xT[:, j, LO].rearrange("p c r -> p (c r)"), pt[:],
                                          xT[:, j, HI].bitcast(F32).rearrange("p c r -> p (c r)"), ALU.subtract).then_inc(xlo_ok, 1)
                    elif what == "mask":
                        dve.wait_ge(in_ps, AHEAD + u + 1)
                        inner = blocks(pin[:, c % 2, 0:CW])
                        dve.tensor_reduce(bm[:], inner, AX.X, ALU.max).then_inc(bm_ok, 1)
                        dve.wait_ge(bm_ok, AHEAD + u + 1)
                        dve.tensor_tensor(eq[:], inner, bm[:].unsqueeze(2).to_broadcast([P, NB, BLK]),
                                          ALU.is_equal).then_inc(eq_ok, 1)
                        dve.wait_ge(eq_ok, AHEAD + u + 1)
                        dve.tensor_tensor(score[:], eq[:], rank[:], ALU.mult).then_inc(score_ok, 1)
                        dve.wait_ge(score_ok, AHEAD + u + 1)
                        dve.tensor_reduce(bs[:], score[:], AX.X, ALU.max).then_inc(bs_ok, 1)
                        dve.wait_ge(bs_ok, AHEAD + u + 1)
                        dve.wait_ge(hm_ok, AHEAD + u + 1 - NCH)
                        dve.tensor_tensor(mask[:, c], score[:], bs[:].unsqueeze(2).to_broadcast([P, NB, BLK]),
                                          ALU.is_equal).then_inc(mask_ok, 1)
                    elif what == "hm":
                        dve.wait_ge(mask_ok, AHEAD + u + 1)
                        dve.wait_ge(h_ps, AHEAD + u + 1)
                        dve.wait_ge(ht_ps, AHEAD + i * len(GT))
                        dve.scalar_tensor_tensor(out=hm[:, c * CW:(c + 1) * CW], in0=ph[:, c % 2, 0:CW], scalar=0.0,
                                                 in1=mask[:, c].rearrange("p n b -> p (n b)"),
                                                 op0=ALU.max, op1=ALU.mult).then_inc(hm_ok, 1)
                    elif what == "hsplit":
                        a, z = GT[c]
                        dve.wait_ge(hhi_ok, AHEAD + i * len(GT) + c + 1)
                        dve.tensor_tensor(hT[:, LO, a:z].rearrange("p c r -> p (c r)"), ptr[:, HB[c], 0:(z - a) * P],
                                          hT[:, HI, a:z].bitcast(F32).rearrange("p c r -> p (c r)"),
                                          ALU.subtract).then_inc(hlo_ok, 1)
                    elif what == "y":
                        dve.wait_ge(y_ps, AHEAD + i + 1)
                        dve.wait_ge(x_in[j], AHEAD + 16 * r + 16)
                        dve.scalar_tensor_tensor(out=xin[:, j], in0=py[:], scalar=gcol[:, 1:2], in1=xin[:, j],
                                                 op0=ALU.mult, op1=ALU.add).then_inc(y_ok, 1)
                pipeline(dve, QT // 2, 2 * T, steps, step, first_steps)


_INS = ["x", "ctx_4096", "g_xattn", "g_ffn", "L0_xattn_Wq", "L0_xattn_Wk", "L0_xattn_Wv", "L0_xattn_Wo",
        "L0_xattn_q_norm_w", "L0_xattn_k_norm_w", "L0_ffn_c1_w", "L0_ffn_c2_w", "L0_ffn_w1", "L0_ffn_w2t"]


def kernel(**inputs):
    import numpy as np
    import concourse.bacc as bacc
    from concourse.bass_utils import run_bass_kernel_spmd

    nc = bacc.Bacc("TRN2", target_bir_lowering=False, num_devices=1)
    arrays, args = {}, []
    for name in _INS:
        a = np.ascontiguousarray(inputs[name])
        arrays[f"in_{name}"] = a
        args.append(nc.dram_tensor(f"in_{name}", a.shape, mybir.dt.from_np(a.dtype), kind="ExternalInput").ap())
    out = nc.dram_tensor("out_x", inputs["x"].shape, F32, kind="ExternalOutput").ap()
    program(nc, *args, out)
    r = run_bass_kernel_spmd(nc, [arrays], core_ids=[0])
    return r.results[0]["out_x"]
```
